# Optimizing a Trainium2 kernel written in Bass

```python
import numpy as np
import jax
import jax.numpy as jnp

def _softmax(x, axis=-1):
    return jax.nn.softmax(x, axis=axis)

def _gelu(x):
    return jax.nn.gelu(x, approximate=True)

def _silu(x):
    return jax.nn.silu(x)

def _sigmoid(x):
    return jax.nn.sigmoid(x)

def _layernorm(x, axis=-1, eps=1e-05):
    m = jnp.mean(x, axis=axis, keepdims=True)
    v = jnp.var(x, axis=axis, keepdims=True)
    return (x - m) / jnp.sqrt(v + eps)

def _scatter_add(tgt, idx, src, axis=0):
    return tgt.at[idx].add(src)

def _segment_sum(src, seg, n):
    return jax.ops.segment_sum(src, seg, n)
kernel_name = 'mk_perceiver_d2_seqx_r4_e5e5e0'

def setup_inputs(seed: int=0):
    np.random.seed(seed)
    _w = jnp.asarray

    def _rec_inputs():
        import jax
        import jax.numpy as jnp
        _rk = jax.random.key(seed)
        x = -0.0002928 + 1 * jax.random.normal(jax.random.fold_in(_rk, 1), (32, 64, 256), jnp.float32)
        _lenS = 64 - jax.random.randint(jax.random.fold_in(_rk, 7), (32,), 0, max(1, 64 // 4) + 1, jnp.int32)
        _lenS2 = 256 - jax.random.randint(jax.random.fold_in(_rk, 8), (32,), 0, max(1, 256 // 4) + 1, jnp.int32)
        _ctx_512P = jax.random.normal(jax.random.fold_in(_rk, 11), (32, 16, 128), jnp.float32)
        _ctx_512c = jax.random.dirichlet(jax.random.fold_in(_rk, 511), 0.3 * jnp.ones((16,), jnp.float32), (32, 256))
        _ctx_512t = jnp.einsum('bsk,bkd->bsd', _ctx_512c, _ctx_512P)
        _ctx_512t = _ctx_512t * jax.lax.rsqrt(jnp.mean(jnp.square(_ctx_512t)) + 1e-12) * 0.953939
        ctx_512 = -0.000514642 + 1.00011 * (_ctx_512t + 0.3 * jax.random.normal(jax.random.fold_in(_rk, 611), (32, 256, 128), jnp.float32))
        return (x, ctx_512)
    x, ctx_512 = _rec_inputs()

    def _L0_xattn_setup():
        import jax, jax.numpy as jnp
        import numpy as np
        DIM = 256
        LATENT_DIM = 128
        NUM_HEADS = 16
        HEAD_DIM = DIM // NUM_HEADS
        SCALE = HEAD_DIM ** (-0.5)
        key = jax.random.key(seed)
        k1, k2, k3, k4, k5 = jax.random.split(key, 5)
        B, xN, zN = (2, 512, 512)
        x = jax.random.normal(k1, (B, xN, DIM), dtype=jnp.float32)
        z = jax.random.normal(k2, (B, zN, LATENT_DIM), dtype=jnp.float32)
        Wq = jax.random.normal(k3, (DIM, DIM), dtype=jnp.float32) * DIM ** (-0.5)
        Wkv = jax.random.normal(k4, (2 * DIM, LATENT_DIM), dtype=jnp.float32) * LATENT_DIM ** (-0.5)
        Wo = jax.random.normal(k5, (DIM, DIM), dtype=jnp.float32) * DIM ** (-0.5)
        return {'x': x, 'z': z, 'Wq': Wq, 'Wkv': Wkv, 'Wo': Wo}
    _L0_xattn_all = _L0_xattn_setup()
    _L0_xattn_in = {k: v for k, v in _L0_xattn_all.items() if k in ('Wq', 'Wkv', 'Wo')}
    del _L0_xattn_all

    def _L0_attn_setup():
        import jax, jax.numpy as jnp
        import numpy as np
        N_HEADS = 16
        key = jax.random.key(seed)
        ks = jax.random.split(key, 5)
        D = 256
        x = jax.random.normal(ks[0], (4, 512, D), dtype=jnp.float32)
        s = 0.02
        w_attn = jax.random.normal(ks[1], (D, 3 * D), dtype=jnp.float32) * s
        b_attn = jnp.zeros((3 * D,), dtype=jnp.float32)
        w_proj = jax.random.normal(ks[2], (D, D), dtype=jnp.float32) * s
        b_proj = jnp.zeros((D,), dtype=jnp.float32)
        return {'x': x, 'w_attn': w_attn, 'b_attn': b_attn, 'w_proj': w_proj, 'b_proj': b_proj}
    _L0_attn_all = _L0_attn_setup()
    _L0_attn_in = {k: v for k, v in _L0_attn_all.items() if k in ('w_attn', 'b_attn', 'w_proj', 'b_proj')}
    del _L0_attn_all

    def _L0_ffn_setup():
        import jax, jax.numpy as jnp
        import numpy as np
        HIDDEN = 256
        INNER = 1024

        def _weight_quant(w):
            scale = 1.0 / jnp.clip(jnp.mean(jnp.abs(w)), 1e-05)
            wq = jnp.clip(jnp.round(w * scale), -1.0, 1.0) / scale
            return w + jax.lax.stop_gradient(wq - w)

        def _act_quant(x):
            scale = 127.0 / jnp.clip(jnp.max(jnp.abs(x), axis=-1, keepdims=True), 1e-05)
            xq = jnp.clip(jnp.round(x * scale), -128.0, 127.0) / scale
            return x + jax.lax.stop_gradient(xq - x)

        def _bitlinear(x, w):
            return jnp.einsum('bsi,oi->bso', _act_quant(x), _weight_quant(w))
        key = jax.random.key(seed)
        k0, k1, k2, k3 = jax.random.split(key, 4)
        x = jax.random.normal(k0, (4, 512, HIDDEN), dtype=jnp.float32)
        w_gate = jax.random.normal(k1, (INNER, HIDDEN), dtype=jnp.float32) / np.sqrt(HIDDEN)
        w_up = jax.random.normal(k2, (INNER, HIDDEN), dtype=jnp.float32) / np.sqrt(HIDDEN)
        w_down = jax.random.normal(k3, (HIDDEN, INNER), dtype=jnp.float32) / np.sqrt(INNER)
        return {'x': x, 'w_gate': w_gate, 'w_up': w_up, 'w_down': w_down}
    _L0_ffn_all = _L0_ffn_setup()
    _L0_ffn_in = {k: v for k, v in _L0_ffn_all.items() if k in ('w_gate', 'w_up', 'w_down')}
    del _L0_ffn_all

    def _L1_xattn_setup():
        import jax, jax.numpy as jnp
        import numpy as np
        B, LQ, LK = (8, 512, 512)
        QD, KD, VD = (256, 128, 128)
        key = jax.random.key(seed)
        ks = jax.random.split(key, 9)
        s = 0.02
        return {'query': jax.random.normal(ks[0], (B, LQ, QD), jnp.float32), 'key': jax.random.normal(ks[1], (B, LK, KD), jnp.float32), 'value': jax.random.normal(ks[2], (B, LK, VD), jnp.float32), 'Wq': jax.random.normal(ks[3], (QD, QD), jnp.float32) * s, 'bq': jnp.zeros((QD,), jnp.float32), 'Wk': jax.random.normal(ks[4], (KD, QD), jnp.float32) * s, 'bk': jnp.zeros((QD,), jnp.float32), 'Wv': jax.random.normal(ks[5], (VD, QD), jnp.float32) * s, 'bv': jnp.zeros((QD,), jnp.float32)}
    _L1_xattn_all = _L1_xattn_setup()
    _L1_xattn_in = {k: v for k, v in _L1_xattn_all.items() if k in ('Wq', 'bq', 'Wk', 'bk', 'Wv', 'bv')}
    del _L1_xattn_all

    def _L1_attn_setup():
        import jax, jax.numpy as jnp
        import numpy as np
        import math
        N_EMBD = 256
        N_HEAD = 16
        N_LAYER = 12
        key = jax.random.key(seed)
        kx, kw, kb = jax.random.split(key, 3)
        B, T, C = (4, 512, N_EMBD)
        x = jax.random.normal(kx, (B, T, C), dtype=jnp.float32)
        bound = 1.0 / math.sqrt(C)
        W = jax.random.uniform(kw, (3 * C, C), minval=-bound, maxval=bound, dtype=jnp.float32)
        W = W * (1.0 / math.sqrt(N_LAYER * 2))
        b = jax.random.uniform(kb, (3 * C,), minval=-bound, maxval=bound, dtype=jnp.float32)
        return {'x': x, 'W': W, 'b': b}
    _L1_attn_all = _L1_attn_setup()
    _L1_attn_in = {k: v for k, v in _L1_attn_all.items() if k in ('W', 'b')}
    del _L1_attn_all

    def _L1_ffn_setup():
        import jax, jax.numpy as jnp
        import numpy as np
        N_EXPERTS = 32
        TOP_K = 8
        N_GROUP = 4
        TOPK_GROUP = 2
        ROUTED_SCALING = 2.5

        def _gate(x, gate_w, gate_bias):
            T, E = (x.shape[0], gate_w.shape[0])
            logits = jnp.einsum('th,eh->te', x, gate_w)
            scores = jax.nn.sigmoid(logits)
            scores_choice = scores + gate_bias[None, :]
            grp = scores_choice.reshape(T, N_GROUP, E // N_GROUP)
            top2, _ = jax.lax.top_k(grp, 2)
            group_scores = top2.sum(-1)
            _, grp_idx = jax.lax.top_k(group_scores, TOPK_GROUP)
            group_mask = jax.nn.one_hot(grp_idx, N_GROUP, dtype=scores.dtype).sum(1)
            expert_mask = jnp.repeat(group_mask, E // N_GROUP, axis=1)
            masked = jnp.where(expert_mask > 0, scores_choice, 0.0)
            _, topk_idx = jax.lax.top_k(masked, TOP_K)
            topk_w = jnp.take_along_axis(scores, topk_idx, axis=1)
            topk_w = topk_w / (topk_w.sum(-1, keepdims=True) + 1e-20)
            topk_w = topk_w * ROUTED_SCALING
            return (topk_idx, topk_w)

        def _mlp(x, wg, wu, wd):
            return jnp.einsum('...i,hi->...h', jax.nn.silu(jnp.einsum('...h,ih->...i', x, wg)) * jnp.einsum('...h,ih->...i', x, wu), wd)
        key = jax.random.key(seed)
        ks = jax.random.split(key, 9)
        B, S, H, I = (2, 128, 256, 128)
        w = 0.02
        return {'hidden_states': jax.random.normal(ks[0], (B, S, H), jnp.float32), 'gate_w': jax.random.normal(ks[1], (N_EXPERTS, H), jnp.float32) * w, 'gate_bias': jax.random.normal(ks[2], (N_EXPERTS,), jnp.float32) * w, 'expert_gate': jax.random.normal(ks[3], (N_EXPERTS, I, H), jnp.float32) * w, 'expert_up': jax.random.normal(ks[4], (N_EXPERTS, I, H), jnp.float32) * w, 'expert_down': jax.random.normal(ks[5], (N_EXPERTS, H, I), jnp.float32) * w, 'shared_gate': jax.random.normal(ks[6], (2 * I, H), jnp.float32) * w, 'shared_up': jax.random.normal(ks[7], (2 * I, H), jnp.float32) * w, 'shared_down': jax.random.normal(ks[8], (H, 2 * I), jnp.float32) * w}
    _L1_ffn_all = _L1_ffn_setup()
    _L1_ffn_in = {k: v for k, v in _L1_ffn_all.items() if k in ('gate_w', 'gate_bias', 'expert_gate', 'expert_up', 'expert_down', 'shared_gate', 'shared_up', 'shared_down')}
    del _L1_ffn_all
    return {'x': x, 'ctx_512': ctx_512, 'L0_xattn_Wq': _L0_xattn_in['Wq'], 'L0_xattn_Wkv': _L0_xattn_in['Wkv'], 'L0_xattn_Wo': _L0_xattn_in['Wo'], 'L0_attn_w_attn': _L0_attn_in['w_attn'], 'L0_attn_b_attn': _L0_attn_in['b_attn'], 'L0_attn_w_proj': _L0_attn_in['w_proj'], 'L0_attn_b_proj': _L0_attn_in['b_proj'], 'L0_ffn_w_gate': _L0_ffn_in['w_gate'], 'L0_ffn_w_up': _L0_ffn_in['w_up'], 'L0_ffn_w_down': _L0_ffn_in['w_down'], 'L1_xattn_Wq': _L1_xattn_in['Wq'], 'L1_xattn_bq': _L1_xattn_in['bq'], 'L1_xattn_Wk': _L1_xattn_in['Wk'], 'L1_xattn_bk': _L1_xattn_in['bk'], 'L1_xattn_Wv': _L1_xattn_in['Wv'], 'L1_xattn_bv': _L1_xattn_in['bv'], 'L1_attn_W': _L1_attn_in['W'], 'L1_attn_b': _L1_attn_in['b'], 'L1_ffn_gate_w': _L1_ffn_in['gate_w'], 'L1_ffn_gate_bias': _L1_ffn_in['gate_bias'], 'L1_ffn_expert_gate': _L1_ffn_in['expert_gate'], 'L1_ffn_expert_up': _L1_ffn_in['expert_up'], 'L1_ffn_expert_down': _L1_ffn_in['expert_down'], 'L1_ffn_shared_gate': _L1_ffn_in['shared_gate'], 'L1_ffn_shared_up': _L1_ffn_in['shared_up'], 'L1_ffn_shared_down': _L1_ffn_in['shared_down']}

def reference(x, ctx_512, L0_xattn_Wq, L0_xattn_Wkv, L0_xattn_Wo, L0_attn_w_attn, L0_attn_b_attn, L0_attn_w_proj, L0_attn_b_proj, L0_ffn_w_gate, L0_ffn_w_up, L0_ffn_w_down, L1_xattn_Wq, L1_xattn_bq, L1_xattn_Wk, L1_xattn_bk, L1_xattn_Wv, L1_xattn_bv, L1_attn_W, L1_attn_b, L1_ffn_gate_w, L1_ffn_gate_bias, L1_ffn_expert_gate, L1_ffn_expert_up, L1_ffn_expert_down, L1_ffn_shared_gate, L1_ffn_shared_up, L1_ffn_shared_down):
    import jax
    import jax.numpy as jnp

    def _L0_xattn_ref(x, z, Wq, Wkv, Wo):
        import jax, jax.numpy as jnp
        import numpy as np
        DIM = 256
        LATENT_DIM = 128
        NUM_HEADS = 16
        HEAD_DIM = DIM // NUM_HEADS
        SCALE = HEAD_DIM ** (-0.5)
        B, xN, _ = x.shape
        _, zN, _ = z.shape
        Q = (x @ Wq.T).reshape(B, xN, NUM_HEADS, HEAD_DIM)
        KV = (z @ Wkv.T).reshape(B, zN, 2, NUM_HEADS, HEAD_DIM)
        K = KV[:, :, 0]
        V = KV[:, :, 1]
        attn = jnp.einsum('bqhd,bkhd->bhqk', Q, K) * SCALE
        attn = jax.nn.softmax(attn, axis=-1)
        O = jnp.einsum('bhqk,bkhd->bqhd', attn, V).reshape(B, xN, DIM)
        return O @ Wo.T

    def _L0_attn_ref(x, w_attn, b_attn, w_proj, b_proj):
        import jax, jax.numpy as jnp
        import numpy as np
        N_HEADS = 16
        B, S, D = x.shape
        H = N_HEADS
        hd = D // H
        qkv = x @ w_attn + b_attn
        q, k, v = jnp.split(qkv, 3, axis=-1)
        q = q.reshape(B, S, H, hd).transpose(0, 2, 1, 3)
        k = k.reshape(B, S, H, hd).transpose(0, 2, 1, 3)
        v = v.reshape(B, S, H, hd).transpose(0, 2, 1, 3)
        att = jnp.einsum('bhqd,bhkd->bhqk', q, k) * (1.0 / np.sqrt(hd))
        causal = jnp.tril(jnp.ones((S, S), dtype=bool))
        att = jnp.where(causal[None, None], att, -jnp.inf)
        att = jax.nn.softmax(att, axis=-1)
        y = jnp.einsum('bhqk,bhkd->bhqd', att, v)
        y = y.transpose(0, 2, 1, 3).reshape(B, S, D)
        return y @ w_proj + b_proj

    def _L0_ffn_ref(x, w_gate, w_up, w_down):
        import jax, jax.numpy as jnp
        import numpy as np
        HIDDEN = 256
        INNER = 1024

        def _weight_quant(w):
            scale = 1.0 / jnp.clip(jnp.mean(jnp.abs(w)), 1e-05)
            wq = jnp.clip(jnp.round(w * scale), -1.0, 1.0) / scale
            return w + jax.lax.stop_gradient(wq - w)

        def _act_quant(x):
            scale = 127.0 / jnp.clip(jnp.max(jnp.abs(x), axis=-1, keepdims=True), 1e-05)
            xq = jnp.clip(jnp.round(x * scale), -128.0, 127.0) / scale
            return x + jax.lax.stop_gradient(xq - x)

        def _bitlinear(x, w):
            return jnp.einsum('bsi,oi->bso', _act_quant(x), _weight_quant(w))
        gate = jax.nn.silu(_bitlinear(x, w_gate))
        up = _bitlinear(x, w_up)
        return _bitlinear(gate * up, w_down)

    def _L1_xattn_ref(query, key, value, Wq, bq, Wk, bk, Wv, bv):
        import jax, jax.numpy as jnp
        import numpy as np
        B, LQ, LK = (8, 512, 512)
        QD, KD, VD = (256, 128, 128)
        q = jnp.einsum('bld,de->ble', query, Wq) + bq
        k = jnp.einsum('bld,de->ble', key, Wk) + bk
        v = jnp.einsum('bld,de->ble', value, Wv) + bv
        scores = jnp.einsum('bqe,bke->bqk', q, k)
        attn = jax.nn.softmax(scores, axis=-1)
        out = jnp.einsum('bqk,bke->bqe', attn, v)
        return out

    def _L1_attn_ref(x, W, b):
        import jax, jax.numpy as jnp
        import numpy as np
        import math
        N_EMBD = 256
        N_HEAD = 16
        N_LAYER = 12
        B, T, C = x.shape
        H = N_HEAD
        D = C // H
        qkv = jnp.einsum('btc,oc->bto', x, W) + b
        q, k, v = jnp.split(qkv, 3, axis=-1)
        q = q.reshape(B, T, H, D).transpose(0, 2, 1, 3)
        k = k.reshape(B, T, H, D).transpose(0, 2, 1, 3)
        v = v.reshape(B, T, H, D).transpose(0, 2, 1, 3)
        att = jnp.einsum('bhtd,bhsd->bhts', q, k) / math.sqrt(D)
        causal = jnp.tril(jnp.ones((T, T), dtype=bool))
        att = jnp.where(causal, att, -jnp.inf)
        att = jax.nn.softmax(att, axis=-1)
        y = jnp.einsum('bhts,bhsd->bhtd', att, v)
        return y.transpose(0, 2, 1, 3).reshape(B, T, C)

    def _L1_ffn_ref(hidden_states, gate_w, gate_bias, expert_gate, expert_up, expert_down, shared_gate, shared_up, shared_down):
        import jax, jax.numpy as jnp
        import numpy as np
        N_EXPERTS = 32
        TOP_K = 8
        N_GROUP = 4
        TOPK_GROUP = 2
        ROUTED_SCALING = 2.5

        def _gate(x, gate_w, gate_bias):
            T, E = (x.shape[0], gate_w.shape[0])
            logits = jnp.einsum('th,eh->te', x, gate_w)
            scores = jax.nn.sigmoid(logits)
            scores_choice = scores + gate_bias[None, :]
            grp = scores_choice.reshape(T, N_GROUP, E // N_GROUP)
            top2, _ = jax.lax.top_k(grp, 2)
            group_scores = top2.sum(-1)
            _, grp_idx = jax.lax.top_k(group_scores, TOPK_GROUP)
            group_mask = jax.nn.one_hot(grp_idx, N_GROUP, dtype=scores.dtype).sum(1)
            expert_mask = jnp.repeat(group_mask, E // N_GROUP, axis=1)
            masked = jnp.where(expert_mask > 0, scores_choice, 0.0)
            _, topk_idx = jax.lax.top_k(masked, TOP_K)
            topk_w = jnp.take_along_axis(scores, topk_idx, axis=1)
            topk_w = topk_w / (topk_w.sum(-1, keepdims=True) + 1e-20)
            topk_w = topk_w * ROUTED_SCALING
            return (topk_idx, topk_w)

        def _mlp(x, wg, wu, wd):
            return jnp.einsum('...i,hi->...h', jax.nn.silu(jnp.einsum('...h,ih->...i', x, wg)) * jnp.einsum('...h,ih->...i', x, wu), wd)
        orig_shape = hidden_states.shape
        H = orig_shape[-1]
        residuals = hidden_states
        x = hidden_states.reshape(-1, H)
        topk_idx, topk_w = _gate(x, gate_w, gate_bias)
        g = jnp.einsum('th,eih->eti', x, expert_gate)
        u = jnp.einsum('th,eih->eti', x, expert_up)
        outs = jnp.einsum('eti,ehi->eth', jax.nn.silu(g) * u, expert_down)
        outs_t = jnp.transpose(outs, (1, 0, 2))
        gathered = jnp.take_along_axis(outs_t, topk_idx[:, :, None], axis=1)
        final = (gathered * topk_w[:, :, None]).sum(1)
        shared = _mlp(residuals, shared_gate, shared_up, shared_down)
        return final.reshape(orig_shape) + shared
    x = x + _L0_xattn_ref(_layernorm(x, axis=-1), ctx_512, L0_xattn_Wq, L0_xattn_Wkv, L0_xattn_Wo)
    x = x + _L0_attn_ref(_layernorm(x, axis=-1), L0_attn_w_attn, L0_attn_b_attn, L0_attn_w_proj, L0_attn_b_proj)
    x = x + _L0_ffn_ref(_layernorm(x, axis=-1), L0_ffn_w_gate, L0_ffn_w_up, L0_ffn_w_down)
    x = x + _L1_xattn_ref(_layernorm(x, axis=-1), ctx_512, ctx_512, L1_xattn_Wq, L1_xattn_bq, L1_xattn_Wk, L1_xattn_bk, L1_xattn_Wv, L1_xattn_bv)
    x = x + _L1_attn_ref(_layernorm(x, axis=-1), L1_attn_W, L1_attn_b)
    x = x + _L1_ffn_ref(_layernorm(x, axis=-1), L1_ffn_gate_w, L1_ffn_gate_bias, L1_ffn_expert_gate, L1_ffn_expert_up, L1_ffn_expert_down, L1_ffn_shared_gate, L1_ffn_shared_up, L1_ffn_shared_down)
    return x

_drawn_inputs = setup_inputs


def setup_inputs(seed=0):
    import zlib

    import numpy as np

    out = dict(_drawn_inputs(seed))
    spreads = {'L0_attn_b_attn': (0.0, 0.1),
     'L0_attn_b_proj': (0.0, 0.1),
     'L1_xattn_bq': (0.0, 0.534),
     'L1_xattn_bk': (0.0, 0.8),
     'L1_xattn_bv': (0.0, 0.1)}
    factors = {'L1_ffn_gate_w': 7.247,
     'L1_ffn_gate_bias': 8.0,
     'L1_ffn_expert_gate': 6.361,
     'L1_ffn_expert_up': 6.308,
     'L1_ffn_expert_down': 6.285,
     'L1_ffn_shared_gate': 3.999,
     'L1_ffn_shared_up': 3.97,
     'L1_ffn_shared_down': 3.967}
    for name, (base, spread) in spreads.items():
        noise = np.random.default_rng([zlib.crc32(name.encode()), seed]).standard_normal(out[name].shape)
        drawn = base * np.exp(spread * noise) if base else spread * noise
        out[name] = jnp.asarray(drawn.astype(out[name].dtype))
    for name, factor in factors.items():
        out[name] = (out[name] * factor).astype(out[name].dtype)
    return out
```

```python
import concourse.bass as bass
from concourse import mybir
from contextlib import ExitStack

F32 = mybir.dt.float32
F32R = mybir.dt.float32r
BF16 = mybir.dt.bfloat16
ALU = mybir.AluOpType
ACT = mybir.ActivationFunctionType
AX = mybir.AxisListType

P = 128
BATCH, SEQ, DIM = 32, 64, 256
CTX, CDIM = 256, 128
HEADS = 16
HD = DIM // HEADS
TOK = BATCH * SEQ
NPAIR = TOK // P
HALF = 2
INNER = 1024
EXPERTS, EDIM, TOPK = 32, 128, 8
NE = EXPERTS + 2
EPS = 1e-5
ROUND = 12582912.0
SCALE = float(HD) ** -0.5
NEG = -1e30


GIVEN = {}


def given(s):
    return GIVEN.get(s.name, 0)


def known(i, low):
    return isinstance(i, int) and i < low


def upto(n, most):
    return min(n, most) if isinstance(n, int) else n


def pipeline(eng, body):
    body(-1, 1, True, False, False, 1)
    body(0, 0, True, True, False, 1)
    with eng.Fori(0, (NPAIR - 2) // 2) as j:
        body(2 * j + 1, 1, True, True, True, j + 2)
        body(2 * j + 2, 0, True, True, True, j + 2)
    body(NPAIR - 1, 1, False, True, True, 0)
    body(NPAIR, 0, False, False, True, 0)


def prev_use(ring, i, k):
    n = len(ring)
    d = next(d for d in range(1, n + 1) if ring[(k - d) % n] == ring[k])
    return n * i + k - d + 1


def build(nc, io, out, stages=6):
    with ExitStack() as ctx:
        def sb(name, shape, dt=F32):
            return ctx.enter_context(nc.sbuf_tensor(name, list(shape), dt))

        credits = {"tensor": [], "vector": [], "scalar": [], "gpsimd": []}

        def sem(name, credit=0, by=None):
            s = ctx.enter_context(nc.semaphore(name))
            if credit:
                GIVEN[s.name] = credit
                credits[by].append(s)
            return s

        ps = ctx.enter_context(nc.psum_tensor("ps", [P, 8, 512], F32))

        X = sb("X", [P, NPAIR, DIM])
        ident = sb("ident", [P, P])
        headmask = sb("headmask", [P, 8])
        oddmask = sb("oddmask", [P, 2])
        causal = sb("causal", [P, SEQ])
        ones = sb("ones", [P, P])

        lnstat = sb("lnstat", [P, 2, 6])
        lnmv = sb("lnmv", [P, 2, 2])
        lneps = sb("lneps", [P, 2, 1])
        lnrs = sb("lnrs", [P, 2, 1])
        mhalf = sb("mhalf", [P, 1])
        epsc = sb("epsc", [P, 1])
        h = sb("h", [P, 2, DIM])
        hT = sb("hT", [P, 2, HALF, P])

        bqs = {2: sb("bqs2", [P, 2]), 5: sb("bqs5", [P, 2])}
        wr6 = sb("wr6", [P, 2, EXPERTS]); br6 = sb("br6", [P, EXPERTS])
        wdram = nc.dram_tensor("token_weights", (NE, TOK), F32, kind="Internal").ap()
        identb = sb("identb", [P, P], BF16)
        wq3 = [sb("wq3g", [P, 2, INNER], BF16), sb("wq3u", [P, 2, INNER], BF16), sb("wq3d", [P, 8, DIM], BF16)]
        wsc = sb("wsc", [P, 3]); wrs = sb("wrs", [P, 3])
        s_const = sem("s_const")
        s_bqs = sem("s_bqs")
        s_x = sem("s_x")
        s_half = sem("s_half")
        s_w1 = sem("s_w1")
        s_xdone = sem("s_xdone", 1, "vector")
        ln_st = sem("ln_st")
        ln_mv = sem("ln_mv")
        ln_eps = sem("ln_eps")
        ln_rs = sem("ln_rs")
        ln_h = sem("ln_h")
        ln_T = sem("ln_T", 2, "tensor")
        ln_hT = sem("ln_hT")

        wq1 = sb("wq1", [P, 2, DIM]); wkv1 = sb("wkv1", [P, 2 * DIM]); wo1 = sb("wo1", [P, 2, DIM])
        wqkv = {2: sb("wqkv2", [P, 2, 3 * DIM]), 5: sb("wqkv5", [P, 2, 3 * DIM])}
        bqk = {2: sb("bqk2", [P, 4]), 5: sb("bqk5", [P, 4])}
        bv = {2: sb("bv2", [P, DIM]), 5: sb("bv5", [P, DIM]), 4: sb("bv4", [P, DIM])}
        wproj = sb("wproj", [P, 2, DIM]); bproj = sb("bproj", [P, DIM])
        wq4 = sb("wq4", [P, 2, DIM]); wk4 = sb("wk4", [P, DIM]); wv4 = sb("wv4", [P, DIM])
        bqk4 = sb("bqk4", [P, 4])

        def cin(v):
            return v.rearrange("(c p) n -> p c n", p=P)

        const_loads = [
            (ident, io["c_ident"]), (headmask, io["c_headmask"]), (oddmask, io["c_oddmask"]),
            (causal, io["c_causal"]), (ones, io["c_ones"]),
            (wq1, cin(io["wq1"])), (wkv1, io["wkv1"]), (wo1, cin(io["wo1"])),
        ]
        late_loads = [
            (wqkv[2], cin(io["wqkv2"])), (wqkv[5], cin(io["wqkv5"])),
            (bqk[2], io["bqk2"]), (bqk[5], io["bqk5"]), (bqk4, io["bqk4"]),
            (bv[2], io["bv2"].partition_broadcast(P)), (bv[5], io["bv5"].partition_broadcast(P)),
            (bv[4], io["bv4"].partition_broadcast(P)),
            (wproj, cin(io["wproj"])), (bproj, io["bproj"].partition_broadcast(P)),
            (wq4, cin(io["wq4"])), (wk4, io["wk4"]), (wv4, io["wv4"]),
            (wr6, cin(io["wr6"])), (br6, io["br6"].partition_broadcast(P)),
        ]

        lnt = [0, NPAIR, None, 2 * NPAIR, 3 * NPAIR, 4 * NPAIR]

        def ln_dve(eng, n, i, u):
            b = NPAIR * n
            if n == 0:
                eng.wait_ge(s_x, 16)
            else:
                eng.wait_ge(s_xdone, given(s_xdone) + b - NPAIR + i + 1)
            eng.bn_stats(lnstat[:, u, :], X[:, i, :]).then_inc(ln_st, 1)
            eng.wait_ge(ln_st, b + i + 1)
            eng.nop(nofuse=True)
            eng.bn_aggr(lnmv[:, u, :], lnstat[:, u, :]).then_inc(ln_mv, 1)

        def ln_dve2(eng, n, i, u, reader=None, _=0):
            b = NPAIR * n
            eng.wait_ge(ln_rs, b + i + 1)
            if reader is None:
                eng.wait_ge(ln_T, given(ln_T) + lnt[n] + i - 1)
            eng.tensor_scalar(h[:, u, :], X[:, i, :], lnmv[:, u, 0:1], lnrs[:, u, :],
                              ALU.subtract, ALU.mult).then_inc(ln_h, 1)

        def ln_pool(eng, n, i, u):
            b = NPAIR * n
            eng.wait_ge(ln_mv, b + i + 1)
            eng.tensor_tensor(lneps[:, u, :], lnmv[:, u, 1:2], epsc[:, :], ALU.add).then_inc(ln_eps, 1)
            eng.wait_ge(ln_eps, b + i + 1)
            eng.tensor_tensor(lnrs[:, u, :], lneps[:, u, :], mhalf[:, :], ALU.pow).then_inc(ln_rs, 1)

        def transpose2(eng, dst, src):
            for c in range(HALF):
                ins = eng.transpose(dst[:, c * P:(c + 1) * P], src[:, c * P:(c + 1) * P], ident[:, :])
            return ins

        def ln_pe(eng, n, i, u, bank):
            eng.wait_ge(ln_h, NPAIR * n + i + 1)
            transpose2(eng, ps[:, bank, :], h[:, u, :]).then_inc(ln_T, 1)

        def ln_act(eng, n, i, u, bank, readers=None):
            eng.wait_ge(ln_T, given(ln_T) + lnt[n] + i + 1)
            if readers is not None:
                readers()
            eng.activation(hT[:, u, :, :], ps[:, bank, 0:DIM], ACT.Copy).then_inc(ln_hT, 1)

        Vs = sb("Vs", [P, 2, 2, DIM])
        with nc.Block() as block:
            @block.sync
            def _(sp):
                sp.dma_start(X[:, :, :], io["x"].rearrange("(n p) d -> p n d", p=P)).then_inc(s_x, 16)
                for dst, src in const_loads:
                    sp.dma_start(dst[:], src).then_inc(s_const, 16)
                for dst, src in late_loads:
                    sp.dma_start(dst[:], src).then_inc(s_w1, 16)

            @block.tensor
            def _(eng):
                eng.wait_ge(s_const, 16 * len(const_loads))

            @block.vector
            def _(eng):
                eng.memset(Vs[:, :, :, :], 0.0).then_inc(s_half, 1)
                eng.wait_ge(s_w1, 16 * len(late_loads))
                for n in (2, 5):
                    eng.tensor_scalar(bqs[n][:, :], bqk[n][:, 0:2], SCALE, None, ALU.mult).then_inc(s_bqs, 1)
                eng.memset(mhalf[:, :], -0.5).then_inc(s_half, 1)
                eng.memset(epsc[:, :], EPS).then_inc(s_half, 1)
                eng.wait_ge(s_const, 16 * len(const_loads))
                eng.tensor_copy(identb[:, :], ident[:, :]).then_inc(s_half, 1)

            @block.scalar
            def _(eng):
                eng.wait_ge(s_const, 16 * len(const_loads))

            @block.gpsimd
            def _(eng):
                eng.wait_ge(s_const, 16 * len(const_loads))
                eng.wait_ge(s_half, 4)

        def load_credits():
            with nc.Block() as block:
                def give(eng, name):
                    for s in credits[name]:
                        eng.sem_inc(s, given(s))
                    credits[name].clear()

                @block.tensor
                def _(eng):
                    give(eng, "tensor")

                @block.vector
                def _(eng):
                    give(eng, "vector")

                @block.scalar
                def _(eng):
                    give(eng, "scalar")

                @block.gpsimd
                def _(eng):
                    give(eng, "gpsimd")

        env = dict(locals())
        number = [0]

        def local(*layers):
            with ExitStack() as stack:
                number[0] += 1
                env["sb"] = lambda name, shape, dt=F32: stack.enter_context(
                    nc.sbuf_tensor(f"{name}_{number[0]}", list(shape), dt))
                for layer, *args in layers:
                    layer(nc, ctx, env, *args)

        if stages >= 1:
            local((cross_heads,))
        if stages >= 2:
            local((self_heads, 2))
        if stages >= 3:
            local((quantise_weights,))
            local((quantised_ffn,))
        if stages >= 4:
            local((cross_single,))
        if stages >= 5:
            local((self_heads, 5))
        if stages >= 6:
            local((router,), (experts,))
            return
        with nc.Block() as block:
            @block.sync
            def _(sp):
                sp.wait_ge(s_xdone, given(s_xdone) + NPAIR * stages)
                sp.dma_start(out.rearrange("(n p) d -> p n d", p=P), X[:, :, :]).then_inc(s_x, 16)
                sp.wait_ge(s_x, 32)


def cross_heads(nc, ctx, env):
    g = env
    sb, sem, ps, X, io = g["sb"], g["sem"], g["ps"], g["X"], g["io"]
    ident, headmask, oddmask, hT = g["ident"], g["headmask"], g["oddmask"], g["hT"]
    ln_dve, ln_dve2, ln_pool, ln_pe, ln_act, transpose2 = (g[k] for k in (
        "ln_dve", "ln_dve2", "ln_pool", "ln_pe", "ln_act", "transpose2"))
    ln_hT, ln_T, s_xdone = g["ln_hT"], g["ln_T"], g["s_xdone"]
    wq, wkv, wo = g["wq1"], g["wkv1"], g["wo1"]

    NS = 8
    cx = sb("cx", [P, 2, 2 * CTX])
    Qs = sb("Qs", [P, 2, HALF, P])
    Qbd = sb("Qbd", [P, 2, HALF, 2, 8 * SEQ])
    KT = sb("KT", [P, 2, HALF, 2 * CTX])
    V = sb("V", [P, 2, 4, DIM])
    Pr = sb("Pr", [P, 2, 2, CTX])
    PT = sb("PT", [P, 2, 2, 2, P])
    mx = sb("mx", [P, 3, 2])
    den = sb("den", [P, 2, 2, HALF, 4])
    rden = sb("rden", [P, HALF, 4, 2])
    Oe = sb("Oe", [P, 2 * HALF, SEQ])
    OT = sb("OT", [P, 2, 2 * HALF, SEQ])
    On = sb("On", [P, 2, DIM])
    OnT = sb("OnT", [P, 2, HALF, P])

    SB = [0, 1, 2, 0, 1, 2, 0, 1]
    TB = [3, 4]
    OB = 5
    FA, FB = 6, 7
    last = 2 * NPAIR

    c_ld = [sem("c_ld0"), sem("c_ld1")]
    c_q = sem("c_q", 2, "tensor"); c_qe = sem("c_qe"); c_qbd = sem("c_qbd", 5, "gpsimd")
    c_k = sem("c_k"); c_ke = sem("c_ke")
    c_v = sem("c_v", 3, "tensor"); c_ve = sem("c_ve", 2, "scalar")
    c_s = sem("c_s", 9, "tensor"); c_max = sem("c_max");
    c_exp = sem("c_exp", 3, "scalar")
    c_t = sem("c_t", 2, "tensor"); c_te = sem("c_te", 2, "vector"); c_pv = sem("c_pv", 9, "tensor")
    c_o1 = sem("c_o1"); c_o2 = sem("c_o2", 1, "vector"); c_rd = sem("c_rd", 8, "vector")
    c_t1 = sem("c_t1", 2, "tensor"); c_on = sem("c_on")
    c_t2 = sem("c_t2", 2, "tensor"); c_t2e = sem("c_t2e", 2, "scalar"); c_wo = sem("c_wo", 2, "tensor")

    order = [(half, b, s) for half in range(HALF) for b in range(2) for s in range(2)]

    g["load_credits"]()
    with nc.Block() as block:
        @block.sync
        def _(sp):
            ctxT = io["ctxT"].rearrange("p (n c) -> p n c", c=2 * CTX)

            def load(i, u):
                sp.wait_ge(c_v, given(c_v) + 2 * i - 2)
                sp.dma_start(cx[:, u, :], ctxT[:, i, :]).then_inc(c_ld[u], 16)

            with sp.Fori(0, NPAIR // 2) as j:
                load(2 * j, 0)
                load(2 * j + 1, 1)

        @block.tensor
        def _(eng):
            def scores(i, u, k):
                half, b, s = order[k]
                eng.wait_ge(c_exp, given(c_exp) + prev_use(SB, i, k))
                for pl in range(2):
                    p = 2 * s + pl
                    ins = eng.matmul(ps[:, SB[k], pl * CTX:(pl + 1) * CTX],
                                     Qbd[:, u, half, b, p * P:(p + 1) * P],
                                     KT[:, u, half, b * CTX:(b + 1) * CTX], start=True, stop=True)
                ins.then_inc(c_s, 1)

            def turn(i, u, k):
                eng.wait_ge(c_exp, given(c_exp) + NS * i + k + 1)
                eng.wait_ge(c_te, given(c_te) + NS * i + k - 1)
                for pl in range(2):
                    for kt in range(2):
                        ins = eng.transpose(ps[:, TB[k % 2], (2 * pl + kt) * P:(2 * pl + kt + 1) * P],
                                            Pr[:, k % 2, pl, kt * P:(kt + 1) * P], ident[:, :])
                ins.then_inc(c_t, 1)

            def pv(i, u, k):
                half, b, s = order[k]
                if k == 0:
                    eng.wait_ge(c_o2, given(c_o2) + i)
                    eng.wait_ge(c_ve, given(c_ve) + 2 * i + 2)
                eng.wait_ge(c_te, given(c_te) + NS * i + k + 1)
                r = 2 * half + b
                for pl in range(2):
                    p = 2 * s + pl
                    for kt in range(2):
                        ins = eng.matmul(ps[32 * p:32 * p + 32, OB, r * P:(r + 1) * P],
                                         V[:, u, 2 * b + kt, half * P + 32 * p:half * P + 32 * p + 32],
                                         PT[:, k % 2, pl, kt, :], start=(kt == 0), stop=(kt == 1),
                                         tile_position=(0, 32 * p))
                ins.then_inc(c_pv, 1)

            def qproj(i, u):
                eng.wait_ge(ln_hT, i + 1)
                for m in range(HALF):
                    for c in range(2):
                        ins = eng.matmul(ps[:, FA, m * P:(m + 1) * P], wq[:, c, m * P:(m + 1) * P],
                                         hT[:, u, c, :], start=(c == 0), stop=(c == 1))
                ins.then_inc(c_q, 1)

            def kproj(i, u, m, ld):
                if m == 0:
                    eng.wait_ge(c_qe, i + 1)
                    eng.wait_ge(c_ld[u], 16 * ld)
                else:
                    eng.wait_ge(c_t2e, given(c_t2e) + i - 1)
                eng.matmul(ps[:, (FA, FB)[m], :], wkv[:, m * P:(m + 1) * P], cx[:, u, :],
                           start=True, stop=True).then_inc(c_k, 1)

            def vproj(i, u, m):
                eng.wait_ge(c_ke, 2 * i + m + 1)
                for t in range(2):
                    ins = eng.matmul(ps[:, (FA, FB)[m], t * DIM:(t + 1) * DIM],
                                     cx[:, u, (2 * m + t) * P:(2 * m + t + 1) * P], wkv[:, DIM:2 * DIM],
                                     start=True, stop=True)
                ins.then_inc(c_v, 1)

            def tail1(t, u):
                eng.wait_ge(c_o2, given(c_o2) + t + 1)
                eng.wait_ge(c_ve, given(c_ve) + upto(2 * (t + 2), last))
                eng.wait_ge(s_xdone, given(s_xdone) + t)
                src = OT[:, u, :, :].rearrange("p r q -> p (r q)")
                transpose2(eng, ps[:, FB, :], src).then_inc(c_t1, 1)

            def tail2(t, u):
                eng.wait_ge(c_on, t + 1)
                transpose2(eng, ps[:, FB, :], On[:, u, :]).then_inc(c_t2, 1)

            def tail3(t, u):
                eng.wait_ge(c_t2e, given(c_t2e) + t + 1)
                eng.wait_ge(c_ve, given(c_ve) + upto(2 * (t + 3), last))
                for c in range(HALF):
                    ins = eng.matmul(ps[:, FB, 0:DIM], OnT[:, u, c, :], wo[:, c, :],
                                     start=(c == 0), stop=(c == 1))
                ins.then_inc(c_wo, 1)

            def body(i, u, front, mid, tail, ld):
                v = 1 - u

                def sc(k):
                    if mid:
                        scores(i, u, k)

                def tv(k):
                    if mid:
                        if k < NS:
                            turn(i, u, k)
                        if k >= 1:
                            pv(i, u, k - 1)
                if mid:
                    eng.wait_ge(c_qbd, given(c_qbd) + 4 * i + 4)
                    eng.wait_ge(c_ke, 2 * i + 2)
                sc(0)
                sc(1)
                if front:
                    eng.wait_ge(c_ve, given(c_ve) + 2 * i + 1)
                    ln_pe(eng, 0, i + 1, v, FA)
                sc(2)
                if tail:
                    tail1(i - 1, v)
                tv(0)
                sc(3)
                tv(1)
                sc(4)
                if front:
                    qproj(i + 1, v)
                tv(2)
                sc(5)
                tv(3)
                sc(6)
                if tail:
                    tail2(i - 1, v)
                tv(4)
                sc(7)
                if front:
                    kproj(i + 1, v, 0, ld)
                tv(5)
                if front:
                    kproj(i + 1, v, 1, ld)
                tv(6)
                if front:
                    vproj(i + 1, v, 0)
                tv(7)
                if front:
                    vproj(i + 1, v, 1)
                if tail:
                    tail3(i - 1, v)
                tv(8)

            pipeline(eng, body)

        @block.vector
        def _(eng):
            def rowmax(i, k):
                eng.wait_ge(c_s, given(c_s) + NS * i + k + 1)
                eng.tensor_reduce(mx[:, SB[k], :], ps[:, SB[k], :].rearrange("p (a n) -> p a n", a=2),
                                  AX.X, ALU.max, negate=True).then_inc(c_max, 1)

            def turned(i, k):
                eng.wait_ge(c_t, given(c_t) + NS * i + k + 1)
                eng.wait_ge(c_pv, given(c_pv) + NS * i + k - 1)
                eng.tensor_copy(PT[:, k % 2, :, :, :], ps[:, TB[k % 2], :]).then_inc(c_te, 1)

            def o_out(i, u):
                eng.wait_ge(c_pv, given(c_pv) + NS * i + NS)
                eng.wait_ge(c_t1, given(c_t1) + i - 1)
                O = ps[:, OB, :].rearrange("p (r e q) -> p r e q", r=2 * HALF, e=2)
                eng.tensor_scalar(Oe[:, :, :], O[:, :, 0, :], oddmask[:, 0:1], None,
                                  ALU.mult).then_inc(c_o1, 1)
                eng.wait_ge(c_o1, i + 1)
                eng.scalar_tensor_tensor(out=OT[:, u, :, :], in0=O[:, :, 1, :], scalar=oddmask[:, 1:2],
                                         in1=Oe[:, :, :], op0=ALU.mult, op1=ALU.add).then_inc(c_o2, 1)

            def denominators(t, u):
                eng.wait_ge(c_exp, given(c_exp) + NS * (t + 1))
                for b in range(2):
                    for e in range(2):
                        eng.reciprocal(rden[64 * b:64 * b + 64, :, :, e],
                                       den[64 * e:64 * e + 64, u, b, :, :]).then_inc(c_rd, 1)

            def normalise(t, u):
                eng.wait_ge(c_t1, given(c_t1) + t + 1)
                eng.wait_ge(c_rd, given(c_rd) + 4 * t + 4)
                eng.wait_ge(c_t2, given(c_t2) + t - 1)
                eng.tensor_tensor(On[:, u, :].rearrange("p (h d) -> p h d", d=HD),
                                  ps[:, FB, 0:DIM].rearrange("p (h d) -> p h d", d=HD),
                                  rden[:, :, :, :].rearrange("p a b c -> p (a b c)").unsqueeze(2)
                                  .to_broadcast([P, HEADS, HD]), ALU.mult).then_inc(c_on, 1)

            def add_x(t):
                eng.wait_ge(c_wo, given(c_wo) + t + 1)
                eng.tensor_tensor(X[:, t, :], ps[:, FB, 0:DIM], X[:, t, :], ALU.add).then_inc(s_xdone, 1)

            def body(i, u, front, mid, tail, ld):
                v = 1 - u
                if front:
                    ln_dve(eng, 0, i + 1, v)
                if mid:
                    rowmax(i, 0)
                    rowmax(i, 1)
                if front:
                    ln_dve2(eng, 0, i + 1, v)
                if mid:
                    rowmax(i, 2)
                if tail:
                    denominators(i - 1, v)
                    normalise(i - 1, v)
                if mid:
                    for k in range(NS):
                        turned(i, k)
                        if k + 3 < NS:
                            rowmax(i, k + 3)
                if tail:
                    add_x(i - 1)
                if mid:
                    o_out(i, u)

            pipeline(eng, body)

        @block.scalar
        def _(eng):
            def exps(i, u, k):
                half, b, s = order[k]
                eng.wait_ge(c_max, NS * i + k + 1)
                eng.wait_ge(c_t, given(c_t) + NS * i + k - 1)
                if k == 0:
                    eng.wait_ge(c_rd, given(c_rd) + 4 * (i - 1))
                for pl in range(2):
                    ins = eng.activation(Pr[:, k % 2, pl, :], ps[:, SB[k], pl * CTX:(pl + 1) * CTX], ACT.Exp,
                                         bias=mx[:, SB[k], pl:pl + 1],
                                         accum_out=den[:, u, b, half, 2 * s + pl:2 * s + pl + 1])
                ins.then_inc(c_exp, 1)

            def q_out(i, u):
                eng.wait_ge(c_q, given(c_q) + i + 1)
                eng.wait_ge(c_qbd, given(c_qbd) + 4 * (i - 1))
                eng.activation(Qs[:, u, :, :], ps[:, FA, 0:DIM], ACT.Copy, scale=SCALE).then_inc(c_qe, 1)

            def k_out(i, u, m):
                eng.wait_ge(c_k, 2 * i + m + 1)
                eng.wait_ge(c_s, given(c_s) + NS * (i - 1))
                eng.activation(KT[:, u, m, :], ps[:, (FA, FB)[m], :], ACT.Copy).then_inc(c_ke, 1)

            def v_out(i, u, m):
                eng.wait_ge(c_v, given(c_v) + 2 * i + m + 1)
                eng.wait_ge(c_pv, given(c_pv) + NS * (i - 1))
                eng.activation(V[:, u, 2 * m:2 * m + 2, :], ps[:, (FA, FB)[m], :],
                               ACT.Copy).then_inc(c_ve, 1)

            def ot_out(t, u):
                eng.wait_ge(c_t2, given(c_t2) + t + 1)
                eng.wait_ge(c_wo, given(c_wo) + t - 1)
                eng.activation(OnT[:, u, :, :], ps[:, FB, 0:DIM], ACT.Copy).then_inc(c_t2e, 1)

            def body(i, u, front, mid, tail, ld):
                v = 1 - u

                def ex(*ks):
                    if mid:
                        for k in ks:
                            exps(i, u, k)
                ex(0, 1)
                if front:
                    ln_act(eng, 0, i + 1, v, FA, lambda: eng.wait_ge(c_q, given(c_q) + i))
                ex(2, 3, 4)
                if front:
                    q_out(i + 1, v)
                ex(5, 6)
                if tail:
                    ot_out(i - 1, v)
                ex(7)
                if front:
                    k_out(i + 1, v, 0)
                    k_out(i + 1, v, 1)
                    v_out(i + 1, v, 0)
                    v_out(i + 1, v, 1)

            pipeline(eng, body)

        @block.gpsimd
        def _(eng):
            def spread(i, u):
                eng.wait_ge(c_qe, i + 1)
                eng.wait_ge(c_s, given(c_s) + NS * (i - 1))
                for half in range(HALF):
                    for b in range(2):
                        eng.tensor_tensor(
                            Qbd[:, u, half, b, :].rearrange("p (j q) -> p j q", q=SEQ),
                            Qs[:, u, half, b * SEQ:(b + 1) * SEQ].unsqueeze(1).to_broadcast([P, 8, SEQ]),
                            headmask[:, :].unsqueeze(2).to_broadcast([P, 8, SEQ]),
                            ALU.mult).then_inc(c_qbd, 1)

            def body(i, u, front, mid, tail, ld):
                if front:
                    ln_pool(eng, 0, i + 1, 1 - u)
                    spread(i + 1, 1 - u)

            pipeline(eng, body)


def self_heads(nc, ctx, env, layer):
    g = env
    sb, sem, ps, X = g["sb"], g["sem"], g["ps"], g["X"]
    ident, headmask, oddmask, causal, hT = g["ident"], g["headmask"], g["oddmask"], g["causal"], g["hT"]
    ln_dve, ln_dve2, ln_pool, ln_pe, ln_act, transpose2 = (g[k] for k in (
        "ln_dve", "ln_dve2", "ln_pool", "ln_pe", "ln_act", "transpose2"))
    ln_hT, s_xdone = g["ln_hT"], g["s_xdone"]
    w, bqk, bv = g["wqkv"][layer], g["bqk"][layer], g["bv"][layer]
    proj = layer == 2
    bqs = g["bqs"][layer]
    wproj, bproj = g["wproj"], g["bproj"]
    L = layer - 1
    base = NPAIR * L
    Qs = sb("Qs", [P, 2, HALF, P])
    Qbd = sb("Qbd", [P, 2, HALF, 2, 8 * SEQ])
    KT = sb("KT", [P, 2, HALF, P])
    V = g["Vs"]
    Sm = sb("Sm", [P, 4, 2, 2, SEQ])
    Pr = sb("Pr", [P, 4, 2, P])
    PT = sb("PT", [P, 2, 2, P])
    mx = sb("mx", [P, 4, 4])
    den = sb("den", [P, 2, HALF, 4, 2])
    rden = sb("rden", [P, HALF, 4, 2])
    Oe = sb("Oe", [P, 2 * HALF, SEQ])
    OT = sb("OT", [P, 2, 2 * HALF, SEQ])
    On = sb("On", [P, 2, DIM])
    OnT = sb("OnT", [P, 2, HALF, P])
    xb = sb("xb", [P, 2, DIM])

    NS = 4
    SB = [0, 1, 2, 0]
    TB = [3, 4]
    OB = 5
    FA, FB = 6, 7
    n = f"a{layer}_"
    a_qk = sem(n + "qk", 2, "tensor"); a_qke = sem(n + "qke"); a_qbd = sem(n + "qbd", 5, "gpsimd")
    a_v = sem(n + "v"); a_ve = sem(n + "ve")
    a_s = sem(n + "s", 5, "tensor"); a_m = sem(n + "m", 3, "vector"); a_max = sem(n + "max")
    a_sub = sem(n + "sub"); a_exp = sem(n + "exp", 5, "scalar"); a_sum = sem(n + "sum", 5, "vector")
    a_t = sem(n + "t", 5, "tensor"); a_te = sem(n + "te", 2, "scalar"); a_pv = sem(n + "pv", 5, "tensor")
    a_o1 = sem(n + "o1"); a_o2 = sem(n + "o2", 1, "vector"); a_rd = sem(n + "rd")
    a_t1 = sem(n + "t1", 2, "tensor"); a_on = sem(n + "on", 2, "vector")
    a_t2 = sem(n + "t2", 2, "tensor"); a_t2e = sem(n + "t2e", 2, "scalar"); a_wo = sem(n + "wo", 2, "tensor")
    a_xb = sem(n + "xb")

    g["load_credits"]()
    with nc.Block() as block:
        @block.tensor
        def _(eng):
            def scores(i, u, k):
                half, s = divmod(k, 2)
                eng.wait_ge(a_m, given(a_m) + prev_use(SB, i, k))
                for pl in range(2):
                    p = 2 * s + pl
                    for b in range(2):
                        ins = eng.matmul(ps[:, SB[k], (2 * pl + b) * P:(2 * pl + b + 1) * P],
                                         Qbd[:, u, half, b, p * P:(p + 1) * P], KT[:, u, half, :],
                                         start=True, stop=True)
                ins.then_inc(a_s, 1)

            def turn(i, u, k):
                eng.wait_ge(a_exp, given(a_exp) + NS * i + k + 1)
                eng.wait_ge(a_te, given(a_te) + NS * i + k - 1)
                for pl in range(2):
                    ins = eng.transpose(ps[:, TB[k % 2], pl * P:(pl + 1) * P],
                                        Pr[:, k, pl, :], ident[:, :])
                ins.then_inc(a_t, 1)

            def pv(i, u, k):
                half, s = divmod(k, 2)
                if k == 0:
                    eng.wait_ge(a_o2, given(a_o2) + i)
                    eng.wait_ge(a_ve, 2 * i + 2)
                eng.wait_ge(a_te, given(a_te) + NS * i + k + 1)
                for b in range(2):
                    r = 2 * half + b
                    for pl in range(2):
                        p = 2 * s + pl
                        ins = eng.matmul(ps[32 * p:32 * p + 32, OB, r * P:(r + 1) * P],
                                         V[:, u, b, half * P + 32 * p:half * P + 32 * p + 32],
                                         PT[:, k % 2, pl, :], start=True, stop=True,
                                         tile_position=(0, 32 * p))
                ins.then_inc(a_pv, 1)

            def qkproj(i, u):
                eng.wait_ge(ln_hT, g["lnt"][L] + i + 1)
                for m in range(4):
                    for c in range(2):
                        ins = eng.matmul(ps[:, FA, m * P:(m + 1) * P], w[:, c, m * P:(m + 1) * P],
                                         hT[:, u, c, :], start=(c == 0), stop=(c == 1))
                ins.then_inc(a_qk, 1)

            def vproj(i, u):
                if proj:
                    eng.wait_ge(a_t2e, given(a_t2e) + i - 1)
                else:
                    eng.wait_ge(a_on, given(a_on) + i - 1)
                for c in range(2):
                    ins = eng.matmul(ps[:, FB, 0:DIM], hT[:, u, c, :], w[:, c, 2 * DIM:3 * DIM],
                                     start=(c == 0), stop=(c == 1))
                ins.then_inc(a_v, 1)

            def tail1(t, u):
                eng.wait_ge(a_o2, given(a_o2) + t + 1)
                eng.wait_ge(a_ve, upto(2 * t + 4, 2 * NPAIR))
                if proj:
                    eng.wait_ge(s_xdone, given(s_xdone) + base + t)
                src = OT[:, u, :, :].rearrange("p r q -> p (r q)")
                transpose2(eng, ps[:, FB, :], src).then_inc(a_t1, 1)

            def tail2(t, u):
                eng.wait_ge(a_on, given(a_on) + t + 1)
                transpose2(eng, ps[:, FB, :], On[:, u, :]).then_inc(a_t2, 1)

            def tail3(t, u):
                eng.wait_ge(a_t2e, given(a_t2e) + t + 1)
                eng.wait_ge(a_ve, upto(2 * t + 6, 2 * NPAIR))
                for c in range(HALF):
                    ins = eng.matmul(ps[:, FB, 0:DIM], OnT[:, u, c, :], wproj[:, c, :],
                                     start=(c == 0), stop=(c == 1))
                ins.then_inc(a_wo, 1)

            def body(i, u, front, mid, tail, ld):
                v = 1 - u

                def sc(k):
                    if mid:
                        scores(i, u, k)

                def tv(k):
                    if mid:
                        if k < NS:
                            turn(i, u, k)
                        if k >= 1:
                            pv(i, u, k - 1)
                if mid:
                    eng.wait_ge(a_qbd, given(a_qbd) + 4 * i + 4)
                    eng.wait_ge(a_qke, 4 * i + 4)
                sc(0)
                sc(1)
                if front:
                    if not known(i, 0):
                        eng.wait_ge(a_qke, 4 * i + 4)
                    ln_pe(eng, L, i + 1, v, FA)
                sc(2)
                if tail:
                    tail1(i - 1, v)
                tv(0)
                sc(3)
                tv(1)
                if front:
                    qkproj(i + 1, v)
                if tail and proj:
                    tail2(i - 1, v)
                tv(2)
                tv(3)
                if front:
                    vproj(i + 1, v)
                if tail and proj:
                    tail3(i - 1, v)
                tv(4)

            pipeline(eng, body)

        @block.vector
        def _(eng):
            def mask(i, k):
                eng.wait_ge(a_s, given(a_s) + NS * i + k + 1)
                eng.wait_ge(a_exp, given(a_exp) + NS * (i - 1) + k + 1)
                S = ps[:, SB[k], :].rearrange("p (a c n) -> p a c n", a=2, c=4)[:, :, 0:4:3, :]
                eng.tensor_tensor(Sm[:, k, :, :, :], S,
                                  causal[:, :].unsqueeze(1).unsqueeze(1).to_broadcast([P, 2, 2, SEQ]),
                                  ALU.add).then_inc(a_m, 1)
                eng.wait_ge(a_m, given(a_m) + NS * i + k + 1)
                eng.tensor_reduce(mx[:, k, :], Sm[:, k, :, :, :], AX.X, ALU.max).then_inc(a_max, 1)

            def rowsum(i, u, k):
                half, s = divmod(k, 2)
                eng.wait_ge(a_exp, given(a_exp) + NS * i + k + 1)
                eng.tensor_reduce(den[:, u, half, 2 * s:2 * s + 2, :],
                                  Pr[:, k, :, :].rearrange("p a (b n) -> p a b n", b=2), AX.X,
                                  ALU.add).then_inc(a_sum, 1)

            def v_out(i, u):
                eng.wait_ge(a_v, i + 1)
                eng.wait_ge(a_pv, given(a_pv) + NS * (i - 1))
                for b in range(2):
                    r = slice(64 * b, 64 * b + 64)
                    eng.tensor_tensor(V[r, u, b, :], ps[r, FB, 0:DIM], bv[r, :], ALU.add).then_inc(a_ve, 1)

            def o_out(i, u):
                eng.wait_ge(a_pv, given(a_pv) + NS * i + NS)
                eng.wait_ge(a_t1, given(a_t1) + i - 1)
                O = ps[:, OB, :].rearrange("p (r e q) -> p r e q", r=2 * HALF, e=2)
                eng.tensor_scalar(Oe[:, :, :], O[:, :, 0, :], oddmask[:, 0:1], None,
                                  ALU.mult).then_inc(a_o1, 1)
                eng.wait_ge(a_o1, i + 1)
                eng.scalar_tensor_tensor(out=OT[:, u, :, :], in0=O[:, :, 1, :], scalar=oddmask[:, 1:2],
                                         in1=Oe[:, :, :], op0=ALU.mult, op1=ALU.add).then_inc(a_o2, 1)

            def denominators(t, u):
                eng.wait_ge(a_sum, given(a_sum) + NS * (t + 1))
                for b in range(2):
                    for e in range(2):
                        eng.reciprocal(rden[64 * b:64 * b + 64, :, :, e],
                                       den[64 * e:64 * e + 64, u, :, :, b]).then_inc(a_rd, 1)

            def normalise(t, u):
                eng.wait_ge(a_t1, given(a_t1) + t + 1)
                eng.wait_ge(a_rd, 4 * t + 4)
                if proj:
                    eng.wait_ge(a_t2, given(a_t2) + t - 1)
                eng.tensor_tensor(On[:, u, :].rearrange("p (h d) -> p h d", d=HD),
                                  ps[:, FB, 0:DIM].rearrange("p (h d) -> p h d", d=HD),
                                  rden[:, :, :, :].rearrange("p a b c -> p (a b c)").unsqueeze(2)
                                  .to_broadcast([P, HEADS, HD]), ALU.mult).then_inc(a_on, 1)

            def add_x(t, u):
                if proj:
                    eng.wait_ge(a_wo, given(a_wo) + t + 1)
                    eng.wait_ge(a_xb, t + 1)
                    eng.tensor_tensor(X[:, t, :], ps[:, FB, 0:DIM], xb[:, u, :],
                                      ALU.add).then_inc(s_xdone, 1)
                else:
                    eng.wait_ge(a_on, given(a_on) + t + 1)
                    eng.tensor_tensor(X[:, t, :], On[:, u, :], X[:, t, :], ALU.add).then_inc(s_xdone, 1)

            def body(i, u, front, mid, tail, ld):
                v = 1 - u
                if front:
                    ln_dve(eng, L, i + 1, v)
                if mid:
                    mask(i, 0)
                    mask(i, 1)
                if front:
                    ln_dve2(eng, L, i + 1, v)
                if mid:
                    mask(i, 2)
                if tail:
                    denominators(i - 1, v)
                    normalise(i - 1, v)
                if mid:
                    rowsum(i, u, 0)
                    mask(i, 3)
                    rowsum(i, u, 1)
                    rowsum(i, u, 2)
                if front:
                    v_out(i + 1, v)
                if mid:
                    rowsum(i, u, 3)
                if tail:
                    add_x(i - 1, v)
                if mid:
                    o_out(i, u)

            pipeline(eng, body)

        @block.scalar
        def _(eng):
            def exps(i, u, k):
                eng.wait_ge(a_sub, NS * i + k + 1)
                eng.wait_ge(a_t, given(a_t) + NS * (i - 1) + k + 1)
                eng.wait_ge(a_sum, given(a_sum) + NS * (i - 1) + k + 1)
                eng.activation(Pr[:, k, :, :], Sm[:, k, :, :, :].rearrange("p a b n -> p a (b n)"),
                               ACT.Exp).then_inc(a_exp, 1)

            def turned(i, k):
                eng.wait_ge(a_t, given(a_t) + NS * i + k + 1)
                eng.wait_ge(a_pv, given(a_pv) + NS * i + k - 1)
                eng.activation(PT[:, k % 2, :, :], ps[:, TB[k % 2], 0:2 * P], ACT.Copy).then_inc(a_te, 1)

            def qk_out(i, u):
                eng.wait_ge(a_qk, given(a_qk) + i + 1)
                eng.wait_ge(a_qbd, given(a_qbd) + 4 * (i - 1))
                for m in range(2):
                    eng.activation(Qs[:, u, m, :], ps[:, FA, m * P:(m + 1) * P], ACT.Identity,
                                   bias=bqs[:, m:m + 1], scale=SCALE).then_inc(a_qke, 1)
                eng.wait_ge(a_s, given(a_s) + NS * (i - 1))
                for m in range(2):
                    eng.activation(KT[:, u, m, :], ps[:, FA, (2 + m) * P:(3 + m) * P], ACT.Identity,
                                   bias=bqk[:, 2 + m:3 + m]).then_inc(a_qke, 1)

            def ot_out(t, u):
                eng.wait_ge(a_t2, given(a_t2) + t + 1)
                eng.wait_ge(a_wo, given(a_wo) + t - 1)
                eng.activation(OnT[:, u, :, :], ps[:, FB, 0:DIM], ACT.Copy).then_inc(a_t2e, 1)

            def body(i, u, front, mid, tail, ld):
                v = 1 - u
                if mid:
                    exps(i, u, 0)
                if front:
                    if not known(i, 1):
                        eng.wait_ge(a_v, i)
                    ln_act(eng, L, i + 1, v, FA)
                if mid:
                    exps(i, u, 1)
                    turned(i, 0)
                    exps(i, u, 2)
                    turned(i, 1)
                if front:
                    qk_out(i + 1, v)
                if tail and proj:
                    ot_out(i - 1, v)
                if mid:
                    exps(i, u, 3)
                    turned(i, 2)
                    turned(i, 3)

            pipeline(eng, body)

        @block.gpsimd
        def _(eng):
            def spread(i, u):
                eng.wait_ge(a_qke, 4 * i + 2)
                eng.wait_ge(a_s, given(a_s) + NS * (i - 1))
                for half in range(HALF):
                    for b in range(2):
                        eng.tensor_tensor(
                            Qbd[:, u, half, b, :].rearrange("p (j q) -> p j q", q=SEQ),
                            Qs[:, u, half, b * SEQ:(b + 1) * SEQ].unsqueeze(1).to_broadcast([P, 8, SEQ]),
                            headmask[:, :].unsqueeze(2).to_broadcast([P, 8, SEQ]),
                            ALU.mult).then_inc(a_qbd, 1)

            def shift(i, k):
                eng.wait_ge(a_max, NS * i + k + 1)
                m = Sm[:, k, :, :, :].rearrange("p a b n -> p (a b) n")
                eng.tensor_tensor(m, m, mx[:, k, :].unsqueeze(2).to_broadcast([P, 4, SEQ]),
                                  ALU.subtract).then_inc(a_sub, 1)

            def body(i, u, front, mid, tail, ld):
                v = 1 - u
                if front:
                    ln_pool(eng, L, i + 1, v)
                if mid:
                    for k in range(NS):
                        shift(i, k)
                if tail and proj:
                    eng.wait_ge(a_wo, given(a_wo) + i - 2)
                    eng.wait_ge(s_xdone, given(s_xdone) + base + i - 2)
                    eng.tensor_tensor(xb[:, v, :], X[:, i - 1, :], bproj[:, :], ALU.add).then_inc(a_xb, 1)
                if front:
                    spread(i + 1, v)

            pipeline(eng, body)


def quantise_weights(nc, ctx, env):
    g = env
    sb, sem, ps, io = g["sb"], g["sem"], g["ps"], g["io"]
    wq3, wsc, wrs = g["wq3"], g["wsc"], g["wrs"]
    raw = [sb("raw3g", [P, 2, INNER]), sb("raw3u", [P, 2, INNER]), sb("raw3d", [P, 8, DIM])]
    ones = g["ones"]
    part = sb("part3", [P, 3])
    mean = sb("mean3", [P, 3])
    rounded = sb("rounded3", [P, 2048])
    q_ld, q_part, q_sum, q_mean, q_sc, q_rs = (sem(f"q_{n}") for n in ("ld", "part", "sum", "mean", "sc", "rs"))
    q_r, q_c = sem("q_r"), sem("q_c")
    g["s_q3"] = s_q3 = sem("s_q3")
    with nc.Block() as block:
        @block.sync
        def _(sp):
            for n, name in enumerate(("wg3", "wu3", "wd3")):
                sp.dma_start(raw[n][:, :, :], io[name].rearrange("(c p) n -> p c n", p=P)).then_inc(q_ld, 16)

        @block.vector
        def _(eng):
            eng.wait_ge(q_ld, 48)
            for n in range(3):
                eng.tensor_reduce(part[:, n:n + 1], raw[n][:, :, :], AX.XY, ALU.add,
                                  apply_absolute_value=True).then_inc(q_part, 1)
            eng.wait_ge(q_sum, 1)
            eng.tensor_scalar(wsc[:, :], ps[:, 0, 0:3], 1.0 / (DIM * INNER), 1e-5, ALU.mult,
                              ALU.max).then_inc(q_sc, 1)
            eng.wait_ge(q_sc, 1)
            eng.reciprocal(wrs[:, :], wsc[:, :]).then_inc(q_rs, 1)
            eng.wait_ge(q_rs, 1)
            for n in range(3):
                flat = raw[n][:, :, :].rearrange("p c n -> p (c n)")
                eng.tensor_scalar(rounded[:, :], flat, wrs[:, n:n + 1], ROUND, ALU.mult,
                                  ALU.add).then_inc(q_r, 1)
                eng.wait_ge(q_r, n + 1)
                eng.tensor_scalar(flat, rounded[:, :], ROUND, 1.0, ALU.subtract, ALU.min).then_inc(q_c, 1)
                eng.wait_ge(q_c, n + 1)
                eng.tensor_scalar(wq3[n][:, :, :].rearrange("p c n -> p (c n)"), flat, -1.0, None,
                                  ALU.max).then_inc(s_q3, 1)

        @block.tensor
        def _(eng):
            eng.wait_ge(q_part, 3)
            eng.matmul(ps[:, 0, 0:3], ones[:, :], part[:, :], start=True, stop=True).then_inc(q_sum, 1)


def quantised_ffn(nc, ctx, env):
    g = env
    sb, sem, ps, X = g["sb"], g["sem"], g["ps"], g["X"]
    ln_dve, ln_dve2, ln_pool = g["ln_dve"], g["ln_dve2"], g["ln_pool"]
    ln_h, ln_T, s_xdone, h, identb = g["ln_h"], g["ln_T"], g["s_xdone"], g["h"], g["identb"]
    wg, wu, wd = g["wq3"]
    wsc = g["wsc"]
    L = 2
    base = NPAIR * L
    am = sb("am3", [P, 2, 1]); ac = sb("ac3", [P, 2, 1]); sc = sb("sc3", [P, 2, 1]); dq = sb("dq3", [P, 2, 3])
    am2 = sb("am32", [P, 2, 1]); ac2 = sb("ac32", [P, 2, 1]); sc2 = sb("sc32", [P, 2, 1]); dq2 = sb("dq32", [P, 2, 1])
    r = sb("r3", [P, 2, DIM]); xq = sb("xq3", [P, 2, DIM], BF16); xqT = sb("xqT3", [P, 2, HALF, P], BF16)
    sg = sb("sg3", [P, 2, INNER]); a = sb("a3", [P, 2, INNER]); ar = sb("ar3", [P, 2, INNER])
    aq = sb("aq3", [P, 2, INNER], BF16); aqT = sb("aqT3", [P, 2, 8, P], BF16)
    rnd = sb("rnd3", [P, 1])
    GB, UB = [0, 2], [1, 3]
    XT, AT, OB = 4, 5, 6
    n = "f_"
    f_am = sem(n + "am"); f_ac = sem(n + "ac"); f_sc = sem(n + "sc"); f_dq = sem(n + "dq", 5, "vector")
    f_r = sem(n + "r"); f_xq = sem(n + "xq"); f_xt = sem(n + "xt", 2, "tensor"); f_xte = sem(n + "xte")
    f_g = sem(n + "g", 3, "tensor"); f_u = sem(n + "u"); f_sg = sem(n + "sg", 3, "scalar"); f_a = sem(n + "a", 3, "vector")
    f_am2 = sem(n + "am2"); f_ac2 = sem(n + "ac2"); f_sc2 = sem(n + "sc2"); f_dq2 = sem(n + "dq2")
    f_ar = sem(n + "ar", 3, "scalar"); f_aq = sem(n + "aq", 3, "gpsimd"); f_at = sem(n + "at", 3, "tensor")
    f_ate = sem(n + "ate", 2, "scalar"); f_o = sem(n + "o", 3, "tensor"); f_rnd = sem(n + "rnd")

    g["load_credits"]()
    with nc.Block() as block:
        @block.tensor
        def _(eng):
            eng.wait_ge(g["s_q3"], 3)

            def xt(i, u):
                eng.wait_ge(f_xq, i + 1)
                if not known(i, 1):
                    eng.wait_ge(f_xte, i)
                out = ps[:, XT, :].bitcast(BF16)
                for c in range(HALF):
                    ins = eng.transpose(out[:, c * P:(c + 1) * P], xq[:, u, c * P:(c + 1) * P], identb[:, :])
                ins.then_inc(f_xt, 1)

            def gu(i, u):
                eng.wait_ge(f_xte, i + 1)
                for q in range(2):
                    eng.wait_ge(f_sg, given(f_sg) + 2 * (i - 1) + q + 1)
                    for c in range(HALF):
                        ins = eng.matmul(ps[:, GB[q], :], xqT[:, u, c, :], wg[:, c, q * 512:(q + 1) * 512],
                                         start=(c == 0), stop=(c == 1))
                    ins.then_inc(f_g, 1)
                    eng.wait_ge(f_a, given(f_a) + 2 * (i - 1) + q + 1)
                    for c in range(HALF):
                        ins = eng.matmul(ps[:, UB[q], :], xqT[:, u, c, :], wu[:, c, q * 512:(q + 1) * 512],
                                         start=(c == 0), stop=(c == 1))
                    ins.then_inc(f_u, 1)

            def at(t, u):
                eng.wait_ge(f_aq, given(f_aq) + t + 1)
                eng.wait_ge(f_ate, given(f_ate) + t)
                out = ps[:, AT, :].bitcast(BF16)
                for c in range(8):
                    ins = eng.transpose(out[:, c * P:(c + 1) * P], aq[:, u, c * P:(c + 1) * P], identb[:, :])
                ins.then_inc(f_at, 1)

            def down(t, u):
                eng.wait_ge(f_ate, given(f_ate) + t + 1)
                eng.wait_ge(s_xdone, given(s_xdone) + base + t)
                for c in range(8):
                    ins = eng.matmul(ps[:, OB, 0:DIM], aqT[:, u, c, :], wd[:, c, :], start=(c == 0), stop=(c == 7))
                ins.then_inc(f_o, 1)

            def body(i, u, front, mid, tail, ld):
                v = 1 - u
                if mid:
                    gu(i, u)
                if tail:
                    at(i - 1, v)
                if front:
                    xt(i + 1, v)
                if tail:
                    down(i - 1, v)

            pipeline(eng, body)

        @block.vector
        def _(eng):
            eng.memset(rnd[:, :], ROUND).then_inc(f_rnd, 1)

            def front1(i, u):
                eng.wait_ge(ln_h, base + i + 1)
                eng.tensor_reduce(am[:, u, :], h[:, u, :], AX.X, ALU.max,
                                  apply_absolute_value=True).then_inc(f_am, 1)
                eng.wait_ge(f_am, i + 1)
                eng.tensor_scalar(ac[:, u, :], am[:, u, :], 1e-5, None, ALU.max).then_inc(f_ac, 1)
                eng.wait_ge(f_ac, 2 * i + 1)
                eng.reciprocal(sc[:, u, :], ac[:, u, :]).then_inc(f_ac, 1)
                eng.wait_ge(f_ac, 2 * i + 2)
                eng.tensor_scalar(sc[:, u, :], sc[:, u, :], 127.0, None, ALU.mult).then_inc(f_sc, 1)
                eng.wait_ge(f_sg, given(f_sg) + 2 * (i - 1))
                eng.tensor_scalar(dq[:, u, :], wsc[:, :], ac[:, u, :], 1.0 / 127.0, ALU.mult,
                                  ALU.mult).then_inc(f_dq, 1)
                eng.wait_ge(f_sc, i + 1)
                eng.tensor_scalar(r[:, u, :], h[:, u, :], sc[:, u, :], ROUND, ALU.mult, ALU.add).then_inc(f_r, 1)
                eng.wait_ge(f_r, i + 1)
                eng.wait_ge(f_xt, given(f_xt) + i - 1)
                eng.tensor_scalar(xq[:, u, :], r[:, u, :], ROUND, None, ALU.subtract).then_inc(f_xq, 1)

            def mul(i, u, q):
                eng.wait_ge(f_sg, given(f_sg) + 2 * i + q + 1)
                eng.wait_ge(f_u, 2 * i + q + 1)
                eng.wait_ge(f_dq, given(f_dq) + i + 1)
                eng.wait_ge(f_ar, given(f_ar) + i - 1)
                eng.scalar_tensor_tensor(out=a[:, u, q * 512:(q + 1) * 512], in0=ps[:, UB[q], :],
                                         scalar=dq[:, u, 1:2], in1=sg[:, u, q * 512:(q + 1) * 512],
                                         op0=ALU.mult, op1=ALU.mult).then_inc(f_a, 1)

            def amax2(i, u):
                eng.wait_ge(f_a, given(f_a) + 2 * i + 2)
                eng.tensor_reduce(am2[:, u, :], a[:, u, :], AX.X, ALU.max,
                                  apply_absolute_value=True).then_inc(f_am2, 1)
                eng.wait_ge(f_am2, i + 1)
                eng.tensor_scalar(ac2[:, u, :], am2[:, u, :], 1e-5, None, ALU.max).then_inc(f_ac2, 1)
                eng.wait_ge(f_ac2, 2 * i + 1)
                eng.reciprocal(sc2[:, u, :], ac2[:, u, :]).then_inc(f_ac2, 1)
                eng.wait_ge(f_ac2, 2 * i + 2)
                eng.tensor_scalar(sc2[:, u, :], sc2[:, u, :], 127.0, None, ALU.mult).then_inc(f_sc2, 1)
                eng.tensor_scalar(dq2[:, u, :], wsc[:, 2:3], ac2[:, u, :], 1.0 / 127.0, ALU.mult,
                                  ALU.mult).then_inc(f_dq2, 1)

            def add_x(t, u):
                eng.wait_ge(f_o, given(f_o) + t + 1)
                eng.wait_ge(f_dq2, t + 1)
                eng.scalar_tensor_tensor(out=X[:, t, :], in0=ps[:, OB, 0:DIM], scalar=dq2[:, u, :],
                                         in1=X[:, t, :], op0=ALU.mult, op1=ALU.add).then_inc(s_xdone, 1)

            def body(i, u, front, mid, tail, ld):
                v = 1 - u
                if front:
                    ln_dve(eng, L, i + 1, v)
                if mid:
                    mul(i, u, 0)
                if front:
                    ln_dve2(eng, L, i + 1, v, f_r, 0)
                    front1(i + 1, v)
                if mid:
                    mul(i, u, 1)
                if tail:
                    add_x(i - 1, v)
                if mid:
                    amax2(i, u)

            pipeline(eng, body)

        @block.scalar
        def _(eng):
            eng.wait_ge(f_rnd, 1)

            def silu(i, u, q):
                eng.wait_ge(f_g, given(f_g) + 2 * i + q + 1)
                eng.wait_ge(f_dq, given(f_dq) + i + 1)
                eng.wait_ge(f_a, given(f_a) + 2 * (i - 1))
                eng.activation(sg[:, u, q * 512:(q + 1) * 512], ps[:, GB[q], :], ACT.Silu,
                               scale=dq[:, u, 0:1]).then_inc(f_sg, 1)

            def round2(i, u):
                eng.wait_ge(f_sc2, i + 1)
                eng.wait_ge(f_aq, given(f_aq) + i - 1)
                eng.activation(ar[:, u, :], a[:, u, :], ACT.Identity, bias=rnd[:, :],
                               scale=sc2[:, u, :]).then_inc(f_ar, 1)

            def xt_out(i, u):
                eng.wait_ge(f_xt, given(f_xt) + i + 1)
                eng.wait_ge(f_g, given(f_g) + 2 * (i - 1))
                if not known(i, 2):
                    eng.wait_ge(f_u, 2 * (i - 1))
                eng.activation(xqT[:, u, :, :], ps[:, XT, :].bitcast(BF16)[:, 0:DIM], ACT.Copy).then_inc(f_xte, 1)

            def at_out(t, u):
                eng.wait_ge(f_at, given(f_at) + t + 1)
                eng.wait_ge(f_o, given(f_o) + t - 1)
                eng.activation(aqT[:, u, :, :], ps[:, AT, :].bitcast(BF16), ACT.Copy).then_inc(f_ate, 1)

            def body(i, u, front, mid, tail, ld):
                v = 1 - u
                if mid:
                    silu(i, u, 0)
                    silu(i, u, 1)
                if tail:
                    at_out(i - 1, v)
                if front:
                    xt_out(i + 1, v)
                if mid:
                    round2(i, u)

            pipeline(eng, body)

        @block.gpsimd
        def _(eng):
            def body(i, u, front, mid, tail, ld):
                v = 1 - u
                if front:
                    ln_pool(eng, L, i + 1, v)
                if mid:
                    eng.wait_ge(f_ar, given(f_ar) + i + 1)
                    eng.wait_ge(f_at, given(f_at) + i - 1)
                    eng.tensor_tensor(aq[:, u, :], ar[:, u, :], rnd[:, :].to_broadcast([P, INNER]),
                                      ALU.subtract).then_inc(f_aq, 1)

            eng.wait_ge(f_rnd, 1)
            pipeline(eng, body)


def cross_single(nc, ctx, env):
    g = env
    sb, sem, ps, X, io = g["sb"], g["sem"], g["ps"], g["X"], g["io"]
    ident, hT = g["ident"], g["hT"]
    ln_dve, ln_dve2, ln_pool, ln_pe, ln_act = (g[k] for k in ("ln_dve", "ln_dve2", "ln_pool", "ln_pe", "ln_act"))
    ln_hT, s_xdone = g["ln_hT"], g["s_xdone"]
    wq, wk, wv, bqk, bv = g["wq4"], g["wk4"], g["wv4"], g["bqk4"], g["bv"][4]
    cx = sb("cx", [P, 2, 2 * CTX])
    QT = sb("QT4", [P, 2, HALF, P])
    KT = sb("KT4", [P, 2, HALF, 2 * CTX])
    V = sb("V4", [P, 2, 4, DIM])
    Pr = sb("Pr4", [P, 2, CTX]); PT = sb("PT4", [P, 2, 2, P])
    mx = sb("mx4", [P, 2, 1]); den = sb("den4", [P, 2, 1]); rd = sb("rd4", [P, 2, 1])
    L = 3
    base = NPAIR * L
    SB, TB, OB = [0, 1], [2, 3], [4, 5]
    FA, FB = 6, 7
    n = "d_"
    d_ld = [sem(n + "ld0"), sem(n + "ld1")]
    d_q = sem(n + "q"); d_qe = sem(n + "qe", 3, "scalar"); d_k = sem(n + "k"); d_ke = sem(n + "ke", 3, "scalar")
    d_v = sem(n + "v", 3, "tensor"); d_ve = sem(n + "ve", 1, "vector"); d_s = sem(n + "s", 2, "tensor")
    d_max = sem(n + "max"); d_exp = sem(n + "exp", 2, "scalar"); d_t = sem(n + "t", 2, "tensor")
    d_te = sem(n + "te", 2, "scalar"); d_o = sem(n + "o", 2, "tensor"); d_rd = sem(n + "rd", 2, "vector")

    g["load_credits"]()
    with nc.Block() as block:
        @block.sync
        def _(sp):
            ctxT = io["ctxT"].rearrange("p (n c) -> p n c", c=2 * CTX)

            def load(i, u):
                sp.wait_ge(d_v, given(d_v) + 2 * i - 2)
                sp.dma_start(cx[:, u, :], ctxT[:, i, :]).then_inc(d_ld[u], 16)

            with sp.Fori(0, NPAIR // 2) as j:
                load(2 * j, 0)
                load(2 * j + 1, 1)

        @block.tensor
        def _(eng):
            def qproj(i, u):
                eng.wait_ge(ln_hT, g["lnt"][L] + i + 1)
                for m in range(HALF):
                    for c in range(2):
                        ins = eng.matmul(ps[:, FA, m * P:(m + 1) * P], wq[:, c, m * P:(m + 1) * P],
                                         hT[:, u, c, :], start=(c == 0), stop=(c == 1))
                ins.then_inc(d_q, 1)

            def kproj(i, u, m, ld):
                if m == 0:
                    eng.wait_ge(d_qe, given(d_qe) + 2 * i + 2)
                    eng.wait_ge(d_ld[u], 16 * ld)
                else:
                    eng.wait_ge(d_ve, given(d_ve) + 2 * i)
                eng.matmul(ps[:, (FA, FB)[m], :], wk[:, m * P:(m + 1) * P], cx[:, u, :],
                           start=True, stop=True).then_inc(d_k, 1)

            def vproj(i, u, m):
                eng.wait_ge(d_ke, given(d_ke) + 2 * i + m + 1)
                for t in range(2):
                    ins = eng.matmul(ps[:, (FA, FB)[m], t * DIM:(t + 1) * DIM],
                                     cx[:, u, (2 * m + t) * P:(2 * m + t + 1) * P], wv[:, :],
                                     start=True, stop=True)
                ins.then_inc(d_v, 1)

            def scores(i, u):
                eng.wait_ge(d_qe, given(d_qe) + 2 * i + 2)
                eng.wait_ge(d_ke, given(d_ke) + 2 * i + 2)
                eng.wait_ge(d_exp, given(d_exp) + i - 1)
                for b in range(2):
                    for c in range(HALF):
                        ins = eng.matmul(ps[64 * b:64 * b + 64, SB[u], 0:CTX], QT[:, u, c, 64 * b:64 * b + 64],
                                         KT[:, u, c, b * CTX:(b + 1) * CTX], start=(c == 0), stop=(c == 1),
                                         tile_position=(0, 64 * b))
                ins.then_inc(d_s, 1)

            def turn(i, u):
                eng.wait_ge(d_exp, given(d_exp) + i + 1)
                eng.wait_ge(d_te, given(d_te) + i - 1)
                for kt in range(2):
                    ins = eng.transpose(ps[:, TB[u], kt * P:(kt + 1) * P], Pr[:, u, kt * P:(kt + 1) * P],
                                        ident[:, :])
                ins.then_inc(d_t, 1)

            def pv(i, u):
                eng.wait_ge(d_te, given(d_te) + i + 1)
                eng.wait_ge(d_ve, given(d_ve) + 2 * i + 2)
                eng.wait_ge(s_xdone, given(s_xdone) + base + i - 1)
                for b in range(2):
                    for kt in range(2):
                        ins = eng.matmul(ps[64 * b:64 * b + 64, OB[u], 0:DIM], PT[:, u, kt, 64 * b:64 * b + 64],
                                         V[:, u, 2 * b + kt, :], start=(kt == 0), stop=(kt == 1),
                                         tile_position=(0, 64 * b))
                ins.then_inc(d_o, 1)

            def body(i, u, front, mid, tail, ld):
                v = 1 - u
                if mid:
                    scores(i, u)
                if front:
                    eng.wait_ge(d_ve, given(d_ve) + 2 * i + 1)
                    ln_pe(eng, L, i + 1, v, FA)
                    qproj(i + 1, v)
                    kproj(i + 1, v, 0, ld)
                if mid:
                    turn(i, u)
                if front:
                    kproj(i + 1, v, 1, ld)
                    vproj(i + 1, v, 0)
                if mid:
                    pv(i, u)
                if front:
                    vproj(i + 1, v, 1)

            pipeline(eng, body)

        @block.vector
        def _(eng):
            def rowmax(i, u):
                eng.wait_ge(d_s, given(d_s) + i + 1)
                eng.wait_ge(d_exp, given(d_exp) + i - 1)
                eng.tensor_reduce(mx[:, u, :], ps[:, SB[u], 0:CTX], AX.X, ALU.max, negate=True).then_inc(d_max, 1)

            def v_out(i, u, m):
                eng.wait_ge(d_v, given(d_v) + 2 * i + m + 1)
                eng.wait_ge(d_o, given(d_o) + i - 1)
                eng.tensor_tensor(V[:, u, 2 * m:2 * m + 2, :], ps[:, (FA, FB)[m], :].rearrange("p (t n) -> p t n", t=2),
                                  bv[:, :].unsqueeze(1).to_broadcast([P, 2, DIM]), ALU.add).then_inc(d_ve, 1)

            def add_x(i, u):
                eng.wait_ge(d_exp, given(d_exp) + i + 1)
                eng.reciprocal(rd[:, u, :], den[:, u, :]).then_inc(d_rd, 1)
                eng.wait_ge(d_rd, given(d_rd) + i + 1)
                eng.wait_ge(d_o, given(d_o) + i + 1)
                eng.scalar_tensor_tensor(out=X[:, i, :], in0=ps[:, OB[u], 0:DIM], scalar=rd[:, u, :],
                                         in1=X[:, i, :], op0=ALU.mult, op1=ALU.add).then_inc(s_xdone, 1)

            def body(i, u, front, mid, tail, ld):
                v = 1 - u
                if front:
                    ln_dve(eng, L, i + 1, v)
                if mid:
                    rowmax(i, u)
                if front:
                    ln_dve2(eng, L, i + 1, v)
                    v_out(i + 1, v, 0)
                if mid:
                    add_x(i, u)
                if front:
                    v_out(i + 1, v, 1)

            pipeline(eng, body)

        @block.scalar
        def _(eng):
            def q_out(i, u):
                eng.wait_ge(d_q, i + 1)
                eng.wait_ge(d_s, given(d_s) + i - 1)
                for m in range(HALF):
                    eng.activation(QT[:, u, m, :], ps[:, FA, m * P:(m + 1) * P], ACT.Identity,
                                   bias=bqk[:, m:m + 1]).then_inc(d_qe, 1)

            def k_out(i, u, m):
                eng.wait_ge(d_k, 2 * i + m + 1)
                eng.activation(KT[:, u, m, :], ps[:, (FA, FB)[m], :], ACT.Identity,
                               bias=bqk[:, 2 + m:3 + m]).then_inc(d_ke, 1)

            def exps(i, u):
                eng.wait_ge(d_max, i + 1)
                eng.wait_ge(d_t, given(d_t) + i - 1)
                eng.wait_ge(d_rd, given(d_rd) + i - 1)
                eng.activation(Pr[:, u, :], ps[:, SB[u], 0:CTX], ACT.Exp, bias=mx[:, u, :],
                               accum_out=den[:, u, :]).then_inc(d_exp, 1)

            def turned(i, u):
                eng.wait_ge(d_t, given(d_t) + i + 1)
                eng.wait_ge(d_o, given(d_o) + i - 1)
                eng.activation(PT[:, u, :, :], ps[:, TB[u], 0:DIM], ACT.Copy).then_inc(d_te, 1)

            def body(i, u, front, mid, tail, ld):
                v = 1 - u
                if mid:
                    exps(i, u)
                if front:
                    if not known(i, 1):
                        eng.wait_ge(d_q, i)
                    ln_act(eng, L, i + 1, v, FA)
                    q_out(i + 1, v)
                    k_out(i + 1, v, 0)
                if mid:
                    turned(i, u)
                if front:
                    k_out(i + 1, v, 1)

            pipeline(eng, body)

        @block.gpsimd
        def _(eng):
            def body(i, u, front, mid, tail, ld):
                if front:
                    ln_pool(eng, L, i + 1, 1 - u)

            pipeline(eng, body)


def router(nc, ctx, env):
    g = env
    sb, sem, ps, X, io = g["sb"], g["sem"], g["ps"], g["X"], g["io"]
    ident, hT = g["ident"], g["hT"]
    ln_dve, ln_dve2, ln_pool, ln_pe, ln_act = (g[k] for k in ("ln_dve", "ln_dve2", "ln_pool", "ln_pe", "ln_act"))
    ln_hT = g["ln_hT"]
    wr, br = g["wr6"], g["br6"]
    g["Hh"] = Hh = sb("Hh", [P, HALF, NPAIR, P], F32R)
    g["Hl"] = Hl = sb("Hl", [P, HALF, NPAIR, P], F32R)
    L = 5
    hb = g["lnt"][L]
    NG, GE, TOPG = 4, EXPERTS // 4, 2
    W = sb("W6", [P, NPAIR, NE])
    score = sb("score6", [P, NPAIR, EXPERTS])
    choice = sb("choice6", [P, NPAIR, EXPERTS])
    gm = sb("gm6", [P, NPAIR, NG, 8])
    gs = sb("gs6", [P, NPAIR, 10])
    g8 = sb("g86", [P, NPAIR, 8]); gr = sb("gr6", [P, NPAIR, 10]); gsel = sb("gsel6", [P, NPAIR, NG])
    msk = sb("msk6", [P, NPAIR, EXPERTS]); m8 = sb("m86", [P, NPAIR, 8]); mr = sb("mr6", [P, NPAIR, EXPERTS])
    tot = sb("tot6", [P, NPAIR, 1]); WT = sb("WT6", [NE, TOK])
    dram = g["wdram"]
    FA, LB = 0, [1, 2]
    n = "r_"
    r_hh = sem(n + "hh"); r_hl = sem(n + "hl"); r_l = sem(n + "l"); r_sc = sem(n + "sc", 2, "scalar")
    r_c = sem(n + "c"); r_w = sem(n + "w"); r_t = sem(n + "t"); r_wt = sem(n + "wt")
    g["r_dram"] = r_dram = sem(n + "dram")

    g["load_credits"]()
    with nc.Block() as block:
        @block.tensor
        def _(eng):
            def body(i, u, front, mid, tail, ld):
                if front:
                    eng.wait_ge(ln_hT, hb + i + 1)
                    ln_pe(eng, L, i + 1, 1 - u, FA)
                if mid:
                    eng.wait_ge(ln_hT, hb + i + 1)
                    eng.wait_ge(r_sc, given(r_sc) + i - 1)
                    for c in range(HALF):
                        ins = eng.matmul(ps[:, LB[u], 0:EXPERTS], hT[:, u, c, :], wr[:, c, :],
                                         start=(c == 0), stop=(c == 1))
                    ins.then_inc(r_l, 1)

            pipeline(eng, body)
            for t in range(NPAIR):
                if t == 0:
                    eng.wait_ge(r_w, 1)
                ins = eng.transpose(ps[0:NE, 4 + t // 4, (t % 4) * P:(t % 4 + 1) * P], W[:, t, :], ident[:, :])
            ins.then_inc(r_t, 1)

        @block.scalar
        def _(eng):
            def body(i, u, front, mid, tail, ld):
                if front:
                    def reads():
                        if not known(i, 1):
                            eng.wait_ge(r_hl, i)
                            eng.wait_ge(r_l, i)
                    ln_act(eng, L, i + 1, 1 - u, FA, reads)
                if mid:
                    eng.wait_ge(ln_hT, hb + i + 1)
                    eng.activation(Hh[:, :, i, :], hT[:, u, :, :], ACT.Copy).then_inc(r_hh, 1)
                    eng.wait_ge(r_l, i + 1)
                    eng.activation(score[:, i, :], ps[:, LB[u], 0:EXPERTS], ACT.Sigmoid).then_inc(r_sc, 1)

            pipeline(eng, body)
            eng.wait_ge(r_t, 1)
            eng.activation(WT[:, :].rearrange("e (b n) -> e b n", b=4), ps[0:NE, 4:8, :], ACT.Copy).then_inc(r_wt, 1)

        @block.vector
        def _(eng):
            eng.memset(gs[:, :, :], NEG).then_inc(r_c, 1)
            eng.memset(W[:, :, EXPERTS:NE], 1.0).then_inc(r_c, 1)

            def body(i, u, front, mid, tail, ld):
                if front:
                    ln_dve(eng, L, i + 1, 1 - u)
                    ln_dve2(eng, L, i + 1, 1 - u)
                if mid:
                    eng.wait_ge(r_hh, i + 1)
                    eng.tensor_tensor(Hl[:, :, i, :], hT[:, u, :, :], Hh[:, :, i, :].bitcast(F32),
                                      ALU.subtract).then_inc(r_hl, 1)

            pipeline(eng, body)
            done = [2]

            def step(ins, k=1):
                ins.then_inc(r_c, 1)
                done[0] += k
                eng.wait_ge(r_c, done[0])

            eng.wait_ge(r_sc, given(r_sc) + NPAIR)
            step(eng.tensor_tensor(choice[:, :, :], score[:, :, :],
                                   br[:, :].unsqueeze(1).to_broadcast([P, NPAIR, EXPERTS]), ALU.add))
            for t in range(NPAIR):
                for q in range(NG):
                    ins = eng.max(gm[:, t, q, :], choice[:, t, q * GE:(q + 1) * GE])
            step(ins)
            step(eng.tensor_tensor(gs[:, :, 0:NG], gm[:, :, :, 0], gm[:, :, :, 1], ALU.add))
            for t in range(NPAIR):
                ins = eng.max(g8[:, t, :], gs[:, t, :])
            step(ins)
            step(eng.memset(g8[:, :, TOPG:8], NEG))
            for t in range(NPAIR):
                ins = eng.match_replace(gr[:, t, :], g8[:, t, :], gs[:, t, :], -NEG)
            step(ins)
            step(eng.tensor_tensor(gsel[:, :, :], gr[:, :, 0:NG], gs[:, :, 0:NG], ALU.not_equal))
            step(eng.tensor_tensor(msk[:, :, :].rearrange("p t (a b) -> p (t a) b", b=GE),
                                   choice[:, :, :].rearrange("p t (a b) -> p (t a) b", b=GE),
                                   gsel[:, :, :].rearrange("p t a -> p (t a)").unsqueeze(2)
                                   .to_broadcast([P, NPAIR * NG, GE]), ALU.mult))
            for t in range(NPAIR):
                ins = eng.max(m8[:, t, :], msk[:, t, :])
            step(ins)
            for t in range(NPAIR):
                ins = eng.match_replace(mr[:, t, :], m8[:, t, :], msk[:, t, :], NEG)
            step(ins)
            step(eng.tensor_tensor(mr[:, :, :], mr[:, :, :], msk[:, :, :], ALU.not_equal))
            step(eng.tensor_tensor(msk[:, :, :], mr[:, :, :], score[:, :, :], ALU.mult))
            step(eng.tensor_reduce(tot[:, :, :], msk[:, :, :], AX.X, ALU.add))
            step(eng.tensor_scalar(tot[:, :, :], tot[:, :, :], 1e-20, None, ALU.add))
            step(eng.reciprocal(tot[:, :, :], tot[:, :, :]))
            step(eng.tensor_scalar(tot[:, :, :], tot[:, :, :], 2.5, None, ALU.mult))
            eng.tensor_tensor(W[:, :, 0:EXPERTS], msk[:, :, :],
                              tot[:, :, :].to_broadcast([P, NPAIR, EXPERTS]), ALU.mult).then_inc(r_w, 1)

        @block.gpsimd
        def _(eng):
            def body(i, u, front, mid, tail, ld):
                if front:
                    ln_pool(eng, L, i + 1, 1 - u)

            pipeline(eng, body)

        @block.sync
        def _(sp):
            sp.wait_ge(r_wt, 1)
            sp.dma_start(dram, WT[:, :]).then_inc(r_dram, 16)
            sp.wait_ge(r_dram, 16)


def experts(nc, ctx, env):
    g = env
    sb, sem, ps, X, io, out = g["sb"], g["sem"], g["ps"], g["X"], g["io"], g["out"]
    ident, Hh, Hl, dram = g["ident"], g["Hh"], g["Hl"], g["wdram"]
    SG = 2
    UT = 512
    raw = sb("raw6", [P, 2, 768])
    wh = sb("wh6", [P, 2, 768], F32R); wl = sb("wl6", [P, 2, 768], F32R)
    wb = sb("wb6", [P, 2, 2 * UT])
    sg = sb("sg6", [P, 2, UT]); sw = sb("sw6", [P, 2, UT]); a = sb("a6", [P, 2, UT])
    ah = sb("ah6", [P, 2, UT], F32R); al = sb("al6", [P, 2, UT], F32R)
    OT = sb("OT6", [P, 4, UT])
    GB, UB, OB = [0, 1], [2, 3], [[4, 5], [6, 7]]
    GU, DN = slice(0, 512), slice(512, 768)
    n = "m_"
    m_ld = [sem(n + "ld0"), sem(n + "ld1")]; m_wb = [sem(n + "wb0"), sem(n + "wb1")]
    m_hg = sem(n + "hg"); m_lg = sem(n + "lg", 2, "vector"); m_hd = sem(n + "hd"); m_ld_ = sem(n + "lowd", 2, "vector")
    m_g = sem(n + "g", 5, "tensor"); m_u = sem(n + "u", 5, "tensor"); m_d = sem(n + "d", 5, "tensor")
    m_sg = sem(n + "sg", 3, "scalar"); m_sw = sem(n + "sw", 3, "gpsimd"); m_a = sem(n + "a", 3, "vector")
    m_ah = sem(n + "ah", 3, "scalar"); m_al = sem(n + "al", 3, "vector")
    m_ot = sem(n + "ot"); m_tt = sem(n + "tt"); m_y = sem(n + "y")
    g["m_out"] = m_out = sem(n + "out")
    HhT = Hh[:, :, :, :].rearrange("p c n t -> p c (n t)")
    HlT = Hl[:, :, :, :].rearrange("p c n t -> p c (n t)")

    def each_expert(eng, s, body):
        k, q = NE * s, NE // 2 * s
        body(0, k, 0, q + 1)
        with eng.Fori(0, NE // 2 - 1) as j:
            body(2 * j + 1, 2 * j + 1 + k, 1, j + 1 + q)
            body(2 * j + 2, 2 * j + 2 + k, 0, j + 2 + q)
        body(NE - 1, NE - 1 + k, 1, NE // 2 + q)

    g["load_credits"]()
    with nc.Block() as block:
        @block.sync
        def _(sp):
            for s in range(SG):
                def body(e, E, u, ld):
                    sp.wait_ge(m_lg, given(m_lg) + E - 1)
                    sp.wait_ge(m_ld_, given(m_ld_) + E - 1)
                    sp.dma_start(raw[:, u, :], io["ew6"][e, :, :]).then_inc(m_ld[u], 16)
                    sp.wait_ge(m_sw, given(m_sw) + 2 * (E - 1))
                    src = dram[bass.ds(e, 1), 2 * UT * s:2 * UT * (s + 1)]
                    sp.dma_start(wb[:, u, :], src.to_broadcast([P, 2 * UT])).then_inc(m_wb[u], 16)

                each_expert(sp, s, body)
            for s in range(SG):
                sp.wait_ge(m_y, 8 * (s + 1))
                sp.dma_start(out.rearrange("(n p) d -> p n d", p=P)[:, 8 * s:8 * s + 8, :],
                             X[:, 8 * s:8 * s + 8, :]).then_inc(m_out, 16)
            sp.wait_ge(m_out, 16 * SG)

        @block.tensor
        def _(eng):
            for s in range(SG):
                def gate_up(E, u, tt):
                    if tt == 0:
                        eng.wait_ge(m_hg, E + 1)
                        eng.wait_ge(m_lg, given(m_lg) + E + 1)
                    cols = slice(2 * UT * s + UT * tt, 2 * UT * s + UT * (tt + 1))
                    for bank, at, free, done in ((GB[tt], 0, m_sg, m_g), (UB[tt], 256, m_a, m_u)):
                        eng.wait_ge(free, given(free) + 2 * (E - 1) + tt + 1)
                        for c in range(HALF):
                            w = slice(at + c * P, at + (c + 1) * P)
                            eng.matmul(ps[:, bank, :], wh[:, u, w], HhT[:, c, cols], start=(c == 0), stop=False)
                            eng.matmul(ps[:, bank, :], wh[:, u, w], HlT[:, c, cols], start=False, stop=False)
                            ins = eng.matmul(ps[:, bank, :], wl[:, u, w], HhT[:, c, cols], start=False,
                                             stop=(c == 1))
                        ins.then_inc(done, 1)

                def down(E, u, tt, first, last):
                    eng.wait_ge(m_al, given(m_al) + 2 * E + tt + 1)
                    if tt == 0:
                        eng.wait_ge(m_ld_, given(m_ld_) + E + 1)
                    for m in range(2):
                        w = slice(512 + m * P, 512 + (m + 1) * P)
                        bank = ps[:, OB[m][tt], :]
                        eng.matmul(bank, wh[:, u, w], ah[:, tt, :], start=first, stop=False)
                        eng.matmul(bank, wh[:, u, w], al[:, tt, :], start=False, stop=False)
                        ins = eng.matmul(bank, wl[:, u, w], ah[:, tt, :], start=False, stop=last)
                    ins.then_inc(m_d, 1)

                k = NE * s
                if s:
                    eng.wait_ge(m_ot, 4 * s)
                    eng.wait_ge(m_y, 8 * s)
                gate_up(k, 0, 0)
                gate_up(k, 0, 1)
                for tt in range(2):
                    gate_up(k + 1, 1, tt)
                    down(k, 0, tt, True, False)
                with eng.Fori(0, NE // 2 - 1) as j:
                    for tt in range(2):
                        gate_up(2 * j + 2 + k, 0, tt)
                        down(2 * j + 1 + k, 1, tt, False, False)
                    for tt in range(2):
                        gate_up(2 * j + 3 + k, 1, tt)
                        down(2 * j + 2 + k, 0, tt, False, False)
                down(k + NE - 1, 1, 0, False, True)
                down(k + NE - 1, 1, 1, False, True)
                eng.wait_ge(m_ot, 4 * s + 4)
                for q in range(8):
                    if q == 0:
                        eng.wait_ge(m_a, given(m_a) + 2 * NE * (s + 1))
                        eng.wait_ge(m_sg, given(m_sg) + 2 * NE * (s + 1))
                    for m in range(2):
                        ins = eng.transpose(ps[:, q // 2, (q % 2) * DIM + m * P:(q % 2) * DIM + (m + 1) * P],
                                            OT[:, 2 * m + q // 4, (q % 4) * P:(q % 4 + 1) * P], ident[:, :])
                    if q % 2:
                        ins.then_inc(m_tt, 1)

        @block.scalar
        def _(eng):
            for s in range(SG):
                def high_gu(E, u, ld):
                    eng.wait_ge(m_ld[u], 16 * ld)
                    eng.wait_ge(m_u, given(m_u) + 2 * (E - 1))
                    eng.activation(wh[:, u, GU], raw[:, u, GU], ACT.Copy).then_inc(m_hg, 1)

                def high_d(E, u):
                    eng.wait_ge(m_d, given(m_d) + 2 * (E - 1))
                    eng.activation(wh[:, u, DN], raw[:, u, DN], ACT.Copy).then_inc(m_hd, 1)

                def silu(E, tt):
                    eng.wait_ge(m_g, given(m_g) + 2 * E + tt + 1)
                    eng.wait_ge(m_sw, given(m_sw) + 2 * (E - 1) + tt + 1)
                    eng.activation(sg[:, tt, :], ps[:, GB[tt], :], ACT.Silu).then_inc(m_sg, 1)

                def high_a(E, tt):
                    eng.wait_ge(m_a, given(m_a) + 2 * E + tt + 1)
                    eng.wait_ge(m_d, given(m_d) + 2 * (E - 1) + tt + 1)
                    eng.activation(ah[:, tt, :], a[:, tt, :], ACT.Copy).then_inc(m_ah, 1)

                def body(e, E, u, ld):
                    high_d(E, u)
                    silu(E, 0)
                    if not (isinstance(e, int) and e == NE - 1):
                        high_gu(E + 1, 1 - u, ld if u == 0 else ld + 1)
                    high_a(E, 0)
                    silu(E, 1)
                    high_a(E, 1)

                high_gu(NE * s, 0, NE // 2 * s + 1)
                each_expert(eng, s, body)
                eng.wait_ge(m_d, given(m_d) + 2 * NE * (s + 1))
                if s:
                    eng.wait_ge(m_tt, 4 * s)
                for m in range(2):
                    for tt in range(2):
                        eng.activation(OT[:, 2 * m + tt, :], ps[:, OB[m][tt], :], ACT.Copy).then_inc(m_ot, 1)

        @block.vector
        def _(eng):
            for s in range(SG):
                def low_gu(E, u):
                    eng.wait_ge(m_hg, E + 1)
                    eng.tensor_tensor(wl[:, u, GU], raw[:, u, GU], wh[:, u, GU].bitcast(F32),
                                      ALU.subtract).then_inc(m_lg, 1)

                def low_d(E, u):
                    eng.wait_ge(m_hd, E + 1)
                    eng.tensor_tensor(wl[:, u, DN], raw[:, u, DN], wh[:, u, DN].bitcast(F32),
                                      ALU.subtract).then_inc(m_ld_, 1)

                def mul(E, tt):
                    eng.wait_ge(m_sw, given(m_sw) + 2 * E + tt + 1)
                    eng.wait_ge(m_u, given(m_u) + 2 * E + tt + 1)
                    eng.wait_ge(m_ah, given(m_ah) + 2 * (E - 1) + tt + 1)
                    eng.tensor_tensor(a[:, tt, :], sw[:, tt, :], ps[:, UB[tt], :], ALU.mult).then_inc(m_a, 1)

                def low_a(E, tt):
                    eng.wait_ge(m_ah, given(m_ah) + 2 * E + tt + 1)
                    eng.tensor_tensor(al[:, tt, :], a[:, tt, :], ah[:, tt, :].bitcast(F32),
                                      ALU.subtract).then_inc(m_al, 1)

                def body(e, E, u, ld):
                    low_d(E, u)
                    mul(E, 0)
                    if not (isinstance(e, int) and e == NE - 1):
                        low_gu(E + 1, 1 - u)
                    low_a(E, 0)
                    mul(E, 1)
                    low_a(E, 1)

                low_gu(NE * s, 0)
                each_expert(eng, s, body)
                for q in range(4):
                    eng.wait_ge(m_tt, 4 * s + q + 1)
                    for r in range(2):
                        i = 8 * s + 2 * q + r
                        eng.tensor_tensor(X[:, i, :], ps[:, q, r * DIM:(r + 1) * DIM], X[:, i, :],
                                          ALU.add).then_inc(m_y, 1)

        @block.gpsimd
        def _(eng):
            for s in range(SG):
                def body(e, E, u, ld):
                    eng.wait_ge(m_wb[u], 16 * ld)
                    for tt in range(2):
                        eng.wait_ge(m_sg, given(m_sg) + 2 * E + tt + 1)
                        eng.wait_ge(m_a, given(m_a) + 2 * (E - 1) + tt + 1)
                        eng.tensor_tensor(sw[:, tt, :], sg[:, tt, :], wb[:, u, tt * UT:(tt + 1) * UT],
                                          ALU.mult).then_inc(m_sw, 1)

                each_expert(eng, s, body)


def layout(inputs):
    import numpy as np
    a = {k: np.asarray(v) for k, v in inputs.items()}
    f = np.float32
    row = lambda v: np.ascontiguousarray(v.reshape(1, -1))
    cols = lambda v: np.ascontiguousarray(v.reshape(-1, P).T)
    c = np.arange(P)
    q = c % SEQ

    def part(name, at):
        gate, up, down = (a[f"L1_ffn_{name}_{k}"] for k in ("gate", "up", "down"))
        if name == "shared":
            gate, up, down = gate[None, at], up[None, at], down[None, :, at]
        up_ = lambda w: w.reshape(-1, EDIM, 2, P).transpose(0, 3, 2, 1).reshape(-1, P, 2 * EDIM)
        return np.concatenate([up_(gate), up_(up), down.transpose(0, 2, 1)], axis=2)

    ew = np.concatenate([part("expert", None), part("shared", slice(0, EDIM)),
                         part("shared", slice(EDIM, 2 * EDIM))], axis=0)
    arrays = {
        "x": a["x"].reshape(TOK, DIM),
        "ctxT": a["ctx_512"].reshape(BATCH * CTX, CDIM).T,
        "wq1": a["L0_xattn_Wq"].T, "wkv1": a["L0_xattn_Wkv"].T, "wo1": a["L0_xattn_Wo"].T,
        "wqkv2": a["L0_attn_w_attn"], "bqk2": cols(a["L0_attn_b_attn"][:2 * DIM]),
        "bv2": row(a["L0_attn_b_attn"][2 * DIM:]),
        "wproj": a["L0_attn_w_proj"], "bproj": row(a["L0_attn_b_proj"]),
        "wg3": a["L0_ffn_w_gate"].T, "wu3": a["L0_ffn_w_up"].T, "wd3": a["L0_ffn_w_down"].T,
        "wq4": a["L1_xattn_Wq"], "wk4": a["L1_xattn_Wk"], "wv4": a["L1_xattn_Wv"],
        "bqk4": np.concatenate([cols(a["L1_xattn_bq"]), cols(a["L1_xattn_bk"])], axis=1),
        "bv4": row(a["L1_xattn_bv"]),
        "wqkv5": a["L1_attn_W"].T, "bqk5": cols(a["L1_attn_b"][:2 * DIM]), "bv5": row(a["L1_attn_b"][2 * DIM:]),
        "wr6": a["L1_ffn_gate_w"].T, "br6": row(a["L1_ffn_gate_bias"]),
        "ew6": ew,
        "c_ident": np.eye(P, dtype=f),
        "c_headmask": (c[:, None] // HD == np.arange(8)[None]).astype(f),
        "c_oddmask": ((c[:, None] // HD) % 2 == np.arange(2)[None]).astype(f),
        "c_causal": np.where(np.arange(SEQ)[None] > q[:, None], NEG, 0.0).astype(f),
        "c_ones": np.ones((P, P), f),
    }
    return {k: np.ascontiguousarray(v) for k, v in arrays.items()}


def kernel(**inputs):
    import concourse.bacc as bacc
    from concourse.bass_utils import run_bass_kernel_spmd

    nc = bacc.Bacc("TRN2", target_bir_lowering=False, num_devices=1)
    arrays = {"in_" + k: v for k, v in layout(inputs).items()}
    io = {k[3:]: nc.dram_tensor(k, v.shape, mybir.dt.from_np(v.dtype), kind="ExternalInput").ap()
          for k, v in arrays.items()}
    out = nc.dram_tensor("out", (TOK, DIM), F32, kind="ExternalOutput").ap()
    build(nc, io, out)
    r = run_bass_kernel_spmd(nc, [arrays], core_ids=[0])
    return r.results[0]["out"].reshape(BATCH, SEQ, DIM)
```

```python
import concourse.bass as bass
from concourse import mybir
from contextlib import ExitStack

F32 = mybir.dt.float32
F32R = mybir.dt.float32r
BF16 = mybir.dt.bfloat16
ALU = mybir.AluOpType
ACT = mybir.ActivationFunctionType
AX = mybir.AxisListType

P = 128
BATCH, SEQ, DIM = 32, 64, 256
CTX, CDIM = 256, 128
HEADS = 16
HD = DIM // HEADS
TOK = BATCH * SEQ
NPAIR = TOK // P
HALF = 2
INNER = 1024
EXPERTS, EDIM, TOPK = 32, 128, 8
NE = EXPERTS + 2
EPS = 1e-5
ROUND = 12582912.0
SCALE = float(HD) ** -0.5
NEG = -1e30


GIVEN = {}


def given(s):
    return GIVEN.get(s.name, 0)


def known(i, low):
    return isinstance(i, int) and i < low


def upto(n, most):
    return min(n, most) if isinstance(n, int) else n


def pipeline(eng, body, once=None):
    body(-1, 1, True, False, False, 1)
    body(0, 0, True, True, False, 1)
    if once:
        once()
    with eng.Fori(0, (NPAIR - 2) // 2) as j:
        body(2 * j + 1, 1, True, True, True, j + 2)
        body(2 * j + 2, 0, True, True, True, j + 2)
    body(NPAIR - 1, 1, False, True, True, 0)
    body(NPAIR, 0, False, False, True, 0)


def long_pipeline(eng, body):
    body(-1, 1, True, False, False, False, 1)
    body(0, 0, True, True, False, False, 1)
    body(1, 1, True, True, True, False, 2)
    with eng.Fori(0, (NPAIR - 4) // 2) as j:
        body(2 * j + 2, 0, True, True, True, True, j + 2)
        body(2 * j + 3, 1, True, True, True, True, j + 3)
    body(NPAIR - 2, 0, True, True, True, True, NPAIR // 2)
    body(NPAIR - 1, 1, False, True, True, True, 0)
    body(NPAIR, 0, False, False, True, True, 0)
    body(NPAIR + 1, 1, False, False, False, True, 0)


def prev_use(ring, i, k):
    n = len(ring)
    d = next(d for d in range(1, n + 1) if ring[(k - d) % n] == ring[k])
    return n * i + k - d + 1


def build(nc, io, out, stages=6):
    with ExitStack() as ctx:
        def sb(name, shape, dt=F32):
            return ctx.enter_context(nc.sbuf_tensor(name, list(shape), dt))

        credits = {"tensor": [], "vector": [], "scalar": [], "gpsimd": []}

        def sem(name, credit=0, by=None):
            s = ctx.enter_context(nc.semaphore(name))
            if credit:
                GIVEN[s.name] = credit
                credits[by].append(s)
            return s

        ps = ctx.enter_context(nc.psum_tensor("ps", [P, 8, 512], F32))

        X = sb("X", [P, NPAIR, DIM])
        ident = sb("ident", [P, P])
        headmask = sb("headmask", [P, 8])
        oddmask = sb("oddmask", [P, 2])
        causal = sb("causal", [P, SEQ])
        ones = sb("ones", [P, P])

        lnstat = sb("lnstat", [P, 2, 6])
        lnmv = sb("lnmv", [P, 2, 2])
        lneps = sb("lneps", [P, 2, 1])
        lnrs = sb("lnrs", [P, 2, 1])
        mhalf = sb("mhalf", [P, 1])
        epsc = sb("epsc", [P, 1])
        h = sb("h", [P, 2, DIM])
        hT = sb("hT", [P, 2, HALF, P])

        bqs = {2: sb("bqs2", [P, 2]), 5: sb("bqs5", [P, 2])}
        wr6 = sb("wr6", [P, 2, EXPERTS]); br6 = sb("br6", [P, EXPERTS])
        wdram = nc.dram_tensor("token_weights", (NE, TOK), F32, kind="Internal").ap()
        identb = sb("identb", [P, P], BF16)
        wq3 = [sb("wq3g", [P, 2, INNER], BF16), sb("wq3u", [P, 2, INNER], BF16), sb("wq3d", [P, 8, DIM], BF16)]
        wsc = sb("wsc", [P, 3]); wrs = sb("wrs", [P, 3])
        s_const = sem("s_const")
        s_x0 = sem("s_x0"); s_x = sem("s_x")
        s_half = sem("s_half")
        s_w1 = sem("s_w1")
        s_xdone = sem("s_xdone", 1, "vector")
        ln_st = sem("ln_st")
        ln_mv = sem("ln_mv")
        ln_eps = sem("ln_eps")
        ln_rs = sem("ln_rs")
        ln_h = sem("ln_h")
        ln_T = sem("ln_T", 2, "tensor")
        ln_hT = sem("ln_hT")

        wq1 = sb("wq1", [P, 2, DIM]); wkv1 = sb("wkv1", [P, 2 * DIM]); wo1 = sb("wo1", [P, 2, DIM])
        wqkv = {2: sb("wqkv2", [P, 2, 3 * DIM]), 5: sb("wqkv5", [P, 2, 3 * DIM])}
        bqk = {2: sb("bqk2", [P, 4]), 5: sb("bqk5", [P, 4])}
        bv = {2: sb("bv2", [P, DIM]), 5: sb("bv5", [P, DIM]), 4: sb("bv4", [P, DIM])}
        wproj = sb("wproj", [P, 2, DIM]); bproj = sb("bproj", [P, DIM])
        wq4 = sb("wq4", [P, 2, DIM]); wk4 = sb("wk4", [P, DIM]); wv4 = sb("wv4", [P, DIM])
        bqk4 = sb("bqk4", [P, 4])

        def cin(v):
            return v.rearrange("(c p) n -> p c n", p=P)

        const_loads = [
            (ident, io["c_ident"]), (wq1, cin(io["wq1"])), (headmask, io["c_headmask"]),
            (wkv1, io["wkv1"]), (oddmask, io["c_oddmask"]), (wo1, cin(io["wo1"])), (ones, io["c_ones"]),
        ]
        late_loads = [
            (causal, io["c_causal"]),
            (wqkv[2], cin(io["wqkv2"])), (wqkv[5], cin(io["wqkv5"])),
            (bqk[2], io["bqk2"]), (bqk[5], io["bqk5"]), (bqk4, io["bqk4"]),
            (bv[2], io["bv2"].partition_broadcast(P)), (bv[5], io["bv5"].partition_broadcast(P)),
            (bv[4], io["bv4"].partition_broadcast(P)),
            (wproj, cin(io["wproj"])), (bproj, io["bproj"].partition_broadcast(P)),
            (wq4, cin(io["wq4"])), (wk4, io["wk4"]), (wv4, io["wv4"]),
            (wr6, cin(io["wr6"])), (br6, io["br6"].partition_broadcast(P)),
        ]

        lnt = [0, NPAIR, None, 2 * NPAIR, 3 * NPAIR, 4 * NPAIR]

        def ln_dve(eng, n, i, u):
            b = NPAIR * n
            if n == 0:
                if known(i, 2):
                    eng.wait_ge(s_x0, 16)
                else:
                    eng.wait_ge(s_x, 32)
            else:
                eng.wait_ge(s_xdone, given(s_xdone) + b - NPAIR + i + 1)
            eng.bn_stats(lnstat[:, u, :], X[:, i, :]).then_inc(ln_st, 1)
            eng.wait_ge(ln_st, b + i + 1)
            eng.nop(nofuse=True)
            eng.bn_aggr(lnmv[:, u, :], lnstat[:, u, :]).then_inc(ln_mv, 1)

        def ln_dve2(eng, n, i, u, reader=None, _=0):
            b = NPAIR * n
            eng.wait_ge(ln_rs, b + i + 1)
            if reader is None:
                eng.wait_ge(ln_T, given(ln_T) + lnt[n] + i - 1)
            eng.tensor_scalar(h[:, u, :], X[:, i, :], lnmv[:, u, 0:1], lnrs[:, u, :],
                              ALU.subtract, ALU.mult).then_inc(ln_h, 1)

        def ln_pool(eng, n, i, u):
            b = NPAIR * n
            eng.wait_ge(ln_mv, b + i + 1)
            eng.tensor_tensor(lneps[:, u, :], lnmv[:, u, 1:2], epsc[:, :], ALU.add).then_inc(ln_eps, 1)
            eng.wait_ge(ln_eps, b + i + 1)
            eng.tensor_tensor(lnrs[:, u, :], lneps[:, u, :], mhalf[:, :], ALU.pow).then_inc(ln_rs, 1)

        def transpose2(eng, dst, src):
            for c in range(HALF):
                ins = eng.transpose(dst[:, c * P:(c + 1) * P], src[:, c * P:(c + 1) * P], ident[:, :])
            return ins

        def ln_pe(eng, n, i, u, bank):
            eng.wait_ge(ln_h, NPAIR * n + i + 1)
            transpose2(eng, ps[:, bank, :], h[:, u, :]).then_inc(ln_T, 1)

        def ln_act(eng, n, i, u, bank, readers=None):
            eng.wait_ge(ln_T, given(ln_T) + lnt[n] + i + 1)
            if readers is not None:
                readers()
            eng.activation(hT[:, u, :, :], ps[:, bank, 0:DIM], ACT.Copy).then_inc(ln_hT, 1)

        Vs = sb("Vs", [P, 2, 2, DIM])
        with nc.Block() as block:
            @block.sync
            def _(sp):
                xin = io["x"].rearrange("(n p) d -> p n d", p=P)
                sp.dma_start(X[:, 0:2, :], xin[:, 0:2, :]).then_inc(s_x0, 16)
                for dst, src in const_loads:
                    sp.dma_start(dst[:], src).then_inc(s_const, 16)

            @block.vector
            def _(eng):
                eng.memset(mhalf[:, :], -0.5).then_inc(s_half, 1)
                eng.memset(epsc[:, :], EPS).then_inc(s_half, 1)
                eng.memset(Vs[:, :, :, :], 0.0).then_inc(s_half, 1)

        def give(eng, name):
            for s in credits[name]:
                eng.sem_inc(s, given(s))
            credits[name].clear()

        env = dict(locals())
        number = [0]

        def local(*layers):
            with ExitStack() as stack:
                number[0] += 1
                env["sb"] = lambda name, shape, dt=F32: stack.enter_context(
                    nc.sbuf_tensor(f"{name}_{number[0]}", list(shape), dt))
                for layer, *args in layers:
                    layer(nc, ctx, env, *args)

        if stages >= 1:
            local((cross_heads,))
        if stages >= 2:
            local((self_heads, 2))
        if stages >= 3:
            local((quantised_ffn,))
        if stages >= 4:
            local((cross_single,))
        if stages >= 5:
            local((self_heads, 5))
        if stages >= 6:
            local((router,), (experts,))
            return
        with nc.Block() as block:
            @block.sync
            def _(sp):
                sp.wait_ge(s_xdone, given(s_xdone) + NPAIR * stages)
                sp.dma_start(out.rearrange("(n p) d -> p n d", p=P), X[:, :, :]).then_inc(s_x, 16)
                sp.wait_ge(s_x, 48)


def cross_heads(nc, ctx, env):
    g = env
    sb, sem, ps, X, io = g["sb"], g["sem"], g["ps"], g["X"], g["io"]
    ident, headmask, oddmask, hT = g["ident"], g["headmask"], g["oddmask"], g["hT"]
    ln_dve, ln_dve2, ln_pool, ln_pe, ln_act, transpose2 = (g[k] for k in (
        "ln_dve", "ln_dve2", "ln_pool", "ln_pe", "ln_act", "transpose2"))
    ln_hT, ln_T, s_xdone = g["ln_hT"], g["ln_T"], g["s_xdone"]
    wq, wkv, wo = g["wq1"], g["wkv1"], g["wo1"]

    NS = 8
    cx = sb("cx", [P, 2, 2 * CTX])
    cxh = sb("cxh", [P, 2 * CTX], F32R); cxl = sb("cxl", [P, 2 * CTX], F32R)
    wkvh = sb("wkvh", [P, 2 * DIM], F32R); wkvl = sb("wkvl", [P, 2 * DIM], F32R)
    Qs = sb("Qs", [P, 2, HALF, P])
    Qh = sb("Qh", [P, 2, HALF, P], F32R); Ql = sb("Ql", [P, HALF, P])
    Qbh = sb("Qbh", [P, 2, HALF, 2, 8 * SEQ], F32R)
    Qbl = sb("Qbl", [P, 2, HALF, 2, 8 * SEQ], F32R)
    KTh = sb("KTh", [P, 2, HALF, 2 * CTX], F32R); KTl = sb("KTl", [P, 2, HALF, 2 * CTX], F32R)
    V = sb("V", [P, 2, 4, DIM])
    Pr = sb("Pr", [P, 4, 2, CTX])
    PT = sb("PT", [P, 2, 2, 2, P])
    mx = sb("mx", [P, 3, 2])
    den = sb("den", [P, 2, 2, HALF, 4])
    rden = sb("rden", [P, HALF, 4, 2])
    Oe = sb("Oe", [P, 2 * HALF, SEQ])
    OT = sb("OT", [P, 2, 2 * HALF, SEQ])
    On = sb("On", [P, 2, DIM])
    OnT = sb("OnT", [P, 2, HALF, P])

    raw3 = [sb("raw3g", [P, 2, INNER]), sb("raw3u", [P, 2, INNER]), sb("raw3d", [P, 8, DIM])]
    QW = 2 * INNER // NPAIR
    rounded = sb("rounded3", [P, 3, QW])
    absw = sb("absw3", [P, 2 * INNER]); part = sb("part3", [P, 3])
    wq3, wsc, wrs, ones = g["wq3"], g["wsc"], g["wrs"], g["ones"]

    SB = [0, 1, 2, 0, 1, 2, 0, 1]
    TB = [3, 4]
    OB = 5
    FA, FB = 6, 7
    last = 2 * NPAIR

    c_ld = [sem("c_ld0"), sem("c_ld1")]
    c_q = sem("c_q", 2, "tensor"); c_qe = sem("c_qe"); c_qbd = sem("c_qbd", 9, "gpsimd"); c_ql = sem("c_ql")
    c_k = sem("c_k", 3, "tensor"); c_kh = sem("c_kh"); c_ke = sem("c_ke"); c_w = sem("c_w"); c_cxh = sem("c_cxh"); c_cxl = sem("c_cxl", 2, "gpsimd")
    c_v = sem("c_v", 3, "tensor"); c_ve = sem("c_ve", 2, "scalar")
    c_s = sem("c_s", 9, "tensor"); c_max = sem("c_max");
    c_exp = sem("c_exp", 3, "scalar")
    c_t = sem("c_t", 4, "tensor"); c_te = sem("c_te", 2, "vector"); c_pv = sem("c_pv", 9, "tensor")
    c_o1 = sem("c_o1"); c_o2 = sem("c_o2", 1, "vector"); c_rd = sem("c_rd", 8, "vector")
    c_t1 = sem("c_t1", 2, "tensor"); c_on = sem("c_on")
    c_t2 = sem("c_t2", 2, "tensor"); c_t2e = sem("c_t2e", 2, "scalar"); c_wo = sem("c_wo", 2, "tensor")

    q_ld = sem("q_ld"); q_part = sem("q_part"); q_sum = sem("q_sum"); q_sc = sem("q_sc"); q_rs = sem("q_rs")
    q_r = sem("q_r"); q_c = sem("q_c"); s_q3 = sem("s_q3")
    s_const, s_half, s_w1, s_x = g["s_const"], g["s_half"], g["s_w1"], g["s_x"]
    all_consts = 16 * len(g["const_loads"])

    order = [(half, b, s) for half in range(HALF) for b in range(2) for s in range(2)]

    with nc.Block() as block:
        @block.sync
        def _(sp):
            ctxT = io["ctxT"].rearrange("p (n c) -> p n c", c=2 * CTX)

            def load(i, u):
                sp.wait_ge(c_cxl, given(c_cxl) + i - 1)
                sp.dma_start(cx[:, u, :], ctxT[:, i, :]).then_inc(c_ld[u], 16)

            load(0, 0)
            load(1, 1)
            xin = io["x"].rearrange("(n p) d -> p n d", p=P)
            sp.dma_start(X[:, 2:4, :], xin[:, 2:4, :]).then_inc(s_x, 16)
            for n, name in enumerate(("wg3", "wu3", "wd3")):
                sp.dma_start(raw3[n][:, :, :], io[name].rearrange("(c p) n -> p c n", p=P)).then_inc(q_ld, 16)
            sp.dma_start(X[:, 4:NPAIR, :], xin[:, 4:NPAIR, :]).then_inc(s_x, 16)
            for dst, src in g["late_loads"]:
                sp.dma_start(dst[:], src).then_inc(s_w1, 16)
            with sp.Fori(1, NPAIR // 2) as j:
                load(2 * j, 0)
                load(2 * j + 1, 1)

        @block.tensor
        def _(eng):
            g["give"](eng, "tensor")
            eng.wait_ge(s_const, all_consts)
            def scores(i, u, k):
                half, b, s = order[k]
                if k % 4 == 0:
                    eng.wait_ge(c_qbd, given(c_qbd) + 8 * i + 4 * half + 4)
                    eng.wait_ge(c_ke, 2 * i + half + 1)
                eng.wait_ge(c_exp, given(c_exp) + prev_use(SB, i, k))
                for pl in range(2):
                    p = 2 * s + pl
                    out = ps[:, SB[k], pl * CTX:(pl + 1) * CTX]
                    qh, ql = (q[:, u, half, b, p * P:(p + 1) * P] for q in (Qbh, Qbl))
                    kh, kl = (q[:, u, half, b * CTX:(b + 1) * CTX] for q in (KTh, KTl))
                    eng.matmul(out, qh, kh, start=True, stop=False)
                    eng.matmul(out, qh, kl, start=False, stop=False)
                    ins = eng.matmul(out, ql, kh, start=False, stop=True)
                ins.then_inc(c_s, 1)

            def turn(i, u, k):
                eng.wait_ge(c_exp, given(c_exp) + NS * i + k + 1)
                eng.wait_ge(c_te, given(c_te) + NS * i + k - 1)
                for pl in range(2):
                    for kt in range(2):
                        ins = eng.transpose(ps[:, TB[k % 2], (2 * pl + kt) * P:(2 * pl + kt + 1) * P],
                                            Pr[:, k % 4, pl, kt * P:(kt + 1) * P], ident[:, :])
                ins.then_inc(c_t, 1)

            def pv(i, u, k):
                half, b, s = order[k]
                if k == 0:
                    eng.wait_ge(c_o2, given(c_o2) + i)
                    eng.wait_ge(c_ve, given(c_ve) + 2 * i + 2)
                eng.wait_ge(c_te, given(c_te) + NS * i + k + 1)
                r = 2 * half + b
                for pl in range(2):
                    p = 2 * s + pl
                    for kt in range(2):
                        ins = eng.matmul(ps[32 * p:32 * p + 32, OB, r * P:(r + 1) * P],
                                         V[:, u, 2 * b + kt, half * P + 32 * p:half * P + 32 * p + 32],
                                         PT[:, k % 2, pl, kt, :], start=(kt == 0), stop=(kt == 1),
                                         tile_position=(0, 32 * p))
                ins.then_inc(c_pv, 1)

            def qproj(i, u):
                eng.wait_ge(ln_hT, i + 1)
                for m in range(HALF):
                    for c in range(2):
                        ins = eng.matmul(ps[:, FA, m * P:(m + 1) * P], wq[:, c, m * P:(m + 1) * P],
                                         hT[:, u, c, :], start=(c == 0), stop=(c == 1))
                ins.then_inc(c_q, 1)

            def kproj(i, u, m, ld):
                if m == 0:
                    eng.wait_ge(c_qe, i + 1)
                    eng.wait_ge(c_cxl, given(c_cxl) + i + 1)
                    if known(i, 1):
                        eng.wait_ge(c_w, 2)
                else:
                    if not known(i, 1):
                        eng.wait_ge(s_xdone, given(s_xdone) + i - 1)
                out, w = ps[:, (FA, FB)[m], :], slice(m * P, (m + 1) * P)
                eng.matmul(out, wkvh[:, w], cxh[:, :], start=True, stop=False)
                eng.matmul(out, wkvh[:, w], cxl[:, :], start=False, stop=False)
                eng.matmul(out, wkvl[:, w], cxh[:, :], start=False, stop=True).then_inc(c_k, 1)

            def vproj(i, u, m):
                if m == 0:
                    eng.wait_ge(c_ke, 2 * i + 1)
                else:
                    eng.wait_ge(c_ve, given(c_ve) + 2 * i + 1)
                for t in range(2):
                    out, c = ps[:, FA, t * DIM:(t + 1) * DIM], slice((2 * m + t) * P, (2 * m + t + 1) * P)
                    eng.matmul(out, cxh[:, c], wkvh[:, DIM:2 * DIM], start=True, stop=False)
                    eng.matmul(out, cxl[:, c], wkvh[:, DIM:2 * DIM], start=False, stop=False)
                    ins = eng.matmul(out, cxh[:, c], wkvl[:, DIM:2 * DIM], start=False, stop=True)
                ins.then_inc(c_v, 1)

            def tail1(t, u):
                eng.wait_ge(c_o2, given(c_o2) + t + 1)
                eng.wait_ge(c_ke, upto(2 * (t + 2), last))
                eng.wait_ge(s_xdone, given(s_xdone) + t)
                src = OT[:, u, :, :].rearrange("p r q -> p (r q)")
                transpose2(eng, ps[:, FB, :], src).then_inc(c_t1, 1)

            def tail2(t, u):
                eng.wait_ge(c_on, t + 1)
                transpose2(eng, ps[:, FB, :], On[:, u, :]).then_inc(c_t2, 1)

            def tail3(t, u):
                eng.wait_ge(c_t2e, given(c_t2e) + t + 1)
                for c in range(HALF):
                    ins = eng.matmul(ps[:, FB, 0:DIM], OnT[:, u, c, :], wo[:, c, :],
                                     start=(c == 0), stop=(c == 1))
                ins.then_inc(c_wo, 1)

            def body(i, u, front, mid, tail, ld):
                v = 1 - u

                def step(k):
                    if mid and k < NS:
                        scores(i, u, k)
                    if mid and k >= 2:
                        turn(i, u, k - 2)
                    elif tail and k < 2:
                        turn(i - 1, v, NS - 2 + k)
                    if mid and k >= 3:
                        pv(i, u, k - 3)
                    elif tail and k < 3:
                        pv(i - 1, v, NS - 3 + k)

                step(0)
                step(1)
                if front:
                    eng.wait_ge(c_ve, given(c_ve) + 2 * i + 2)
                    ln_pe(eng, 0, i + 1, v, FA)
                step(2)
                if front:
                    qproj(i + 1, v)
                step(3)
                if tail:
                    tail1(i - 1, v)
                if front:
                    kproj(i + 1, v, 0, ld)
                step(4)
                if tail:
                    tail2(i - 1, v)
                if front:
                    vproj(i + 1, v, 0)
                step(5)
                if tail:
                    tail3(i - 1, v)
                if front:
                    vproj(i + 1, v, 1)
                step(6)
                if front:
                    kproj(i + 1, v, 1, ld)
                step(7)

            def weight_sums():
                eng.wait_ge(q_part, 3)
                eng.wait_ge(c_ke, 4)
                eng.matmul(ps[:, FB, 0:3], ones[:, :], part[:, :], start=True, stop=True).then_inc(q_sum, 1)
                eng.wait_ge(q_sc, 1)

            pipeline(eng, body, weight_sums)

        @block.vector
        def _(eng):
            g["give"](eng, "vector")

            def rowmax(i, k):
                eng.wait_ge(c_s, given(c_s) + NS * i + k + 1)
                eng.tensor_reduce(mx[:, SB[k], :], ps[:, SB[k], :].rearrange("p (a n) -> p a n", a=2),
                                  AX.X, ALU.max, negate=True).then_inc(c_max, 1)

            def turned(i, k):
                eng.wait_ge(c_t, given(c_t) + NS * i + k + 1)
                eng.wait_ge(c_pv, given(c_pv) + NS * i + k - 1)
                eng.tensor_copy(PT[:, k % 2, :, :, :], ps[:, TB[k % 2], :]).then_inc(c_te, 1)

            def k_low(i, u, m):
                eng.wait_ge(c_kh, 2 * i + m + 1)
                eng.tensor_tensor(KTl[:, u, m, :], ps[:, (FA, FB)[m], :], KTh[:, u, m, :].bitcast(F32),
                                  ALU.subtract).then_inc(c_ke, 1)

            def o_out(i, u):
                eng.wait_ge(c_pv, given(c_pv) + NS * i + NS)
                eng.wait_ge(c_t1, given(c_t1) + i - 1)
                O = ps[:, OB, :].rearrange("p (r e q) -> p r e q", r=2 * HALF, e=2)
                eng.tensor_scalar(Oe[:, :, :], O[:, :, 0, :], oddmask[:, 0:1], None,
                                  ALU.mult).then_inc(c_o1, 1)
                eng.wait_ge(c_o1, i + 1)
                eng.scalar_tensor_tensor(out=OT[:, u, :, :], in0=O[:, :, 1, :], scalar=oddmask[:, 1:2],
                                         in1=Oe[:, :, :], op0=ALU.mult, op1=ALU.add).then_inc(c_o2, 1)

            def denominators(t, u):
                eng.wait_ge(c_exp, given(c_exp) + NS * (t + 1))
                for b in range(2):
                    for e in range(2):
                        eng.reciprocal(rden[64 * b:64 * b + 64, :, :, e],
                                       den[64 * e:64 * e + 64, u, b, :, :]).then_inc(c_rd, 1)

            def normalise(t, u):
                eng.wait_ge(c_t1, given(c_t1) + t + 1)
                eng.wait_ge(c_rd, given(c_rd) + 4 * t + 4)
                eng.wait_ge(c_t2, given(c_t2) + t - 1)
                eng.tensor_tensor(On[:, u, :].rearrange("p (h d) -> p h d", d=HD),
                                  ps[:, FB, 0:DIM].rearrange("p (h d) -> p h d", d=HD),
                                  rden[:, :, :, :].rearrange("p a b c -> p (a b c)").unsqueeze(2)
                                  .to_broadcast([P, HEADS, HD]), ALU.mult).then_inc(c_on, 1)

            def add_x(t):
                eng.wait_ge(c_wo, given(c_wo) + t + 1)
                eng.tensor_tensor(X[:, t, :], ps[:, FB, 0:DIM], X[:, t, :], ALU.add).then_inc(s_xdone, 1)

            def quantise(t):
                at = bass.ds(QW * t, QW) if not isinstance(t, int) else slice(QW * t, QW * (t + 1))
                flat = [w[:, :, :].rearrange("p c n -> p (c n)") for w in raw3]
                out = [w[:, :, :].rearrange("p c n -> p (c n)") for w in wq3]
                if not known(t, 1):
                    eng.wait_ge(s_q3, 3 * t)
                else:
                    eng.wait_ge(q_rs, 1)
                eng.nop(nofuse=True)
                for n in range(3):
                    eng.tensor_scalar(rounded[:, n, :], flat[n][:, at], wrs[:, n:n + 1], ROUND, ALU.mult,
                                      ALU.add).then_inc(q_r, 1)
                eng.wait_ge(q_r, 3 * t + 3)
                eng.tensor_scalar(rounded[:, :, :], rounded[:, :, :], ROUND, 1.0, ALU.subtract,
                                  ALU.min).then_inc(q_c, 1)
                eng.wait_ge(q_c, t + 1)
                for n in range(3):
                    eng.tensor_scalar(out[n][:, at], rounded[:, n, :], -1.0, None, ALU.max).then_inc(s_q3, 1)

            def body(i, u, front, mid, tail, ld):
                v = 1 - u
                def step(k):
                    if mid:
                        rowmax(i, k)
                    if mid and k >= 2:
                        turned(i, k - 2)
                    elif tail and k < 2:
                        turned(i - 1, NS - 2 + k)

                if front:
                    ln_dve(eng, 0, i + 1, v)
                step(0)
                if front:
                    ln_dve2(eng, 0, i + 1, v)
                step(1)
                step(2)
                if tail:
                    o_out(i - 1, v)
                if tail:
                    denominators(i - 1, v)
                step(3)
                if tail:
                    normalise(i - 1, v)
                if front:
                    k_low(i + 1, v, 0)
                step(4)
                if tail:
                    quantise(i - 1)
                step(5)
                if tail:
                    add_x(i - 1)
                step(6)
                step(7)
                if front:
                    k_low(i + 1, v, 1)

            def weight_scales():
                eng.wait_ge(q_sum, 1)
                eng.tensor_scalar(wsc[:, :], ps[:, FB, 0:3], 1.0 / (DIM * INNER), 1e-5, ALU.mult,
                                  ALU.max).then_inc(q_sc, 1)
                eng.wait_ge(q_sc, 1)
                eng.reciprocal(wrs[:, :], wsc[:, :]).then_inc(q_rs, 1)

            eng.wait_ge(s_const, all_consts)
            pipeline(eng, body, weight_scales)
            eng.wait_ge(s_w1, 16 * len(g["late_loads"]))
            for n in (2, 5):
                eng.tensor_scalar(g["bqs"][n][:, :], g["bqk"][n][:, 0:2], SCALE, None, ALU.mult)
            eng.tensor_copy(g["identb"][:, :], ident[:, :])

        @block.scalar
        def _(eng):
            g["give"](eng, "scalar")
            def exps(i, u, k):
                half, b, s = order[k]
                eng.wait_ge(c_max, NS * i + k + 1)
                eng.wait_ge(c_t, given(c_t) + NS * i + k - 3)
                if k == 0:
                    eng.wait_ge(c_rd, given(c_rd) + 4 * (i - 1))
                for pl in range(2):
                    ins = eng.activation(Pr[:, k % 4, pl, :], ps[:, SB[k], pl * CTX:(pl + 1) * CTX], ACT.Exp,
                                         bias=mx[:, SB[k], pl:pl + 1],
                                         accum_out=den[:, u, b, half, 2 * s + pl:2 * s + pl + 1])
                ins.then_inc(c_exp, 1)

            def q_out(i, u):
                eng.wait_ge(c_q, given(c_q) + i + 1)
                eng.wait_ge(c_qbd, given(c_qbd) + 8 * (i - 1))
                eng.activation(Qh[:, u, :, :], ps[:, FA, 0:DIM], ACT.Copy, scale=SCALE)
                eng.activation(Qs[:, u, :, :], ps[:, FA, 0:DIM], ACT.Copy, scale=SCALE).then_inc(c_qe, 1)

            def k_out(i, u, m):
                eng.wait_ge(c_k, given(c_k) + 2 * i + m + 1)
                eng.wait_ge(c_s, given(c_s) + NS * (i - 1))
                eng.activation(KTh[:, u, m, :], ps[:, (FA, FB)[m], :], ACT.Copy).then_inc(c_kh, 1)

            def cx_high(i, u, ld):
                eng.wait_ge(c_ld[u], 16 * ld)
                eng.wait_ge(c_k, given(c_k) + 2 * i)
                eng.activation(cxh[:, :], cx[:, u, :], ACT.Copy).then_inc(c_cxh, 1)

            def v_out(i, u, m):
                eng.wait_ge(c_v, given(c_v) + 2 * i + m + 1)
                eng.wait_ge(c_pv, given(c_pv) + NS * (i - 1))
                eng.activation(V[:, u, 2 * m:2 * m + 2, :], ps[:, FA, :],
                               ACT.Copy).then_inc(c_ve, 1)

            def ot_out(t, u):
                eng.wait_ge(c_t2, given(c_t2) + t + 1)
                eng.wait_ge(c_wo, given(c_wo) + t - 1)
                eng.activation(OnT[:, u, :, :], ps[:, FB, 0:DIM], ACT.Copy).then_inc(c_t2e, 1)

            def weight_part(n):
                eng.wait_ge(q_ld, 48)
                if n:
                    eng.wait_ge(q_part, n)
                eng.activation(absw[:, :], raw3[n][:, :, :].rearrange("p c n -> p (c n)"), ACT.Abs,
                               accum_out=part[:, n:n + 1]).then_inc(q_part, 1)

            def body(i, u, front, mid, tail, ld):
                v = 1 - u

                def ex(*ks):
                    if mid:
                        for k in ks:
                            exps(i, u, k)
                ex(0)
                if front:
                    cx_high(i + 1, v, ld)
                ex(1)
                if front:
                    ln_act(eng, 0, i + 1, v, FA, lambda: eng.wait_ge(c_q, given(c_q) + i))
                ex(2)
                if mid and known(i, 1):
                    weight_part(0)
                if front:
                    q_out(i + 1, v)
                ex(3)
                if front:
                    k_out(i + 1, v, 0)
                ex(4)
                if mid and known(i, 1):
                    weight_part(1)
                if tail:
                    ot_out(i - 1, v)
                if front:
                    v_out(i + 1, v, 0)
                ex(5)
                if front:
                    v_out(i + 1, v, 1)
                ex(6)
                if mid and known(i, 1):
                    weight_part(2)
                if front:
                    k_out(i + 1, v, 1)
                ex(7)

            eng.wait_ge(s_const, all_consts)
            eng.activation(wkvh[:, :], wkv[:, :], ACT.Copy).then_inc(c_w, 1)
            pipeline(eng, body)

        @block.gpsimd
        def _(eng):
            g["give"](eng, "gpsimd")
            eng.wait_ge(s_half, 2)
            eng.wait_ge(s_const, all_consts)

            eng.wait_ge(c_w, 1)
            eng.tensor_tensor(wkvl[:, :], wkv[:, :], wkvh[:, :].bitcast(F32), ALU.subtract).then_inc(c_w, 1)

            def cx_low(i, u):
                eng.wait_ge(c_cxh, i + 1)
                eng.wait_ge(c_k, given(c_k) + 2 * i)
                eng.tensor_tensor(cxl[:, :], cx[:, u, :], cxh[:, :].bitcast(F32), ALU.subtract).then_inc(c_cxl, 1)

            def spread(i, u):
                eng.wait_ge(c_qe, i + 1)
                eng.wait_ge(c_qbd, given(c_qbd) + 8 * i)
                eng.tensor_tensor(Ql[:, :, :], Qs[:, u, :, :], Qh[:, u, :, :].bitcast(F32),
                                  ALU.subtract).then_inc(c_ql, 1)
                eng.wait_ge(c_ql, i + 1)
                eng.wait_ge(c_s, given(c_s) + NS * (i - 1))
                for half in range(HALF):
                    for src, dst in ((Qh[:, u, :, :].bitcast(F32), Qbh), (Ql[:, :, :], Qbl)):
                        for b in range(2):
                            eng.tensor_tensor(
                                dst[:, u, half, b, :].rearrange("p (j q) -> p j q", q=SEQ),
                                src[:, half, b * SEQ:(b + 1) * SEQ].unsqueeze(1).to_broadcast([P, 8, SEQ]),
                                headmask[:, :].unsqueeze(2).to_broadcast([P, 8, SEQ]),
                                ALU.mult).then_inc(c_qbd, 1)

            def body(i, u, front, mid, tail, ld):
                if front:
                    ln_pool(eng, 0, i + 1, 1 - u)
                    cx_low(i + 1, 1 - u)
                    spread(i + 1, 1 - u)

            pipeline(eng, body)


def self_heads(nc, ctx, env, layer):
    g = env
    sb, sem, ps, X = g["sb"], g["sem"], g["ps"], g["X"]
    ident, headmask, oddmask, causal, hT = g["ident"], g["headmask"], g["oddmask"], g["causal"], g["hT"]
    ln_dve, ln_dve2, ln_pool, ln_pe, ln_act, transpose2 = (g[k] for k in (
        "ln_dve", "ln_dve2", "ln_pool", "ln_pe", "ln_act", "transpose2"))
    ln_hT, s_xdone = g["ln_hT"], g["s_xdone"]
    w, bqk, bv = g["wqkv"][layer], g["bqk"][layer], g["bv"][layer]
    proj = layer == 2
    bqs = g["bqs"][layer]
    wproj, bproj = g["wproj"], g["bproj"]
    L = layer - 1
    base = NPAIR * L
    Qs = sb("Qs", [P, 2, HALF, P])
    Qbd = sb("Qbd", [P, 2, HALF, 2, 8 * SEQ])
    KT = sb("KT", [P, 2, HALF, P])
    V = g["Vs"]
    Sm = sb("Sm", [P, 4, 2, 2, SEQ])
    Pr = sb("Pr", [P, 4, 2, P])
    PT = sb("PT", [P, 2, 2, P])
    mx = sb("mx", [P, 4, 4])
    den = sb("den", [P, 2, HALF, 4, 2])
    rden = sb("rden", [P, HALF, 4, 2])
    Oe = sb("Oe", [P, 2 * HALF, SEQ])
    OT = sb("OT", [P, 2, 2 * HALF, SEQ])
    On = sb("On", [P, 2, DIM])
    OnT = sb("OnT", [P, 2, HALF, P])
    xb = sb("xb", [P, 2, DIM])

    NS = 4
    SB = [0, 1, 2, 0]
    TB = [3, 4]
    OB = 5
    FA, FB = 6, 7
    per_pair = {"qk": 1, "qke": 4, "qbd": 4, "v": 1, "ve": 2, "s": 4, "m": 4, "max": 4, "exp": 4, "t": 4, "te": 4,
                "pv": 4, "o1": 1, "o2": 1, "rd": 4, "t1": 1, "on": 1, "t2": 1, "t2e": 1, "wo": 1, "xb": 1}

    def counter(name, credit=0, by=None):
        if layer == 2:
            g["a_" + name] = sem("a_" + name, credit, by)
        else:
            GIVEN[g["a_" + name].name] = credit + per_pair[name] * NPAIR
        return g["a_" + name]

    a_qk = counter("qk", 2, "tensor"); a_qke = counter("qke"); a_qbd = counter("qbd", 5, "gpsimd")
    a_v = counter("v"); a_ve = counter("ve")
    a_s = counter("s", 5, "tensor"); a_m = counter("m", 3, "vector"); a_max = counter("max")
    a_exp = counter("exp", 5, "scalar");
    a_t = counter("t", 5, "tensor"); a_te = counter("te", 2, "scalar"); a_pv = counter("pv", 5, "tensor")
    a_o1 = counter("o1"); a_o2 = counter("o2", 1, "vector"); a_rd = counter("rd", 8, "vector")
    a_t1 = counter("t1", 2, "tensor"); a_on = counter("on", 2, "vector")
    a_t2 = counter("t2", 2, "tensor"); a_t2e = counter("t2e", 2, "scalar"); a_wo = counter("wo", 2, "tensor")
    a_xb = counter("xb")

    with nc.Block() as block:
        @block.tensor
        def _(eng):
            g["give"](eng, "tensor")
            def scores(i, u, k):
                half, s = divmod(k, 2)
                if s == 0:
                    eng.wait_ge(a_qbd, given(a_qbd) + 4 * i + 2 * half + 2)
                eng.wait_ge(a_m, given(a_m) + prev_use(SB, i, k))
                for pl in range(2):
                    p = 2 * s + pl
                    for b in range(2):
                        ins = eng.matmul(ps[:, SB[k], (2 * pl + b) * P:(2 * pl + b + 1) * P],
                                         Qbd[:, u, half, b, p * P:(p + 1) * P], KT[:, u, half, :],
                                         start=True, stop=True)
                ins.then_inc(a_s, 1)

            def turn(i, u, k):
                eng.wait_ge(a_exp, given(a_exp) + NS * i + k + 1)
                eng.wait_ge(a_te, given(a_te) + NS * i + k - 1)
                for pl in range(2):
                    ins = eng.transpose(ps[:, TB[k % 2], pl * P:(pl + 1) * P],
                                        Pr[:, k, pl, :], ident[:, :])
                ins.then_inc(a_t, 1)

            def pv(i, u, k):
                half, s = divmod(k, 2)
                if k == 0:
                    eng.wait_ge(a_o2, given(a_o2) + i)
                    eng.wait_ge(a_ve, given(a_ve) + 2 * i + 2)
                eng.wait_ge(a_te, given(a_te) + NS * i + k + 1)
                for b in range(2):
                    r = 2 * half + b
                    for pl in range(2):
                        p = 2 * s + pl
                        ins = eng.matmul(ps[32 * p:32 * p + 32, OB, r * P:(r + 1) * P],
                                         V[:, u, b, half * P + 32 * p:half * P + 32 * p + 32],
                                         PT[:, k % 2, pl, :], start=True, stop=True,
                                         tile_position=(0, 32 * p))
                ins.then_inc(a_pv, 1)

            def qkproj(i, u):
                eng.wait_ge(ln_hT, g["lnt"][L] + i + 1)
                for m in range(4):
                    for c in range(2):
                        ins = eng.matmul(ps[:, FA, m * P:(m + 1) * P], w[:, c, m * P:(m + 1) * P],
                                         hT[:, u, c, :], start=(c == 0), stop=(c == 1))
                ins.then_inc(a_qk, 1)

            def vproj(i, u):
                eng.wait_ge(a_qke, given(a_qke) + 4 * i + 4)
                for c in range(2):
                    ins = eng.matmul(ps[:, FA, 0:DIM], hT[:, u, c, :], w[:, c, 2 * DIM:3 * DIM],
                                     start=(c == 0), stop=(c == 1))
                ins.then_inc(a_v, 1)

            def tail1(t, u):
                eng.wait_ge(a_o2, given(a_o2) + t + 1)
                if proj:
                    eng.wait_ge(s_xdone, given(s_xdone) + base + t)
                else:
                    eng.wait_ge(a_on, given(a_on) + t)
                src = OT[:, u, :, :].rearrange("p r q -> p (r q)")
                transpose2(eng, ps[:, FB, :], src).then_inc(a_t1, 1)

            def tail2(t, u):
                eng.wait_ge(a_on, given(a_on) + t + 1)
                transpose2(eng, ps[:, FB, :], On[:, u, :]).then_inc(a_t2, 1)

            def tail3(t, u):
                eng.wait_ge(a_t2e, given(a_t2e) + t + 1)
                for c in range(HALF):
                    ins = eng.matmul(ps[:, FB, 0:DIM], OnT[:, u, c, :], wproj[:, c, :],
                                     start=(c == 0), stop=(c == 1))
                ins.then_inc(a_wo, 1)

            def body(i, u, front, mid, tail, late, ld):
                v = 1 - u

                def step(k, between=None):
                    if mid:
                        scores(i, u, k)
                    if mid and k >= 2:
                        turn(i, u, k - 2)
                    elif tail and k < 2:
                        turn(i - 1, v, NS - 2 + k)
                    if between:
                        between()
                    if mid and k >= 3:
                        pv(i, u, k - 3)
                    elif tail and k < 3:
                        pv(i - 1, v, NS - 3 + k)

                if mid:
                    eng.wait_ge(a_qke, given(a_qke) + 4 * i + 4)
                step(0)
                if late and proj:
                    tail2(i - 2, u)

                def normed():
                    if front:
                        if not known(i, 0):
                            eng.wait_ge(a_ve, given(a_ve) + 2 * i + 2)
                        ln_pe(eng, L, i + 1, v, FA)

                def queries():
                    if front:
                        qkproj(i + 1, v)

                step(1, normed)
                step(2, queries)
                if late and proj:
                    tail3(i - 2, u)

                def values():
                    if tail:
                        tail1(i - 1, v)
                    if front:
                        vproj(i + 1, v)

                step(3, values)

            long_pipeline(eng, body)

        @block.vector
        def _(eng):
            g["give"](eng, "vector")
            def mask(i, k):
                eng.wait_ge(a_s, given(a_s) + NS * i + k + 1)
                eng.wait_ge(a_exp, given(a_exp) + NS * (i - 1) + k + 1)
                S = ps[:, SB[k], :].rearrange("p (a c n) -> p a c n", a=2, c=4)[:, :, 0:4:3, :]
                eng.tensor_tensor(Sm[:, k, :, :, :], S,
                                  causal[:, :].unsqueeze(1).unsqueeze(1).to_broadcast([P, 2, 2, SEQ]),
                                  ALU.add).then_inc(a_m, 1)
                eng.wait_ge(a_m, given(a_m) + NS * i + k + 1)
                eng.tensor_reduce(mx[:, k, :], Sm[:, k, :, :, :], AX.X, ALU.max,
                                  negate=True).then_inc(a_max, 1)

            def v_out(i, u):
                eng.wait_ge(a_v, given(a_v) + i + 1)
                eng.wait_ge(a_pv, given(a_pv) + NS * (i - 1))
                for b in range(2):
                    r = slice(64 * b, 64 * b + 64)
                    eng.tensor_tensor(V[r, u, b, :], ps[r, FA, 0:DIM], bv[r, :], ALU.add).then_inc(a_ve, 1)

            def o_out(i, u):
                eng.wait_ge(a_pv, given(a_pv) + NS * i + NS)
                eng.wait_ge(a_t1, given(a_t1) + i - 1)
                O = ps[:, OB, :].rearrange("p (r e q) -> p r e q", r=2 * HALF, e=2)
                eng.tensor_scalar(Oe[:, :, :], O[:, :, 0, :], oddmask[:, 0:1], None,
                                  ALU.mult).then_inc(a_o1, 1)
                eng.wait_ge(a_o1, given(a_o1) + i + 1)
                eng.scalar_tensor_tensor(out=OT[:, u, :, :], in0=O[:, :, 1, :], scalar=oddmask[:, 1:2],
                                         in1=Oe[:, :, :], op0=ALU.mult, op1=ALU.add).then_inc(a_o2, 1)

            def denominators(t, u):
                eng.wait_ge(a_exp, given(a_exp) + NS * (t + 1))
                eng.wait_ge(a_on, given(a_on) + t)
                for b in range(2):
                    for e in range(2):
                        eng.reciprocal(rden[64 * b:64 * b + 64, :, :, e],
                                       den[64 * e:64 * e + 64, u, :, :, b]).then_inc(a_rd, 1)

            def normalise(t, u):
                eng.wait_ge(a_t1, given(a_t1) + t + 1)
                eng.wait_ge(a_rd, given(a_rd) + 4 * t + 4)
                if proj:
                    eng.wait_ge(a_t2, given(a_t2) + t - 1)
                eng.tensor_tensor(On[:, u, :].rearrange("p (h d) -> p h d", d=HD),
                                  ps[:, FB, 0:DIM].rearrange("p (h d) -> p h d", d=HD),
                                  rden[:, :, :, :].rearrange("p a b c -> p (a b c)").unsqueeze(2)
                                  .to_broadcast([P, HEADS, HD]), ALU.mult).then_inc(a_on, 1)

            def add_x(t, u):
                if proj:
                    eng.wait_ge(a_wo, given(a_wo) + t + 1)
                    eng.wait_ge(a_xb, given(a_xb) + t + 1)
                    eng.tensor_tensor(X[:, t, :], ps[:, FB, 0:DIM], xb[:, u, :],
                                      ALU.add).then_inc(s_xdone, 1)
                else:
                    eng.wait_ge(a_on, given(a_on) + t + 1)
                    eng.tensor_tensor(X[:, t, :], On[:, u, :], X[:, t, :], ALU.add).then_inc(s_xdone, 1)

            def body(i, u, front, mid, tail, late, ld):
                v = 1 - u
                if front:
                    ln_dve(eng, L, i + 1, v)
                if mid:
                    mask(i, 0)
                if front:
                    ln_dve2(eng, L, i + 1, v)
                if mid:
                    mask(i, 1)
                if tail:
                    denominators(i - 1, v)
                if mid:
                    mask(i, 2)
                if tail:
                    o_out(i - 1, v)
                if late and proj:
                    add_x(i - 2, u)
                if mid:
                    mask(i, 3)
                if tail:
                    normalise(i - 1, v)
                if tail and not proj:
                    add_x(i - 1, v)
                if front:
                    v_out(i + 1, v)

            long_pipeline(eng, body)

        @block.scalar
        def _(eng):
            g["give"](eng, "scalar")
            def exps(i, u, k):
                half, s = divmod(k, 2)
                eng.wait_ge(a_max, given(a_max) + NS * i + k + 1)
                eng.wait_ge(a_t, given(a_t) + NS * (i - 1) + k + 1)
                if k == 0:
                    eng.wait_ge(a_rd, given(a_rd) + 4 * (i - 1))
                for pl in range(2):
                    for b in range(2):
                        ins = eng.activation(Pr[:, k, pl, b * SEQ:(b + 1) * SEQ], Sm[:, k, pl, b, :], ACT.Exp,
                                             bias=mx[:, k, 2 * pl + b:2 * pl + b + 1],
                                             accum_out=den[:, u, half, 2 * s + pl, b:b + 1])
                ins.then_inc(a_exp, 1)

            def turned(i, k):
                eng.wait_ge(a_t, given(a_t) + NS * i + k + 1)
                eng.wait_ge(a_pv, given(a_pv) + NS * i + k - 1)
                eng.activation(PT[:, k % 2, :, :], ps[:, TB[k % 2], 0:2 * P], ACT.Copy).then_inc(a_te, 1)

            def qk_out(i, u):
                eng.wait_ge(a_qk, given(a_qk) + i + 1)
                eng.wait_ge(a_qbd, given(a_qbd) + 4 * (i - 1))
                for m in range(2):
                    eng.activation(Qs[:, u, m, :], ps[:, FA, m * P:(m + 1) * P], ACT.Identity,
                                   bias=bqs[:, m:m + 1], scale=SCALE).then_inc(a_qke, 1)
                eng.wait_ge(a_s, given(a_s) + NS * (i - 1))
                for m in range(2):
                    eng.activation(KT[:, u, m, :], ps[:, FA, (2 + m) * P:(3 + m) * P], ACT.Identity,
                                   bias=bqk[:, 2 + m:3 + m]).then_inc(a_qke, 1)

            def ot_out(t, u):
                eng.wait_ge(a_t2, given(a_t2) + t + 1)
                eng.wait_ge(a_wo, given(a_wo) + t - 1)
                eng.activation(OnT[:, u, :, :], ps[:, FB, 0:DIM], ACT.Copy).then_inc(a_t2e, 1)

            def body(i, u, front, mid, tail, late, ld):
                v = 1 - u
                if tail:
                    turned(i - 1, 2)
                if late and proj:
                    ot_out(i - 2, u)
                if mid:
                    exps(i, u, 0)
                if tail:
                    turned(i - 1, 3)
                if front:
                    if not known(i, 1):
                        eng.wait_ge(a_v, given(a_v) + i)
                    ln_act(eng, L, i + 1, v, FA)
                if mid:
                    exps(i, u, 1)
                    turned(i, 0)
                if front:
                    qk_out(i + 1, v)
                if mid:
                    exps(i, u, 2)
                    turned(i, 1)
                    exps(i, u, 3)

            long_pipeline(eng, body)

        @block.gpsimd
        def _(eng):
            g["give"](eng, "gpsimd")
            def spread(i, u):
                eng.wait_ge(a_qke, given(a_qke) + 4 * i + 2)
                eng.wait_ge(a_s, given(a_s) + NS * (i - 1))
                for half in range(HALF):
                    for b in range(2):
                        eng.tensor_tensor(
                            Qbd[:, u, half, b, :].rearrange("p (j q) -> p j q", q=SEQ),
                            Qs[:, u, half, b * SEQ:(b + 1) * SEQ].unsqueeze(1).to_broadcast([P, 8, SEQ]),
                            headmask[:, :].unsqueeze(2).to_broadcast([P, 8, SEQ]),
                            ALU.mult).then_inc(a_qbd, 1)

            def body(i, u, front, mid, tail, late, ld):
                v = 1 - u
                if front:
                    ln_pool(eng, L, i + 1, v)
                if tail and proj:
                    eng.wait_ge(a_wo, given(a_wo) + i - 2)
                    eng.wait_ge(s_xdone, given(s_xdone) + base + i - 2)
                    eng.tensor_tensor(xb[:, v, :], X[:, i - 1, :], bproj[:, :], ALU.add).then_inc(a_xb, 1)
                if front:
                    spread(i + 1, v)

            long_pipeline(eng, body)


def quantised_ffn(nc, ctx, env):
    g = env
    sb, sem, ps, X = g["sb"], g["sem"], g["ps"], g["X"]
    ln_dve, ln_dve2, ln_pool = g["ln_dve"], g["ln_dve2"], g["ln_pool"]
    ln_h, ln_T, s_xdone, h, identb = g["ln_h"], g["ln_T"], g["s_xdone"], g["h"], g["identb"]
    wg, wu, wd = g["wq3"]
    wsc = g["wsc"]
    L = 2
    base = NPAIR * L
    am = sb("am3", [P, 2, 1]); ac = sb("ac3", [P, 2, 1]); sc = sb("sc3", [P, 2, 1]); dq = sb("dq3", [P, 2, 3])
    am2 = sb("am32", [P, 2, 1]); ac2 = sb("ac32", [P, 2, 1]); sc2 = sb("sc32", [P, 2, 1]); dq2 = sb("dq32", [P, 2, 1])
    r = sb("r3", [P, 2, DIM]); xq = sb("xq3", [P, 2, DIM], BF16); xqT = sb("xqT3", [P, 2, HALF, P], BF16)
    sg = sb("sg3", [P, 2, INNER]); a = sb("a3", [P, 2, INNER]); ar = sb("ar3", [P, 2, INNER])
    aq = sb("aq3", [P, 2, INNER], BF16); aqT = sb("aqT3", [P, 2, 8, P], BF16)
    rnd = sb("rnd3", [P, 2])
    GB, UB = [0, 2], [1, 3]
    XT, AT, OB = 4, 5, 6
    n = "f_"
    f_am = sem(n + "am"); f_ac = sem(n + "ac"); f_sc = sem(n + "sc"); f_dq = sem(n + "dq", 5, "vector")
    f_r = sem(n + "r"); f_xq = sem(n + "xq"); f_xt = sem(n + "xt", 2, "tensor"); f_xte = sem(n + "xte")
    f_g = sem(n + "g", 3, "tensor"); f_u = sem(n + "u"); f_sg = sem(n + "sg", 3, "scalar"); f_a = sem(n + "a", 3, "vector")
    f_am2 = sem(n + "am2"); f_ac2 = sem(n + "ac2"); f_sc2 = sem(n + "sc2"); f_dq2 = sem(n + "dq2")
    f_ar = sem(n + "ar", 3, "scalar"); f_aq = sem(n + "aq", 3, "scalar"); f_at = sem(n + "at", 3, "tensor")
    f_ate = sem(n + "ate", 2, "scalar"); f_o = sem(n + "o", 3, "tensor"); f_rnd = sem(n + "rnd")

    with nc.Block() as block:
        @block.tensor
        def _(eng):
            g["give"](eng, "tensor")

            def xt(i, u):
                eng.wait_ge(f_xq, i + 1)
                if not known(i, 1):
                    eng.wait_ge(f_xte, i)
                out = ps[:, XT, :].bitcast(BF16)
                for c in range(HALF):
                    ins = eng.transpose(out[:, c * P:(c + 1) * P], xq[:, u, c * P:(c + 1) * P], identb[:, :])
                ins.then_inc(f_xt, 1)

            def gu(i, u):
                eng.wait_ge(f_xte, i + 1)
                for q in range(2):
                    eng.wait_ge(f_sg, given(f_sg) + 2 * (i - 1) + q + 1)
                    for c in range(HALF):
                        ins = eng.matmul(ps[:, GB[q], :], xqT[:, u, c, :], wg[:, c, q * 512:(q + 1) * 512],
                                         start=(c == 0), stop=(c == 1))
                    ins.then_inc(f_g, 1)
                    eng.wait_ge(f_a, given(f_a) + 2 * (i - 1) + q + 1)
                    for c in range(HALF):
                        ins = eng.matmul(ps[:, UB[q], :], xqT[:, u, c, :], wu[:, c, q * 512:(q + 1) * 512],
                                         start=(c == 0), stop=(c == 1))
                    ins.then_inc(f_u, 1)

            def at(t, u):
                eng.wait_ge(f_aq, given(f_aq) + t + 1)
                eng.wait_ge(f_ate, given(f_ate) + t)
                out = ps[:, AT, :].bitcast(BF16)
                for c in range(8):
                    ins = eng.transpose(out[:, c * P:(c + 1) * P], aq[:, u, c * P:(c + 1) * P], identb[:, :])
                ins.then_inc(f_at, 1)

            def down(t, u):
                eng.wait_ge(f_ate, given(f_ate) + t + 1)
                eng.wait_ge(s_xdone, given(s_xdone) + base + t)
                for c in range(8):
                    ins = eng.matmul(ps[:, OB, 0:DIM], aqT[:, u, c, :], wd[:, c, :], start=(c == 0), stop=(c == 7))
                ins.then_inc(f_o, 1)

            def body(i, u, front, mid, tail, ld):
                v = 1 - u
                if mid:
                    gu(i, u)
                if front:
                    xt(i + 1, v)
                if tail:
                    at(i - 1, v)
                    down(i - 1, v)

            pipeline(eng, body)

        @block.vector
        def _(eng):
            g["give"](eng, "vector")
            eng.memset(rnd[:, 0:1], ROUND).then_inc(f_rnd, 1)
            eng.memset(rnd[:, 1:2], -ROUND).then_inc(f_rnd, 1)

            def front1(i, u):
                eng.wait_ge(ln_h, base + i + 1)
                eng.tensor_reduce(am[:, u, :], h[:, u, :], AX.X, ALU.max,
                                  apply_absolute_value=True).then_inc(f_am, 1)
                eng.wait_ge(f_am, i + 1)
                eng.tensor_scalar(ac[:, u, :], am[:, u, :], 1e-5, None, ALU.max).then_inc(f_ac, 1)
                eng.wait_ge(f_ac, 2 * i + 1)
                eng.reciprocal(sc[:, u, :], ac[:, u, :]).then_inc(f_ac, 1)
                eng.wait_ge(f_ac, 2 * i + 2)
                eng.tensor_scalar(sc[:, u, :], sc[:, u, :], 127.0, None, ALU.mult).then_inc(f_sc, 1)
                eng.wait_ge(f_sg, given(f_sg) + 2 * (i - 1))
                eng.tensor_scalar(dq[:, u, :], wsc[:, :], ac[:, u, :], 1.0 / 127.0, ALU.mult,
                                  ALU.mult).then_inc(f_dq, 1)
                eng.wait_ge(f_sc, i + 1)
                eng.tensor_scalar(r[:, u, :], h[:, u, :], sc[:, u, :], ROUND, ALU.mult, ALU.add).then_inc(f_r, 1)
                eng.wait_ge(f_r, i + 1)
                eng.wait_ge(f_xt, given(f_xt) + i - 1)
                eng.tensor_scalar(xq[:, u, :], r[:, u, :], ROUND, None, ALU.subtract).then_inc(f_xq, 1)

            def mul(i, u, q):
                eng.wait_ge(f_sg, given(f_sg) + 2 * i + q + 1)
                eng.wait_ge(f_u, 2 * i + q + 1)
                eng.wait_ge(f_dq, given(f_dq) + i + 1)
                eng.wait_ge(f_ar, given(f_ar) + i - 1)
                eng.scalar_tensor_tensor(out=a[:, u, q * 512:(q + 1) * 512], in0=ps[:, UB[q], :],
                                         scalar=dq[:, u, 1:2], in1=sg[:, u, q * 512:(q + 1) * 512],
                                         op0=ALU.mult, op1=ALU.mult).then_inc(f_a, 1)

            def amax2(i, u):
                eng.wait_ge(f_a, given(f_a) + 2 * i + 2)
                eng.tensor_reduce(am2[:, u, :], a[:, u, :], AX.X, ALU.max,
                                  apply_absolute_value=True).then_inc(f_am2, 1)
                eng.wait_ge(f_am2, i + 1)
                eng.tensor_scalar(ac2[:, u, :], am2[:, u, :], 1e-5, None, ALU.max).then_inc(f_ac2, 1)
                eng.wait_ge(f_ac2, 2 * i + 1)
                eng.reciprocal(sc2[:, u, :], ac2[:, u, :]).then_inc(f_ac2, 1)
                eng.wait_ge(f_ac2, 2 * i + 2)
                eng.tensor_scalar(sc2[:, u, :], sc2[:, u, :], 127.0, None, ALU.mult).then_inc(f_sc2, 1)
                eng.tensor_scalar(dq2[:, u, :], wsc[:, 2:3], ac2[:, u, :], 1.0 / 127.0, ALU.mult,
                                  ALU.mult).then_inc(f_dq2, 1)

            def add_x(t, u):
                eng.wait_ge(f_o, given(f_o) + t + 1)
                eng.wait_ge(f_dq2, t + 1)
                eng.scalar_tensor_tensor(out=X[:, t, :], in0=ps[:, OB, 0:DIM], scalar=dq2[:, u, :],
                                         in1=X[:, t, :], op0=ALU.mult, op1=ALU.add).then_inc(s_xdone, 1)

            def body(i, u, front, mid, tail, late, ld):
                v = 1 - u
                if front:
                    ln_dve(eng, L, i + 1, v)
                if late:
                    add_x(i - 2, u)
                if front:
                    ln_dve2(eng, L, i + 1, v, f_r, 0)
                    front1(i + 1, v)
                if mid:
                    mul(i, u, 0)
                    mul(i, u, 1)
                if mid:
                    amax2(i, u)

            long_pipeline(eng, body)

        @block.scalar
        def _(eng):
            g["give"](eng, "scalar")
            eng.wait_ge(f_rnd, 2)

            def silu(i, u, q):
                eng.wait_ge(f_g, given(f_g) + 2 * i + q + 1)
                eng.wait_ge(f_dq, given(f_dq) + i + 1)
                eng.wait_ge(f_a, given(f_a) + 2 * (i - 1))
                eng.activation(sg[:, u, q * 512:(q + 1) * 512], ps[:, GB[q], :], ACT.Silu,
                               scale=dq[:, u, 0:1]).then_inc(f_sg, 1)

            def round2(i, u):
                eng.wait_ge(f_sc2, i + 1)
                eng.wait_ge(f_aq, given(f_aq) + i - 1)
                eng.activation(ar[:, u, :], a[:, u, :], ACT.Identity, bias=rnd[:, 0:1],
                               scale=sc2[:, u, :]).then_inc(f_ar, 1)
                eng.wait_ge(f_ar, given(f_ar) + i + 1)
                eng.wait_ge(f_at, given(f_at) + i - 1)
                eng.activation(aq[:, u, :], ar[:, u, :], ACT.Identity, bias=rnd[:, 1:2]).then_inc(f_aq, 1)

            def xt_out(i, u):
                eng.wait_ge(f_xt, given(f_xt) + i + 1)
                eng.wait_ge(f_g, given(f_g) + 2 * (i - 1))
                if not known(i, 2):
                    eng.wait_ge(f_u, 2 * (i - 1))
                eng.activation(xqT[:, u, :, :], ps[:, XT, :].bitcast(BF16)[:, 0:DIM], ACT.Copy).then_inc(f_xte, 1)

            def at_out(t, u):
                eng.wait_ge(f_at, given(f_at) + t + 1)
                eng.wait_ge(f_o, given(f_o) + t - 1)
                eng.activation(aqT[:, u, :, :], ps[:, AT, :].bitcast(BF16), ACT.Copy).then_inc(f_ate, 1)

            def body(i, u, front, mid, tail, ld):
                v = 1 - u
                if mid:
                    silu(i, u, 0)
                    silu(i, u, 1)
                if front:
                    xt_out(i + 1, v)
                if tail:
                    at_out(i - 1, v)
                if mid:
                    round2(i, u)

            pipeline(eng, body)

        @block.gpsimd
        def _(eng):
            g["give"](eng, "gpsimd")
            def body(i, u, front, mid, tail, ld):
                v = 1 - u
                if front:
                    ln_pool(eng, L, i + 1, v)

            pipeline(eng, body)


def cross_single(nc, ctx, env):
    g = env
    sb, sem, ps, X, io = g["sb"], g["sem"], g["ps"], g["X"], g["io"]
    ident, hT = g["ident"], g["hT"]
    ln_dve, ln_dve2, ln_pool, ln_pe, ln_act = (g[k] for k in ("ln_dve", "ln_dve2", "ln_pool", "ln_pe", "ln_act"))
    ln_hT, s_xdone = g["ln_hT"], g["s_xdone"]
    wq, wk, wv, bqk, bv = g["wq4"], g["wk4"], g["wv4"], g["bqk4"], g["bv"][4]
    cx = sb("cx", [P, 2, 2 * CTX])
    cxh = sb("cxh", [P, 2, 2 * CTX], F32R); cxl = sb("cxl", [P, 2, 2 * CTX], F32R)
    wh = {n: sb(f"w{n}4h", [P, DIM], F32R) for n in "kv"}; wl = {n: sb(f"w{n}4l", [P, DIM], F32R) for n in "kv"}
    QT = sb("QT4", [P, 2, HALF, P])
    KT = sb("KT4", [P, 2, HALF, 2 * CTX])
    V = sb("V4", [P, 2, 4, DIM])
    Pr = sb("Pr4", [P, 2, CTX]); PT = sb("PT4", [P, 2, 2, P])
    mx = sb("mx4", [P, 2, 1]); den = sb("den4", [P, 2, 1]); rd = sb("rd4", [P, 2, 1])
    L = 3
    base = NPAIR * L
    SB, TB, LQ, OB = [0, 1], 2, 3, [4, 5]
    FA, FB = 6, 7
    n = "d_"
    d_ld = [sem(n + "ld0"), sem(n + "ld1")]
    d_q = sem(n + "q"); d_qe = sem(n + "qe", 3, "scalar"); d_k = sem(n + "k", 3, "tensor"); d_ke = sem(n + "ke", 3, "scalar")
    d_v = sem(n + "v", 3, "tensor"); d_ve = sem(n + "ve", 2, "vector"); d_s = sem(n + "s", 2, "tensor")
    d_max = sem(n + "max"); d_exp = sem(n + "exp", 2, "scalar"); d_t = sem(n + "t", 2, "tensor")
    d_w = sem(n + "w"); d_cxh = sem(n + "cxh"); d_cxl = sem(n + "cxl", 2, "gpsimd")
    d_te = sem(n + "te", 2, "scalar"); d_o = sem(n + "o", 2, "tensor"); d_rd = sem(n + "rd", 2, "vector")

    with nc.Block() as block:
        @block.sync
        def _(sp):
            ctxT = io["ctxT"].rearrange("p (n c) -> p n c", c=2 * CTX)

            def load(i, u):
                sp.wait_ge(d_cxl, given(d_cxl) + i - 1)
                sp.dma_start(cx[:, u, :], ctxT[:, i, :]).then_inc(d_ld[u], 16)

            with sp.Fori(0, NPAIR // 2) as j:
                load(2 * j, 0)
                load(2 * j + 1, 1)

        @block.tensor
        def _(eng):
            g["give"](eng, "tensor")
            def qproj(i, u):
                eng.wait_ge(ln_hT, g["lnt"][L] + i + 1)
                for m in range(HALF):
                    for c in range(2):
                        ins = eng.matmul(ps[:, LQ, m * P:(m + 1) * P], wq[:, c, m * P:(m + 1) * P],
                                         hT[:, u, c, :], start=(c == 0), stop=(c == 1))
                ins.then_inc(d_q, 1)

            def kproj(i, u, m, ld):
                if m == 0:
                    eng.wait_ge(d_ve, given(d_ve) + 2 * i - 1)
                    eng.wait_ge(d_cxl, given(d_cxl) + i + 1)
                    if known(i, 1):
                        eng.wait_ge(d_w, 4)
                else:
                    eng.wait_ge(d_ve, given(d_ve) + 2 * i)
                out, w = ps[:, (FA, FB)[m], :], slice(m * P, (m + 1) * P)
                eng.matmul(out, wh["k"][:, w], cxh[:, u, :], start=True, stop=False)
                eng.matmul(out, wh["k"][:, w], cxl[:, u, :], start=False, stop=False)
                eng.matmul(out, wl["k"][:, w], cxh[:, u, :], start=False, stop=True).then_inc(d_k, 1)

            def vproj(i, u, m):
                eng.wait_ge(d_ke, given(d_ke) + 2 * i + m + 1)
                for t in range(2):
                    out = ps[:, (FA, FB)[m], t * DIM:(t + 1) * DIM]
                    c = slice((2 * m + t) * P, (2 * m + t + 1) * P)
                    eng.matmul(out, cxh[:, u, c], wh["v"][:, :], start=True, stop=False)
                    eng.matmul(out, cxl[:, u, c], wh["v"][:, :], start=False, stop=False)
                    ins = eng.matmul(out, cxh[:, u, c], wl["v"][:, :], start=False, stop=True)
                ins.then_inc(d_v, 1)

            def scores(i, u):
                eng.wait_ge(d_qe, given(d_qe) + 2 * i + 2)
                eng.wait_ge(d_ke, given(d_ke) + 2 * i + 2)
                eng.wait_ge(d_exp, given(d_exp) + i - 1)
                for b in range(2):
                    for c in range(HALF):
                        ins = eng.matmul(ps[64 * b:64 * b + 64, SB[u], 0:CTX], QT[:, u, c, 64 * b:64 * b + 64],
                                         KT[:, u, c, b * CTX:(b + 1) * CTX], start=(c == 0), stop=(c == 1),
                                         tile_position=(0, 64 * b))
                ins.then_inc(d_s, 1)

            def turn(i, u):
                eng.wait_ge(d_exp, given(d_exp) + i + 1)
                eng.wait_ge(d_te, given(d_te) + i)
                for kt in range(2):
                    ins = eng.transpose(ps[:, TB, kt * P:(kt + 1) * P], Pr[:, u, kt * P:(kt + 1) * P],
                                        ident[:, :])
                ins.then_inc(d_t, 1)

            def pv(i, u):
                eng.wait_ge(d_te, given(d_te) + i + 1)
                eng.wait_ge(d_ve, given(d_ve) + 2 * i + 2)
                eng.wait_ge(s_xdone, given(s_xdone) + base + i - 1)
                for b in range(2):
                    for kt in range(2):
                        ins = eng.matmul(ps[64 * b:64 * b + 64, OB[u], 0:DIM], PT[:, u, kt, 64 * b:64 * b + 64],
                                         V[:, u, 2 * b + kt, :], start=(kt == 0), stop=(kt == 1),
                                         tile_position=(0, 64 * b))
                ins.then_inc(d_o, 1)

            def body(i, u, front, mid, tail, ld):
                v = 1 - u
                if mid:
                    scores(i, u)
                if front:
                    kproj(i + 1, v, 0, ld)
                    kproj(i + 1, v, 1, ld)
                    eng.wait_ge(d_qe, given(d_qe) + 2 * i + 2)
                    ln_pe(eng, L, i + 1, v, LQ)
                if mid:
                    turn(i, u)
                if front:
                    vproj(i + 1, v, 0)
                    qproj(i + 1, v)
                if mid:
                    pv(i, u)
                if front:
                    vproj(i + 1, v, 1)

            pipeline(eng, body)

        @block.vector
        def _(eng):
            g["give"](eng, "vector")
            def rowmax(i, u):
                eng.wait_ge(d_s, given(d_s) + i + 1)
                eng.wait_ge(d_exp, given(d_exp) + i - 1)
                eng.tensor_reduce(mx[:, u, :], ps[:, SB[u], 0:CTX], AX.X, ALU.max, negate=True).then_inc(d_max, 1)

            def v_out(i, u, m):
                eng.wait_ge(d_v, given(d_v) + 2 * i + m + 1)
                eng.wait_ge(d_o, given(d_o) + i - 1)
                eng.tensor_tensor(V[:, u, 2 * m:2 * m + 2, :], ps[:, (FA, FB)[m], :].rearrange("p (t n) -> p t n", t=2),
                                  bv[:, :].unsqueeze(1).to_broadcast([P, 2, DIM]), ALU.add).then_inc(d_ve, 1)

            def add_x(i, u):
                eng.wait_ge(d_exp, given(d_exp) + i + 1)
                eng.reciprocal(rd[:, u, :], den[:, u, :]).then_inc(d_rd, 1)
                eng.wait_ge(d_rd, given(d_rd) + i + 1)
                eng.wait_ge(d_o, given(d_o) + i + 1)
                eng.scalar_tensor_tensor(out=X[:, i, :], in0=ps[:, OB[u], 0:DIM], scalar=rd[:, u, :],
                                         in1=X[:, i, :], op0=ALU.mult, op1=ALU.add).then_inc(s_xdone, 1)

            def body(i, u, front, mid, tail, ld):
                v = 1 - u
                if front:
                    ln_dve(eng, L, i + 1, v)
                if mid:
                    rowmax(i, u)
                if front:
                    ln_dve2(eng, L, i + 1, v)
                    v_out(i + 1, v, 0)
                if mid:
                    add_x(i, u)
                if front:
                    v_out(i + 1, v, 1)

            pipeline(eng, body)

        @block.scalar
        def _(eng):
            g["give"](eng, "scalar")
            def q_out(i, u):
                eng.wait_ge(d_q, i + 1)
                eng.wait_ge(d_s, given(d_s) + i - 1)
                for m in range(HALF):
                    eng.activation(QT[:, u, m, :], ps[:, LQ, m * P:(m + 1) * P], ACT.Identity,
                                   bias=bqk[:, m:m + 1]).then_inc(d_qe, 1)

            def k_out(i, u, m):
                eng.wait_ge(d_k, given(d_k) + 2 * i + m + 1)
                eng.activation(KT[:, u, m, :], ps[:, (FA, FB)[m], :], ACT.Identity,
                               bias=bqk[:, 2 + m:3 + m]).then_inc(d_ke, 1)

            def cx_high(i, u, ld):
                eng.wait_ge(d_ld[u], 16 * ld)
                eng.wait_ge(d_v, given(d_v) + 2 * i - 2)
                eng.activation(cxh[:, u, :], cx[:, u, :], ACT.Copy).then_inc(d_cxh, 1)

            def exps(i, u):
                eng.wait_ge(d_max, i + 1)
                eng.wait_ge(d_t, given(d_t) + i - 1)
                eng.wait_ge(d_rd, given(d_rd) + i - 1)
                eng.activation(Pr[:, u, :], ps[:, SB[u], 0:CTX], ACT.Exp, bias=mx[:, u, :],
                               accum_out=den[:, u, :]).then_inc(d_exp, 1)

            def turned(i, u):
                eng.wait_ge(d_t, given(d_t) + i + 1)
                eng.wait_ge(d_o, given(d_o) + i - 1)
                eng.activation(PT[:, u, :, :], ps[:, TB, 0:DIM], ACT.Copy).then_inc(d_te, 1)

            def body(i, u, front, mid, tail, ld):
                v = 1 - u
                if front:
                    cx_high(i + 1, v, ld)
                if mid:
                    exps(i, u)
                if front:
                    k_out(i + 1, v, 0)
                    k_out(i + 1, v, 1)
                    if not known(i, 1):
                        eng.wait_ge(d_q, i)
                    ln_act(eng, L, i + 1, v, LQ)
                if mid:
                    turned(i, u)
                if front:
                    q_out(i + 1, v)

            for n, w in (("k", wk), ("v", wv)):
                eng.activation(wh[n][:, :], w[:, :], ACT.Copy).then_inc(d_w, 1)
            pipeline(eng, body)

        @block.gpsimd
        def _(eng):
            g["give"](eng, "gpsimd")
            eng.wait_ge(d_w, 2)
            for n, w in (("k", wk), ("v", wv)):
                eng.tensor_tensor(wl[n][:, :], w[:, :], wh[n][:, :].bitcast(F32), ALU.subtract).then_inc(d_w, 1)

            def cx_low(i, u):
                eng.wait_ge(d_cxh, i + 1)
                eng.wait_ge(d_v, given(d_v) + 2 * i - 2)
                eng.tensor_tensor(cxl[:, u, :], cx[:, u, :], cxh[:, u, :].bitcast(F32), ALU.subtract).then_inc(d_cxl, 1)

            def body(i, u, front, mid, tail, ld):
                if front:
                    cx_low(i + 1, 1 - u)
                    ln_pool(eng, L, i + 1, 1 - u)

            pipeline(eng, body)


def router(nc, ctx, env):
    g = env
    sb, sem, ps, X, io = g["sb"], g["sem"], g["ps"], g["X"], g["io"]
    ident, epsc, mhalf = g["ident"], g["epsc"], g["mhalf"]
    wr, br = g["wr6"], g["br6"]
    g["Hh"] = Hh = sb("Hh", [P, HALF, NPAIR, P], F32R)
    g["Hl"] = Hl = sb("Hl", [P, HALF, NPAIR, P], F32R)
    g["raw6"] = raw = sb("raw6", [P, 2, 768])
    NG, GE, TOPG = 4, EXPERTS // 4, 2
    QUAD, TWO = 4, 2
    stat = sb("stat6", [P, NPAIR, 6]); mv = sb("mv6", [P, NPAIR, 2])
    var = sb("var6", [P, NPAIR]); rs = sb("rs6", [P, NPAIR])
    hn = sb("hn6", [P, NPAIR, DIM]); hT = sb("hT6", [P, HALF, NPAIR, P])
    W = sb("W6", [P, NPAIR, NE])
    score = sb("score6", [P, NPAIR, EXPERTS])
    choice = sb("choice6", [P, NPAIR, EXPERTS])
    gm = sb("gm6", [P, NPAIR, NG, 8])
    gs = sb("gs6", [P, NPAIR, 10])
    g8 = sb("g86", [P, NPAIR, 8]); gr = sb("gr6", [P, NPAIR, 10]); gsel = sb("gsel6", [P, NPAIR, NG])
    msk = sb("msk6", [P, NPAIR, EXPERTS]); m8 = sb("m86", [P, NPAIR, 8]); mr = sb("mr6", [P, NPAIR, EXPERTS])
    tot = sb("tot6", [P, NPAIR, 1])
    g["WT6"] = WT = sb("WT6", [NE, TOK])
    TRB, LB = [0, 1, 2, 3], 4
    n = "r_"
    ln_st, ln_mv, ln_eps, ln_rs, ln_h = (g[k] for k in ("ln_st", "ln_mv", "ln_eps", "ln_rs", "ln_h"))
    before = 5 * NPAIR
    r_T = sem(n + "T"); r_ht = sem(n + "ht", 5, "scalar")
    r_l = sem(n + "l"); r_sc = sem(n + "sc")
    r_c = sem(n + "c"); r_w = sem(n + "w"); r_t = sem(n + "t"); r_wt = sem(n + "wt")
    g["m_ld"] = m_ld = [sem("m_ld0"), sem("m_ld1")]
    steps = NPAIR // TWO

    def two(j, b):
        return bass.ds(len(TRB) * TWO * j + TWO * b, TWO)

    def bank(b):
        return ps[:, TRB[b], :].rearrange("p (n c t) -> p c n t", n=TWO, c=HALF)

    with nc.Block() as block:
        @block.sync
        def _(sp):
            for e in range(2):
                sp.dma_start(raw[:, e, :], io["ew6"][e, :, :]).then_inc(m_ld[e], 16)

        @block.tensor
        def _(eng):
            g["give"](eng, "tensor")
            def logits(k):
                eng.wait_ge(r_ht, given(r_ht) + k + 1)
                for t in range(TWO * k, TWO * (k + 1)):
                    for c in range(HALF):
                        ins = eng.matmul(ps[:, LB, t * EXPERTS:(t + 1) * EXPERTS], hT[:, c, t, :], wr[:, c, :],
                                         start=(c == 0), stop=(c == 1))
                ins.then_inc(r_l, 1)

            for k in range(steps):
                b = k % len(TRB)
                eng.wait_ge(ln_h, before + TWO * k + TWO)
                eng.wait_ge(r_ht, given(r_ht) + k - 3)
                for q in range(TWO):
                    for c in range(HALF):
                        at = (q * HALF + c) * P
                        ins = eng.transpose(ps[:, TRB[b], at:at + P],
                                            hn[:, TWO * k + q, c * P:(c + 1) * P], ident[:, :])
                ins.then_inc(r_T, 1)
                if k:
                    logits(k - 1)
            logits(steps - 1)
            for t in range(NPAIR):
                if t == 0:
                    eng.wait_ge(r_w, 1)
                    eng.wait_ge(r_sc, 1)
                ins = eng.transpose(ps[0:NE, 4 + t // 4, (t % 4) * P:(t % 4 + 1) * P], W[:, t, :], ident[:, :])
            ins.then_inc(r_t, 1)

        @block.scalar
        def _(eng):
            g["give"](eng, "scalar")
            with eng.Fori(0, steps // len(TRB)) as j:
                for b in range(len(TRB)):
                    eng.wait_ge(r_T, len(TRB) * j + b + 1)
                    eng.activation(Hh[:, :, two(j, b), :], bank(b), ACT.Copy)
                    eng.activation(hT[:, :, two(j, b), :], bank(b), ACT.Copy).then_inc(r_ht, 1)
            eng.wait_ge(r_l, steps)
            eng.activation(score[:, :, :].rearrange("p t e -> p (t e)"), ps[:, LB, :], ACT.Sigmoid).then_inc(r_sc, 1)
            eng.wait_ge(r_t, 1)
            eng.activation(WT[:, :].rearrange("e (b n) -> e b n", b=4), ps[0:NE, 4:8, :], ACT.Copy).then_inc(r_wt, 1)

        @block.gpsimd
        def _(eng):
            g["give"](eng, "gpsimd")
            for j in range(NPAIR // QUAD):
                at = slice(QUAD * j, QUAD * (j + 1))
                eng.wait_ge(ln_mv, before + QUAD * (j + 1))
                eng.tensor_tensor(var[:, at], mv[:, at, 1], epsc[:, :].to_broadcast([P, QUAD]), ALU.add).then_inc(ln_eps, 1)
                eng.wait_ge(ln_eps, before + j + 1)
                eng.tensor_tensor(rs[:, at], var[:, at], mhalf[:, :].to_broadcast([P, QUAD]), ALU.pow).then_inc(ln_rs, 1)

        @block.vector
        def _(eng):
            g["give"](eng, "vector")
            eng.memset(gs[:, :, :], NEG).then_inc(r_c, 1)
            eng.memset(W[:, :, 0:NE - EXPERTS], 1.0).then_inc(r_c, 1)
            eng.wait_ge(g["s_xdone"], given(g["s_xdone"]) + 5 * NPAIR)
            for j in range(NPAIR // QUAD):
                for t in range(QUAD * j, QUAD * (j + 1)):
                    eng.bn_stats(stat[:, t, :], X[:, t, :]).then_inc(ln_st, 1)
                eng.wait_ge(ln_st, before + QUAD * (j + 1))
                for t in range(QUAD * j, QUAD * (j + 1)):
                    eng.bn_aggr(mv[:, t, :], stat[:, t, :]).then_inc(ln_mv, 1)
            with eng.Fori(0, NPAIR // QUAD) as j:
                eng.wait_ge(ln_rs, before + j + 1)
                eng.nop(nofuse=True)
                for q in range(QUAD):
                    t = QUAD * j + q
                    eng.tensor_scalar(hn[:, t, :], X[:, t, :], mv[:, t, 0:1], rs[:, bass.ds(t, 1)],
                                      ALU.subtract, ALU.mult).then_inc(ln_h, 1)
            with eng.Fori(0, steps // len(TRB)) as j:
                for b in range(len(TRB)):
                    eng.wait_ge(r_ht, given(r_ht) + len(TRB) * j + b + 1)
                    eng.tensor_tensor(Hl[:, :, two(j, b), :], hT[:, :, two(j, b), :],
                                      Hh[:, :, two(j, b), :].bitcast(F32), ALU.subtract)
            done = [2]

            def step(ins, k=1):
                ins.then_inc(r_c, 1)
                done[0] += k
                eng.wait_ge(r_c, done[0])

            eng.wait_ge(r_sc, 1)
            step(eng.tensor_tensor(choice[:, :, :], score[:, :, :],
                                   br[:, :].unsqueeze(1).to_broadcast([P, NPAIR, EXPERTS]), ALU.add))
            for t in range(NPAIR):
                for q in range(NG):
                    ins = eng.max(gm[:, t, q, :], choice[:, t, q * GE:(q + 1) * GE])
            step(ins)
            step(eng.tensor_tensor(gs[:, :, 0:NG], gm[:, :, :, 0], gm[:, :, :, 1], ALU.add))
            for t in range(NPAIR):
                ins = eng.max(g8[:, t, :], gs[:, t, :])
            step(ins)
            step(eng.memset(g8[:, :, TOPG:8], NEG))
            for t in range(NPAIR):
                ins = eng.match_replace(gr[:, t, :], g8[:, t, :], gs[:, t, :], -NEG)
            step(ins)
            step(eng.tensor_tensor(gsel[:, :, :], gr[:, :, 0:NG], gs[:, :, 0:NG], ALU.not_equal))
            step(eng.tensor_tensor(msk[:, :, :].rearrange("p t (a b) -> p (t a) b", b=GE),
                                   choice[:, :, :].rearrange("p t (a b) -> p (t a) b", b=GE),
                                   gsel[:, :, :].rearrange("p t a -> p (t a)").unsqueeze(2)
                                   .to_broadcast([P, NPAIR * NG, GE]), ALU.mult))
            for t in range(NPAIR):
                ins = eng.max(m8[:, t, :], msk[:, t, :])
            step(ins)
            for t in range(NPAIR):
                ins = eng.match_replace(mr[:, t, :], m8[:, t, :], msk[:, t, :], NEG)
            step(ins)
            step(eng.tensor_tensor(mr[:, :, :], mr[:, :, :], msk[:, :, :], ALU.not_equal))
            step(eng.tensor_tensor(msk[:, :, :], mr[:, :, :], score[:, :, :], ALU.mult))
            step(eng.tensor_reduce(tot[:, :, :], msk[:, :, :], AX.X, ALU.add))
            step(eng.tensor_scalar(tot[:, :, :], tot[:, :, :], 1e-20, None, ALU.add))
            step(eng.reciprocal(tot[:, :, :], tot[:, :, :]))
            step(eng.tensor_scalar(tot[:, :, :], tot[:, :, :], 2.5, None, ALU.mult))
            eng.tensor_tensor(W[:, :, NE - EXPERTS:NE], msk[:, :, :],
                              tot[:, :, :].to_broadcast([P, NPAIR, EXPERTS]), ALU.mult).then_inc(r_w, 1)


def experts(nc, ctx, env):
    g = env
    sb, sem, ps, X, io, out = g["sb"], g["sem"], g["ps"], g["X"], g["io"], g["out"]
    ident, Hh, Hl, dram = g["ident"], g["Hh"], g["Hl"], g["wdram"]
    SG = 2
    UT = 512
    raw, WT = g["raw6"], g["WT6"]
    wh = sb("wh6", [P, 2, 768], F32R); wl = sb("wl6", [P, 2, 768], F32R)
    wb = sb("wb6", [P, 2, 2 * UT])
    sg = sb("sg6", [P, 2, UT]); sw = sb("sw6", [P, 2, UT]); a = sb("a6", [P, 2, UT])
    ah = sb("ah6", [P, 2, UT], F32R); al = sb("al6", [P, 2, UT], F32R)
    OT = sb("OT6", [P, 4, UT])
    GB, UB, OB = [0, 1], [2, 3], [[4, 5], [6, 7]]
    GU, DN = slice(0, 512), slice(512, 768)
    n = "m_"
    r_dram = sem("r_dram"); m_one = sem(n + "one")
    m_ld = g["m_ld"]; m_wb = [sem(n + "wb0"), sem(n + "wb1")]
    m_hg = sem(n + "hg"); m_lg = sem(n + "lg", 2, "vector"); m_hd = sem(n + "hd"); m_ld_ = sem(n + "lowd", 2, "vector")
    m_g = sem(n + "g", 5, "tensor"); m_u = sem(n + "u", 5, "tensor"); m_d = sem(n + "d", 5, "tensor")
    m_sg = sem(n + "sg", 3, "scalar"); m_sw = sem(n + "sw", 3, "gpsimd"); m_a = sem(n + "a", 3, "vector")
    m_ah = sem(n + "ah", 3, "scalar"); m_al = sem(n + "al", 3, "vector")
    m_ot = sem(n + "ot"); m_tt = sem(n + "tt"); m_y = sem(n + "y")
    g["m_out"] = m_out = sem(n + "out")
    HhT = Hh[:, :, :, :].rearrange("p c n t -> p c (n t)")
    HlT = Hl[:, :, :, :].rearrange("p c n t -> p c (n t)")

    def each_expert(eng, s, body):
        k, q = NE * s, NE // 2 * s
        body(0, k, 0, q + 1)
        body(1, k + 1, 1, q + 1)
        with eng.Fori(0, NE // 2 - 2) as j:
            body(2 * j + 2, 2 * j + 2 + k, 0, j + 2 + q)
            body(2 * j + 3, 2 * j + 3 + k, 1, j + 2 + q)
        body(NE - 2, NE - 2 + k, 0, NE // 2 + q)
        body(NE - 1, NE - 1 + k, 1, NE // 2 + q)

    with nc.Block() as block:
        @block.sync
        def _(sp):
            sp.dma_start(dram, WT[:, :]).then_inc(r_dram, 16)
            sp.wait_ge(r_dram, 16)
            for s in range(SG):
                def body(e, E, u, ld):
                    if known(E, 2):
                        return
                    sp.wait_ge(m_lg, given(m_lg) + E - 1)
                    sp.wait_ge(m_ld_, given(m_ld_) + E - 1)
                    sp.dma_start(raw[:, u, :], io["ew6"][e, :, :]).then_inc(m_ld[u], 16)
                    sp.wait_ge(m_sw, given(m_sw) + 2 * (E - 1))
                    src = dram[bass.ds(e, 1), 2 * UT * s:2 * UT * (s + 1)]
                    sp.dma_start(wb[:, u, :], src.to_broadcast([P, 2 * UT])).then_inc(m_wb[u], 16)

                each_expert(sp, s, body)
            for s in range(SG):
                sp.wait_ge(m_y, 8 * (s + 1))
                sp.dma_start(out.rearrange("(n p) d -> p n d", p=P)[:, 8 * s:8 * s + 8, :],
                             X[:, 8 * s:8 * s + 8, :]).then_inc(m_out, 16)
            sp.wait_ge(m_out, 16 * SG)

        @block.tensor
        def _(eng):
            g["give"](eng, "tensor")
            for s in range(SG):
                def gate_up(E, u, tt):
                    if tt == 0:
                        eng.wait_ge(m_hg, E + 1)
                        eng.wait_ge(m_lg, given(m_lg) + E + 1)
                    cols = slice(2 * UT * s + UT * tt, 2 * UT * s + UT * (tt + 1))
                    for bank, at, free, done in ((GB[tt], 0, m_sg, m_g), (UB[tt], 256, m_a, m_u)):
                        eng.wait_ge(free, given(free) + 2 * (E - 1) + tt + 1)
                        for c in range(HALF):
                            w = slice(at + c * P, at + (c + 1) * P)
                            eng.matmul(ps[:, bank, :], wh[:, u, w], HhT[:, c, cols], start=(c == 0), stop=False)
                            eng.matmul(ps[:, bank, :], wh[:, u, w], HlT[:, c, cols], start=False, stop=False)
                            ins = eng.matmul(ps[:, bank, :], wl[:, u, w], HhT[:, c, cols], start=False,
                                             stop=(c == 1))
                        ins.then_inc(done, 1)

                def down(E, u, tt, first, last):
                    eng.wait_ge(m_al, given(m_al) + 2 * E + tt + 1)
                    if tt == 0:
                        eng.wait_ge(m_ld_, given(m_ld_) + E + 1)
                    for m in range(2):
                        w = slice(512 + m * P, 512 + (m + 1) * P)
                        bank = ps[:, OB[m][tt], :]
                        eng.matmul(bank, wh[:, u, w], ah[:, tt, :], start=first, stop=False)
                        eng.matmul(bank, wh[:, u, w], al[:, tt, :], start=False, stop=False)
                        ins = eng.matmul(bank, wl[:, u, w], ah[:, tt, :], start=False, stop=last)
                    ins.then_inc(m_d, 1)

                k = NE * s
                if s:
                    eng.wait_ge(m_ot, 4 * s)
                    eng.wait_ge(m_y, 8 * s)
                gate_up(k, 0, 0)
                gate_up(k, 0, 1)
                for tt in range(2):
                    gate_up(k + 1, 1, tt)
                    down(k, 0, tt, True, False)
                with eng.Fori(0, NE // 2 - 1) as j:
                    for tt in range(2):
                        gate_up(2 * j + 2 + k, 0, tt)
                        down(2 * j + 1 + k, 1, tt, False, False)
                    for tt in range(2):
                        gate_up(2 * j + 3 + k, 1, tt)
                        down(2 * j + 2 + k, 0, tt, False, False)
                down(k + NE - 1, 1, 0, False, True)
                down(k + NE - 1, 1, 1, False, True)
                eng.wait_ge(m_ot, 4 * s + 4)
                for q in range(8):
                    if q == 0:
                        eng.wait_ge(m_a, given(m_a) + 2 * NE * (s + 1))
                        eng.wait_ge(m_sg, given(m_sg) + 2 * NE * (s + 1))
                    for m in range(2):
                        ins = eng.transpose(ps[:, q // 2, (q % 2) * DIM + m * P:(q % 2) * DIM + (m + 1) * P],
                                            OT[:, 2 * m + q // 4, (q % 4) * P:(q % 4 + 1) * P], ident[:, :])
                    if q % 2:
                        ins.then_inc(m_tt, 1)

        @block.scalar
        def _(eng):
            g["give"](eng, "scalar")
            for s in range(SG):
                def high_gu(E, u, ld):
                    eng.wait_ge(m_ld[u], 16 * ld)
                    eng.wait_ge(m_u, given(m_u) + 2 * (E - 1))
                    eng.activation(wh[:, u, GU], raw[:, u, GU], ACT.Copy).then_inc(m_hg, 1)

                def high_d(E, u):
                    eng.wait_ge(m_d, given(m_d) + 2 * (E - 1))
                    eng.activation(wh[:, u, DN], raw[:, u, DN], ACT.Copy).then_inc(m_hd, 1)

                def silu(E, tt):
                    eng.wait_ge(m_g, given(m_g) + 2 * E + tt + 1)
                    eng.wait_ge(m_sw, given(m_sw) + 2 * (E - 1) + tt + 1)
                    eng.activation(sg[:, tt, :], ps[:, GB[tt], :], ACT.Silu).then_inc(m_sg, 1)

                def high_a(E, tt):
                    eng.wait_ge(m_a, given(m_a) + 2 * E + tt + 1)
                    eng.wait_ge(m_d, given(m_d) + 2 * (E - 1) + tt + 1)
                    eng.activation(ah[:, tt, :], a[:, tt, :], ACT.Copy).then_inc(m_ah, 1)

                def body(e, E, u, ld):
                    high_d(E, u)
                    silu(E, 0)
                    if not (isinstance(e, int) and e == NE - 1):
                        high_gu(E + 1, 1 - u, ld if u == 0 else ld + 1)
                    high_a(E, 0)
                    silu(E, 1)
                    high_a(E, 1)

                high_gu(NE * s, 0, NE // 2 * s + 1)
                each_expert(eng, s, body)
                eng.wait_ge(m_d, given(m_d) + 2 * NE * (s + 1))
                if s:
                    eng.wait_ge(m_tt, 4 * s)
                for m in range(2):
                    for tt in range(2):
                        eng.activation(OT[:, 2 * m + tt, :], ps[:, OB[m][tt], :], ACT.Copy).then_inc(m_ot, 1)

        @block.vector
        def _(eng):
            g["give"](eng, "vector")
            for s in range(SG):
                def low_gu(E, u):
                    eng.wait_ge(m_hg, E + 1)
                    eng.tensor_tensor(wl[:, u, GU], raw[:, u, GU], wh[:, u, GU].bitcast(F32),
                                      ALU.subtract).then_inc(m_lg, 1)

                def low_d(E, u):
                    eng.wait_ge(m_hd, E + 1)
                    eng.tensor_tensor(wl[:, u, DN], raw[:, u, DN], wh[:, u, DN].bitcast(F32),
                                      ALU.subtract).then_inc(m_ld_, 1)

                def mul(E, tt):
                    eng.wait_ge(m_sw, given(m_sw) + 2 * E + tt + 1)
                    eng.wait_ge(m_u, given(m_u) + 2 * E + tt + 1)
                    eng.wait_ge(m_ah, given(m_ah) + 2 * (E - 1) + tt + 1)
                    eng.tensor_tensor(a[:, tt, :], sw[:, tt, :], ps[:, UB[tt], :], ALU.mult).then_inc(m_a, 1)

                def low_a(E, tt):
                    eng.wait_ge(m_ah, given(m_ah) + 2 * E + tt + 1)
                    eng.tensor_tensor(al[:, tt, :], a[:, tt, :], ah[:, tt, :].bitcast(F32),
                                      ALU.subtract).then_inc(m_al, 1)

                def body(e, E, u, ld):
                    low_d(E, u)
                    mul(E, 0)
                    if not (isinstance(e, int) and e == NE - 1):
                        low_gu(E + 1, 1 - u)
                    low_a(E, 0)
                    mul(E, 1)
                    low_a(E, 1)

                low_gu(NE * s, 0)
                each_expert(eng, s, body)
                for q in range(4):
                    eng.wait_ge(m_tt, 4 * s + q + 1)
                    for r in range(2):
                        i = 8 * s + 2 * q + r
                        eng.tensor_tensor(X[:, i, :], ps[:, q, r * DIM:(r + 1) * DIM], X[:, i, :],
                                          ALU.add).then_inc(m_y, 1)

        @block.gpsimd
        def _(eng):
            g["give"](eng, "gpsimd")
            eng.memset(wb[:, :, :], 1.0).then_inc(m_one, 1)
            eng.wait_ge(m_one, 1)
            for s in range(SG):
                def body(e, E, u, ld):
                    if not known(E, 2):
                        eng.wait_ge(m_wb[u], 16 * (ld - 1))
                    for tt in range(2):
                        eng.wait_ge(m_sg, given(m_sg) + 2 * E + tt + 1)
                        eng.wait_ge(m_a, given(m_a) + 2 * (E - 1) + tt + 1)
                        eng.tensor_tensor(sw[:, tt, :], sg[:, tt, :], wb[:, u, tt * UT:(tt + 1) * UT],
                                          ALU.mult).then_inc(m_sw, 1)

                each_expert(eng, s, body)


def layout(inputs):
    import numpy as np
    a = {k: np.asarray(v) for k, v in inputs.items()}
    f = np.float32
    row = lambda v: np.ascontiguousarray(v.reshape(1, -1))
    cols = lambda v: np.ascontiguousarray(v.reshape(-1, P).T)
    c = np.arange(P)
    q = c % SEQ

    def part(name, at):
        gate, up, down = (a[f"L1_ffn_{name}_{k}"] for k in ("gate", "up", "down"))
        if name == "shared":
            gate, up, down = gate[None, at], up[None, at], down[None, :, at]
        up_ = lambda w: w.reshape(-1, EDIM, 2, P).transpose(0, 3, 2, 1).reshape(-1, P, 2 * EDIM)
        return np.concatenate([up_(gate), up_(up), down.transpose(0, 2, 1)], axis=2)

    ew = np.concatenate([part("shared", slice(0, EDIM)), part("shared", slice(EDIM, 2 * EDIM)),
                         part("expert", None)], axis=0)
    arrays = {
        "x": a["x"].reshape(TOK, DIM),
        "ctxT": a["ctx_512"].reshape(BATCH * CTX, CDIM).T,
        "wq1": a["L0_xattn_Wq"].T, "wkv1": a["L0_xattn_Wkv"].T, "wo1": a["L0_xattn_Wo"].T,
        "wqkv2": a["L0_attn_w_attn"], "bqk2": cols(a["L0_attn_b_attn"][:2 * DIM]),
        "bv2": row(a["L0_attn_b_attn"][2 * DIM:]),
        "wproj": a["L0_attn_w_proj"], "bproj": row(a["L0_attn_b_proj"]),
        "wg3": a["L0_ffn_w_gate"].T, "wu3": a["L0_ffn_w_up"].T, "wd3": a["L0_ffn_w_down"].T,
        "wq4": a["L1_xattn_Wq"], "wk4": a["L1_xattn_Wk"], "wv4": a["L1_xattn_Wv"],
        "bqk4": np.concatenate([cols(a["L1_xattn_bq"]), cols(a["L1_xattn_bk"])], axis=1),
        "bv4": row(a["L1_xattn_bv"]),
        "wqkv5": a["L1_attn_W"].T, "bqk5": cols(a["L1_attn_b"][:2 * DIM]), "bv5": row(a["L1_attn_b"][2 * DIM:]),
        "wr6": a["L1_ffn_gate_w"].T, "br6": row(a["L1_ffn_gate_bias"]),
        "ew6": ew,
        "c_ident": np.eye(P, dtype=f),
        "c_headmask": (c[:, None] // HD == np.arange(8)[None]).astype(f),
        "c_oddmask": ((c[:, None] // HD) % 2 == np.arange(2)[None]).astype(f),
        "c_causal": np.where(np.arange(SEQ)[None] > q[:, None], NEG, 0.0).astype(f),
        "c_ones": np.ones((P, P), f),
    }
    return {k: np.ascontiguousarray(v) for k, v in arrays.items()}


def kernel(**inputs):
    import concourse.bacc as bacc
    from concourse.bass_utils import run_bass_kernel_spmd

    nc = bacc.Bacc("TRN2", target_bir_lowering=False, num_devices=1)
    arrays = {"in_" + k: v for k, v in layout(inputs).items()}
    io = {k[3:]: nc.dram_tensor(k, v.shape, mybir.dt.from_np(v.dtype), kind="ExternalInput").ap()
          for k, v in arrays.items()}
    out = nc.dram_tensor("out", (TOK, DIM), F32, kind="ExternalOutput").ap()
    build(nc, io, out)
    r = run_bass_kernel_spmd(nc, [arrays], core_ids=[0])
    return r.results[0]["out"].reshape(BATCH, SEQ, DIM)
```

```python
import concourse.bass as bass
from concourse import mybir
from contextlib import ExitStack

F32 = mybir.dt.float32
F32R = mybir.dt.float32r
BF16 = mybir.dt.bfloat16
ALU = mybir.AluOpType
ACT = mybir.ActivationFunctionType
AX = mybir.AxisListType

P = 128
BATCH, SEQ, DIM = 32, 64, 256
CTX, CDIM = 256, 128
HEADS = 16
HD = DIM // HEADS
TOK = BATCH * SEQ
NPAIR = TOK // P
HALF = 2
INNER = 1024
EXPERTS, EDIM, TOPK = 32, 128, 8
NE = EXPERTS + 2
EPS = 1e-5
ROUND = 12582912.0
SCALE = float(HD) ** -0.5
NEG = -1e30


GIVEN = {}


def given(s):
    return GIVEN.get(s.name, 0)


def known(i, low):
    return isinstance(i, int) and i < low


def ahead(i):
    return not (isinstance(i, int) and (i < 0 or i + 2 >= NPAIR))


def opening(i):
    return isinstance(i, int) and i == -1


def closing(i):
    return isinstance(i, int) and i == NPAIR - 1


def upto(n, most):
    return min(n, most) if isinstance(n, int) else n


def pipeline(eng, body, once=None):
    body(-1, 1, True, False, False, 1)
    body(0, 0, True, True, False, 1)
    if once:
        once()
    with eng.Fori(0, (NPAIR - 2) // 2) as j:
        body(2 * j + 1, 1, True, True, True, j + 2)
        body(2 * j + 2, 0, True, True, True, j + 2)
    body(NPAIR - 1, 1, False, True, True, 0)
    body(NPAIR, 0, False, False, True, 0)


def long_pipeline(eng, body):
    body(-1, 1, True, False, False, False, 1)
    body(0, 0, True, True, False, False, 1)
    body(1, 1, True, True, True, False, 2)
    with eng.Fori(0, (NPAIR - 4) // 2) as j:
        body(2 * j + 2, 0, True, True, True, True, j + 2)
        body(2 * j + 3, 1, True, True, True, True, j + 3)
    body(NPAIR - 2, 0, True, True, True, True, NPAIR // 2)
    body(NPAIR - 1, 1, False, True, True, True, 0)
    body(NPAIR, 0, False, False, True, True, 0)
    body(NPAIR + 1, 1, False, False, False, True, 0)


def prev_use(ring, i, k):
    n = len(ring)
    d = next(d for d in range(1, n + 1) if ring[(k - d) % n] == ring[k])
    return n * i + k - d + 1


def build(nc, io, out, stages=6):
    with ExitStack() as ctx:
        def sb(name, shape, dt=F32):
            return ctx.enter_context(nc.sbuf_tensor(name, list(shape), dt))

        credits = {"tensor": [], "vector": [], "scalar": [], "gpsimd": []}

        def sem(name, credit=0, by=None):
            s = ctx.enter_context(nc.semaphore(name))
            if credit:
                GIVEN[s.name] = credit
                credits[by].append(s)
            return s

        ps = ctx.enter_context(nc.psum_tensor("ps", [P, 8, 512], F32))

        X = sb("X", [P, NPAIR, DIM])
        ident = sb("ident", [P, P])
        headmask = sb("headmask", [P, 8])
        oddmask = sb("oddmask", [P, 2])
        causal = sb("causal", [P, SEQ])
        ones = sb("ones", [P, P])

        lnstat = sb("lnstat", [P, 2, 6])
        lnmv = sb("lnmv", [P, 2, 2])
        lneps = sb("lneps", [P, 2, 1])
        lnrs = sb("lnrs", [P, 2, 1])
        mhalf = sb("mhalf", [P, 1])
        epsc = sb("epsc", [P, 1])
        h = sb("h", [P, 2, DIM])
        hT = sb("hT", [P, 2, HALF, P])

        bqs = {2: sb("bqs2", [P, 2]), 5: sb("bqs5", [P, 2])}
        wr6 = sb("wr6", [P, 2, EXPERTS]); br6 = sb("br6", [P, EXPERTS])
        mean6 = sb("mean6", [P, NPAIR]); rs6 = sb("rs6", [P, NPAIR])
        wdram = nc.dram_tensor("token_weights", (NE, TOK), F32, kind="Internal").ap()
        identb = sb("identb", [P, P], BF16)
        wq3 = [sb("wq3g", [P, 2, INNER], BF16), sb("wq3u", [P, 2, INNER], BF16), sb("wq3d", [P, 8, DIM], BF16)]
        wsc = sb("wsc", [P, 3]); wrs = sb("wrs", [P, 3])
        s_const = sem("s_const")
        s_x0 = sem("s_x0"); s_x = sem("s_x")
        s_half = sem("s_half")
        s_w1 = sem("s_w1")
        s_xdone = sem("s_xdone", 1, "vector")
        x_st = sem("x_st"); x_mv = sem("x_mv"); x_eps = sem("x_eps"); x_rs = sem("x_rs", 2, "gpsimd")
        x_mean = sem("x_mean")
        ln_st = sem("ln_st")
        ln_mv = sem("ln_mv")
        ln_eps = sem("ln_eps")
        ln_rs = sem("ln_rs")
        ln_h = sem("ln_h")
        ln_T = sem("ln_T", 2, "tensor")
        ln_hT = sem("ln_hT")

        wq1 = sb("wq1", [P, 2, DIM]); wkv1 = sb("wkv1", [P, 2 * DIM]); wo1 = sb("wo1", [P, 2, DIM])
        wqkv = {2: sb("wqkv2", [P, 2, 3 * DIM]), 5: sb("wqkv5", [P, 2, 3 * DIM])}
        bqk = {2: sb("bqk2", [P, 4]), 5: sb("bqk5", [P, 4])}
        bv = {2: sb("bv2", [P, DIM]), 5: sb("bv5", [P, DIM]), 4: sb("bv4", [P, DIM])}
        wproj = sb("wproj", [P, 2, DIM]); bproj = sb("bproj", [P, DIM])
        wq4 = sb("wq4", [P, 2, DIM]); wk4 = sb("wk4", [P, DIM]); wv4 = sb("wv4", [P, DIM])
        bqk4 = sb("bqk4", [P, 4])

        def cin(v):
            return v.rearrange("(c p) n -> p c n", p=P)

        const_loads = [
            (ident, io["c_ident"]), (wq1, cin(io["wq1"])), (headmask, io["c_headmask"]),
            (wkv1, io["wkv1"]), (oddmask, io["c_oddmask"]), (wo1, cin(io["wo1"])), (ones, io["c_ones"]),
        ]
        late_loads = [
            (causal, io["c_causal"]),
            (wqkv[2], cin(io["wqkv2"])), (wqkv[5], cin(io["wqkv5"])),
            (bqk[2], io["bqk2"]), (bqk[5], io["bqk5"]), (bqk4, io["bqk4"]),
            (bv[2], io["bv2"].partition_broadcast(P)), (bv[5], io["bv5"].partition_broadcast(P)),
            (bv[4], io["bv4"].partition_broadcast(P)),
            (wproj, cin(io["wproj"])), (bproj, io["bproj"].partition_broadcast(P)),
            (wq4, cin(io["wq4"])), (wk4, io["wk4"]), (wv4, io["wv4"]),
            (wr6, cin(io["wr6"])), (br6, io["br6"].partition_broadcast(P)),
        ]

        lnt = [0, NPAIR, 2 * NPAIR, 2 * NPAIR, 3 * NPAIR, 4 * NPAIR]

        def ln_dve(eng, n, i, u, between=None):
            b = NPAIR * n
            if n == 0:
                if known(i, 2):
                    eng.wait_ge(s_x0, 16)
                else:
                    eng.wait_ge(s_x, 32)
            else:
                eng.wait_ge(s_xdone, given(s_xdone) + b - NPAIR + i + 1)
            eng.bn_stats(lnstat[:, u, :], X[:, i, :]).then_inc(ln_st, 1)
            if between:
                between()
            eng.wait_ge(ln_st, b + i + 1)
            eng.nop(nofuse=True)
            eng.bn_aggr(lnmv[:, u, :], lnstat[:, u, :]).then_inc(ln_mv, 1)

        def ln_dve2(eng, n, i, u, reader=None, _=0):
            b = NPAIR * n
            eng.wait_ge(ln_rs, b + i + 1)
            if reader is None:
                eng.wait_ge(ln_T, given(ln_T) + lnt[n] + i - 1)
            eng.tensor_scalar(h[:, u, :], X[:, i, :], lnmv[:, u, 0:1], lnrs[:, u, :],
                              ALU.subtract, ALU.mult).then_inc(ln_h, 1)

        def ln_pool(eng, n, i, u):
            b = NPAIR * n
            eng.wait_ge(ln_mv, b + i + 1)
            eng.tensor_tensor(lneps[:, u, :], lnmv[:, u, 1:2], epsc[:, :], ALU.add).then_inc(ln_eps, 1)
            eng.wait_ge(ln_eps, b + i + 1)
            eng.tensor_tensor(lnrs[:, u, :], lneps[:, u, :], mhalf[:, :], ALU.pow).then_inc(ln_rs, 1)

        def transpose2(eng, dst, src):
            for c in range(HALF):
                ins = eng.transpose(dst[:, c * P:(c + 1) * P], src[:, c * P:(c + 1) * P], ident[:, :])
            return ins

        def ln_pe(eng, n, i, u, bank):
            eng.wait_ge(ln_h, NPAIR * n + i + 1)
            transpose2(eng, ps[:, bank, :], h[:, u, :]).then_inc(ln_T, 1)

        def ln_act(eng, n, i, u, bank, readers=None):
            eng.wait_ge(ln_T, given(ln_T) + lnt[n] + i + 1)
            if readers is not None:
                readers()
            eng.activation(hT[:, u, :, :], ps[:, bank, 0:DIM], ACT.Copy).then_inc(ln_hT, 1)

        Vs = sb("Vs", [P, 2, 2, DIM])
        with nc.Block() as block:
            @block.sync
            def _(sp):
                xin = io["x"].rearrange("(n p) d -> p n d", p=P)
                sp.dma_start(X[:, 0:2, :], xin[:, 0:2, :]).then_inc(s_x0, 16)
                for dst, src in const_loads:
                    sp.dma_start(dst[:], src).then_inc(s_const, 16)

            @block.vector
            def _(eng):
                eng.memset(mhalf[:, :], -0.5).then_inc(s_half, 1)
                eng.memset(epsc[:, :], EPS).then_inc(s_half, 1)
                eng.memset(Vs[:, :, :, :], 0.0).then_inc(s_half, 1)

        def give(eng, name):
            for s in credits[name]:
                eng.sem_inc(s, given(s))
            credits[name].clear()

        env = dict(locals())
        number = [0]

        def local(*layers):
            with ExitStack() as stack:
                number[0] += 1
                env["sb"] = lambda name, shape, dt=F32: stack.enter_context(
                    nc.sbuf_tensor(f"{name}_{number[0]}", list(shape), dt))
                for layer, *args in layers:
                    layer(nc, ctx, env, *args)

        if stages >= 1:
            local((cross_heads,))
        if stages >= 2:
            local((self_heads, 2))
        if stages >= 3:
            local((quantised_ffn,))
        if stages >= 4:
            local((cross_single,))
        if stages >= 5:
            local((self_heads, 5))
        if stages >= 6:
            local((router,), (experts,))
            return
        with nc.Block() as block:
            @block.sync
            def _(sp):
                sp.wait_ge(s_xdone, given(s_xdone) + NPAIR * stages)
                sp.dma_start(out.rearrange("(n p) d -> p n d", p=P), X[:, :, :]).then_inc(s_x, 16)
                sp.wait_ge(s_x, 48)


def cross_heads(nc, ctx, env):
    g = env
    sb, sem, ps, X, io = g["sb"], g["sem"], g["ps"], g["X"], g["io"]
    ident, headmask, oddmask, hT = g["ident"], g["headmask"], g["oddmask"], g["hT"]
    ln_dve, ln_dve2, ln_pool, ln_pe, ln_act, transpose2 = (g[k] for k in (
        "ln_dve", "ln_dve2", "ln_pool", "ln_pe", "ln_act", "transpose2"))
    ln_hT, ln_T, s_xdone = g["ln_hT"], g["ln_T"], g["s_xdone"]
    wq, wkv, wo = g["wq1"], g["wkv1"], g["wo1"]

    NS = 8
    cx = sb("cx", [P, 2, 2 * CTX])
    cxh = sb("cxh", [P, 2 * CTX], F32R); cxl = sb("cxl", [P, 2 * CTX], F32R)
    wkvh = sb("wkvh", [P, 2 * DIM], F32R); wkvl = sb("wkvl", [P, 2 * DIM], F32R)
    Qs = sb("Qs", [P, 2, HALF, P])
    Qh = sb("Qh", [P, 2, HALF, P], F32R); Ql = sb("Ql", [P, HALF, P])
    Qbh = sb("Qbh", [P, 2, HALF, 2, 8 * SEQ], F32R)
    Qbl = sb("Qbl", [P, 2, HALF, 2, 8 * SEQ], F32R)
    KTh = sb("KTh", [P, 2, HALF, 2 * CTX], F32R); KTl = sb("KTl", [P, 2, HALF, 2 * CTX], F32R)
    V = sb("V", [P, 2, 4, DIM])
    Pr = sb("Pr", [P, 4, 2, CTX])
    PT = sb("PT", [P, 2, 2, 2, P])
    mx = sb("mx", [P, 3, 2])
    den = sb("den", [P, 2, 2, HALF, 4])
    rden = sb("rden", [P, HALF, 4, 2])
    Oe = sb("Oe", [P, 2 * HALF, SEQ])
    OT = sb("OT", [P, 2, 2 * HALF, SEQ])
    On = sb("On", [P, 2, DIM])
    OnT = sb("OnT", [P, 2, HALF, P])

    raw3 = [sb("raw3g", [P, 2, INNER]), sb("raw3u", [P, 2, INNER]), sb("raw3d", [P, 8, DIM])]
    QW = 2 * INNER // NPAIR
    rounded = sb("rounded3", [P, 3, QW])
    absw = sb("absw3", [P, 2 * INNER]); part = sb("part3", [P, 3])
    wq3, wsc, wrs, ones = g["wq3"], g["wsc"], g["wrs"], g["ones"]

    SB = [0, 1, 2, 0, 1, 2, 0, 1]
    TB = [3, 4]
    OB = 5
    FA, FB = 6, 7
    last = 2 * NPAIR

    c_ld = [sem("c_ld0"), sem("c_ld1")]
    c_q = sem("c_q", 2, "tensor"); c_qe = sem("c_qe"); c_qbd = sem("c_qbd", 9, "gpsimd"); c_ql = sem("c_ql")
    c_k = sem("c_k", 3, "tensor"); c_kh = sem("c_kh"); c_ke = sem("c_ke"); c_w = sem("c_w"); c_cxh = sem("c_cxh"); c_cxl = sem("c_cxl", 2, "gpsimd")
    c_v = sem("c_v", 3, "tensor"); c_ve = sem("c_ve", 2, "scalar")
    c_s = sem("c_s", 9, "tensor"); c_max = sem("c_max");
    c_exp = sem("c_exp", 3, "scalar")
    c_t = sem("c_t", 4, "tensor"); c_te = sem("c_te", 2, "vector"); c_pv = sem("c_pv", 9, "tensor")
    c_o1 = sem("c_o1"); c_o2 = sem("c_o2", 1, "vector"); c_rd = sem("c_rd", 8, "vector")
    c_t1 = sem("c_t1", 2, "tensor"); c_on = sem("c_on")
    c_t2 = sem("c_t2", 2, "tensor"); c_t2e = sem("c_t2e", 2, "scalar"); c_wo = sem("c_wo", 2, "tensor")

    q_ld = sem("q_ld"); q_part = sem("q_part"); q_sum = sem("q_sum"); q_sc = sem("q_sc"); q_rs = sem("q_rs")
    q_r = sem("q_r"); q_c = sem("q_c"); s_q3 = sem("s_q3")
    s_const, s_half, s_w1, s_x = g["s_const"], g["s_half"], g["s_w1"], g["s_x"]
    all_consts = 16 * len(g["const_loads"])

    order = [(half, b, s) for half in range(HALF) for b in range(2) for s in range(2)]

    with nc.Block() as block:
        @block.sync
        def _(sp):
            ctxT = io["ctxT"].rearrange("p (n c) -> p n c", c=2 * CTX)

            def load(i, u):
                sp.wait_ge(c_cxl, given(c_cxl) + i - 1)
                sp.dma_start(cx[:, u, :], ctxT[:, i, :]).then_inc(c_ld[u], 16)

            load(0, 0)
            load(1, 1)
            xin = io["x"].rearrange("(n p) d -> p n d", p=P)
            sp.dma_start(X[:, 2:4, :], xin[:, 2:4, :]).then_inc(s_x, 16)
            for n, name in enumerate(("wg3", "wu3", "wd3")):
                sp.dma_start(raw3[n][:, :, :], io[name].rearrange("(c p) n -> p c n", p=P)).then_inc(q_ld, 16)
            sp.dma_start(X[:, 4:NPAIR, :], xin[:, 4:NPAIR, :]).then_inc(s_x, 16)
            for dst, src in g["late_loads"]:
                sp.dma_start(dst[:], src).then_inc(s_w1, 16)
            with sp.Fori(1, NPAIR // 2) as j:
                load(2 * j, 0)
                load(2 * j + 1, 1)

        @block.tensor
        def _(eng):
            g["give"](eng, "tensor")
            eng.wait_ge(s_const, all_consts)
            def scores(i, u, k):
                half, b, s = order[k]
                if k % 4 == 0:
                    eng.wait_ge(c_qbd, given(c_qbd) + 8 * i + 4 * half + 4)
                    eng.wait_ge(c_ke, 2 * i + half + 1)
                eng.wait_ge(c_exp, given(c_exp) + prev_use(SB, i, k))
                for pl in range(2):
                    p = 2 * s + pl
                    out = ps[:, SB[k], pl * CTX:(pl + 1) * CTX]
                    qh, ql = (q[:, u, half, b, p * P:(p + 1) * P] for q in (Qbh, Qbl))
                    kh, kl = (q[:, u, half, b * CTX:(b + 1) * CTX] for q in (KTh, KTl))
                    eng.matmul(out, qh, kh, start=True, stop=False)
                    eng.matmul(out, qh, kl, start=False, stop=False)
                    ins = eng.matmul(out, ql, kh, start=False, stop=True)
                ins.then_inc(c_s, 1)

            def turn(i, u, k):
                eng.wait_ge(c_exp, given(c_exp) + NS * i + k + 1)
                eng.wait_ge(c_te, given(c_te) + NS * i + k - 1)
                for pl in range(2):
                    for kt in range(2):
                        ins = eng.transpose(ps[:, TB[k % 2], (2 * pl + kt) * P:(2 * pl + kt + 1) * P],
                                            Pr[:, k % 4, pl, kt * P:(kt + 1) * P], ident[:, :])
                ins.then_inc(c_t, 1)

            def pv(i, u, k):
                half, b, s = order[k]
                if k == 0:
                    eng.wait_ge(c_o2, given(c_o2) + i)
                    eng.wait_ge(c_ve, given(c_ve) + 2 * i + 2)
                eng.wait_ge(c_te, given(c_te) + NS * i + k + 1)
                r = 2 * half + b
                for pl in range(2):
                    p = 2 * s + pl
                    for kt in range(2):
                        ins = eng.matmul(ps[32 * p:32 * p + 32, OB, r * P:(r + 1) * P],
                                         V[:, u, 2 * b + kt, half * P + 32 * p:half * P + 32 * p + 32],
                                         PT[:, k % 2, pl, kt, :], start=(kt == 0), stop=(kt == 1),
                                         tile_position=(0, 32 * p))
                ins.then_inc(c_pv, 1)

            def qproj(i, u):
                eng.wait_ge(ln_hT, i + 1)
                for m in range(HALF):
                    for c in range(2):
                        ins = eng.matmul(ps[:, FA, m * P:(m + 1) * P], wq[:, c, m * P:(m + 1) * P],
                                         hT[:, u, c, :], start=(c == 0), stop=(c == 1))
                ins.then_inc(c_q, 1)

            def kproj(i, u, m, ld):
                if m == 0:
                    eng.wait_ge(c_qe, i + 1)
                    eng.wait_ge(c_cxl, given(c_cxl) + i + 1)
                    if known(i, 1):
                        eng.wait_ge(c_w, 2)
                else:
                    if not known(i, 1):
                        eng.wait_ge(s_xdone, given(s_xdone) + i - 1)
                out, w = ps[:, (FA, FB)[m], :], slice(m * P, (m + 1) * P)
                eng.matmul(out, wkvh[:, w], cxh[:, :], start=True, stop=False)
                eng.matmul(out, wkvh[:, w], cxl[:, :], start=False, stop=False)
                eng.matmul(out, wkvl[:, w], cxh[:, :], start=False, stop=True).then_inc(c_k, 1)

            def vproj(i, u, m):
                if m == 0:
                    eng.wait_ge(c_ke, 2 * i + 1)
                else:
                    eng.wait_ge(c_ve, given(c_ve) + 2 * i + 1)
                for t in range(2):
                    out, c = ps[:, FA, t * DIM:(t + 1) * DIM], slice((2 * m + t) * P, (2 * m + t + 1) * P)
                    eng.matmul(out, cxh[:, c], wkvh[:, DIM:2 * DIM], start=True, stop=False)
                    eng.matmul(out, cxl[:, c], wkvh[:, DIM:2 * DIM], start=False, stop=False)
                    ins = eng.matmul(out, cxh[:, c], wkvl[:, DIM:2 * DIM], start=False, stop=True)
                ins.then_inc(c_v, 1)

            def tail1(t, u):
                eng.wait_ge(c_o2, given(c_o2) + t + 1)
                eng.wait_ge(c_ke, upto(2 * (t + 2), last))
                eng.wait_ge(s_xdone, given(s_xdone) + t)
                src = OT[:, u, :, :].rearrange("p r q -> p (r q)")
                transpose2(eng, ps[:, FB, :], src).then_inc(c_t1, 1)

            def tail2(t, u):
                eng.wait_ge(c_on, t + 1)
                transpose2(eng, ps[:, FB, :], On[:, u, :]).then_inc(c_t2, 1)

            def tail3(t, u):
                eng.wait_ge(c_t2e, given(c_t2e) + t + 1)
                for c in range(HALF):
                    ins = eng.matmul(ps[:, FB, 0:DIM], OnT[:, u, c, :], wo[:, c, :],
                                     start=(c == 0), stop=(c == 1))
                ins.then_inc(c_wo, 1)

            def body(i, u, front, mid, tail, ld):
                v = 1 - u

                def step(k):
                    if mid and k < NS:
                        scores(i, u, k)
                    if mid and k >= 2:
                        turn(i, u, k - 2)
                    elif tail and k < 2:
                        turn(i - 1, v, NS - 2 + k)
                    if mid and k >= 3:
                        pv(i, u, k - 3)
                    elif tail and k < 3:
                        pv(i - 1, v, NS - 3 + k)

                step(0)
                step(1)
                if front:
                    eng.wait_ge(c_ve, given(c_ve) + 2 * i + 2)
                    ln_pe(eng, 0, i + 1, v, FA)
                step(2)
                if front:
                    qproj(i + 1, v)
                step(3)
                if tail:
                    tail1(i - 1, v)
                if front:
                    kproj(i + 1, v, 0, ld)
                step(4)
                if tail:
                    tail2(i - 1, v)
                if front:
                    vproj(i + 1, v, 0)
                step(5)
                if tail:
                    tail3(i - 1, v)
                if front:
                    vproj(i + 1, v, 1)
                step(6)
                if front:
                    kproj(i + 1, v, 1, ld)
                step(7)

            def weight_sums():
                eng.wait_ge(q_part, 3)
                eng.wait_ge(c_ke, 4)
                eng.matmul(ps[:, FB, 0:3], ones[:, :], part[:, :], start=True, stop=True).then_inc(q_sum, 1)
                eng.wait_ge(q_sc, 1)

            pipeline(eng, body, weight_sums)

        @block.vector
        def _(eng):
            g["give"](eng, "vector")

            def rowmax(i, k):
                eng.wait_ge(c_s, given(c_s) + NS * i + k + 1)
                eng.tensor_reduce(mx[:, SB[k], :], ps[:, SB[k], :].rearrange("p (a n) -> p a n", a=2),
                                  AX.X, ALU.max, negate=True).then_inc(c_max, 1)

            def turned(i, k):
                eng.wait_ge(c_t, given(c_t) + NS * i + k + 1)
                eng.wait_ge(c_pv, given(c_pv) + NS * i + k - 1)
                eng.tensor_copy(PT[:, k % 2, :, :, :], ps[:, TB[k % 2], :]).then_inc(c_te, 1)

            def k_low(i, u, m):
                eng.wait_ge(c_kh, 2 * i + m + 1)
                eng.tensor_tensor(KTl[:, u, m, :], ps[:, (FA, FB)[m], :], KTh[:, u, m, :].bitcast(F32),
                                  ALU.subtract).then_inc(c_ke, 1)

            def o_out(i, u):
                eng.wait_ge(c_pv, given(c_pv) + NS * i + NS)
                eng.wait_ge(c_t1, given(c_t1) + i - 1)
                O = ps[:, OB, :].rearrange("p (r e q) -> p r e q", r=2 * HALF, e=2)
                eng.tensor_scalar(Oe[:, :, :], O[:, :, 0, :], oddmask[:, 0:1], None,
                                  ALU.mult).then_inc(c_o1, 1)
                eng.wait_ge(c_o1, i + 1)
                eng.scalar_tensor_tensor(out=OT[:, u, :, :], in0=O[:, :, 1, :], scalar=oddmask[:, 1:2],
                                         in1=Oe[:, :, :], op0=ALU.mult, op1=ALU.add).then_inc(c_o2, 1)

            def denominators(t, u):
                eng.wait_ge(c_exp, given(c_exp) + NS * (t + 1))
                for b in range(2):
                    for e in range(2):
                        eng.reciprocal(rden[64 * b:64 * b + 64, :, :, e],
                                       den[64 * e:64 * e + 64, u, b, :, :]).then_inc(c_rd, 1)

            def normalise(t, u):
                eng.wait_ge(c_t1, given(c_t1) + t + 1)
                eng.wait_ge(c_rd, given(c_rd) + 4 * t + 4)
                eng.wait_ge(c_t2, given(c_t2) + t - 1)
                eng.tensor_tensor(On[:, u, :].rearrange("p (h d) -> p h d", d=HD),
                                  ps[:, FB, 0:DIM].rearrange("p (h d) -> p h d", d=HD),
                                  rden[:, :, :, :].rearrange("p a b c -> p (a b c)").unsqueeze(2)
                                  .to_broadcast([P, HEADS, HD]), ALU.mult).then_inc(c_on, 1)

            def add_x(t):
                eng.wait_ge(c_wo, given(c_wo) + t + 1)
                eng.tensor_tensor(X[:, t, :], ps[:, FB, 0:DIM], X[:, t, :], ALU.add).then_inc(s_xdone, 1)

            def quantise(t):
                at = bass.ds(QW * t, QW) if not isinstance(t, int) else slice(QW * t, QW * (t + 1))
                flat = [w[:, :, :].rearrange("p c n -> p (c n)") for w in raw3]
                out = [w[:, :, :].rearrange("p c n -> p (c n)") for w in wq3]
                if not known(t, 1):
                    eng.wait_ge(s_q3, 3 * t)
                else:
                    eng.wait_ge(q_rs, 1)
                eng.nop(nofuse=True)
                for n in range(3):
                    eng.tensor_scalar(rounded[:, n, :], flat[n][:, at], wrs[:, n:n + 1], ROUND, ALU.mult,
                                      ALU.add).then_inc(q_r, 1)
                eng.wait_ge(q_r, 3 * t + 3)
                eng.tensor_scalar(rounded[:, :, :], rounded[:, :, :], ROUND, 1.0, ALU.subtract,
                                  ALU.min).then_inc(q_c, 1)
                eng.wait_ge(q_c, t + 1)
                for n in range(3):
                    eng.tensor_scalar(out[n][:, at], rounded[:, n, :], -1.0, None, ALU.max).then_inc(s_q3, 1)

            def body(i, u, front, mid, tail, ld):
                v = 1 - u
                def step(k):
                    if mid:
                        rowmax(i, k)
                    if mid and k >= 2:
                        turned(i, k - 2)
                    elif tail and k < 2:
                        turned(i - 1, NS - 2 + k)

                if front:
                    ln_dve(eng, 0, i + 1, v)
                elif closing(i):
                    ln_dve(eng, 1, 0, v)
                step(0)
                if front:
                    ln_dve2(eng, 0, i + 1, v)
                elif closing(i):
                    ln_dve2(eng, 1, 0, v)
                step(1)
                step(2)
                if tail:
                    o_out(i - 1, v)
                if tail:
                    denominators(i - 1, v)
                step(3)
                if tail:
                    normalise(i - 1, v)
                if front:
                    k_low(i + 1, v, 0)
                step(4)
                if tail:
                    quantise(i - 1)
                step(5)
                if tail:
                    add_x(i - 1)
                step(6)
                step(7)
                if front:
                    k_low(i + 1, v, 1)

            def weight_scales():
                eng.wait_ge(q_sum, 1)
                eng.tensor_scalar(wsc[:, :], ps[:, FB, 0:3], 1.0 / (DIM * INNER), 1e-5, ALU.mult,
                                  ALU.max).then_inc(q_sc, 1)
                eng.wait_ge(q_sc, 1)
                eng.reciprocal(wrs[:, :], wsc[:, :]).then_inc(q_rs, 1)

            eng.wait_ge(s_const, all_consts)
            pipeline(eng, body, weight_scales)
            eng.wait_ge(s_w1, 16 * len(g["late_loads"]))
            for n in (2, 5):
                eng.tensor_scalar(g["bqs"][n][:, :], g["bqk"][n][:, 0:2], SCALE, None, ALU.mult)
            eng.tensor_copy(g["identb"][:, :], ident[:, :])

        @block.scalar
        def _(eng):
            g["give"](eng, "scalar")
            def exps(i, u, k):
                half, b, s = order[k]
                eng.wait_ge(c_max, NS * i + k + 1)
                eng.wait_ge(c_t, given(c_t) + NS * i + k - 3)
                if k == 0:
                    eng.wait_ge(c_rd, given(c_rd) + 4 * (i - 1))
                for pl in range(2):
                    ins = eng.activation(Pr[:, k % 4, pl, :], ps[:, SB[k], pl * CTX:(pl + 1) * CTX], ACT.Exp,
                                         bias=mx[:, SB[k], pl:pl + 1],
                                         accum_out=den[:, u, b, half, 2 * s + pl:2 * s + pl + 1])
                ins.then_inc(c_exp, 1)

            def q_out(i, u):
                eng.wait_ge(c_q, given(c_q) + i + 1)
                eng.wait_ge(c_qbd, given(c_qbd) + 8 * (i - 1))
                eng.activation(Qh[:, u, :, :], ps[:, FA, 0:DIM], ACT.Copy, scale=SCALE)
                eng.activation(Qs[:, u, :, :], ps[:, FA, 0:DIM], ACT.Copy, scale=SCALE).then_inc(c_qe, 1)

            def k_out(i, u, m):
                eng.wait_ge(c_k, given(c_k) + 2 * i + m + 1)
                eng.wait_ge(c_s, given(c_s) + NS * (i - 1))
                eng.activation(KTh[:, u, m, :], ps[:, (FA, FB)[m], :], ACT.Copy).then_inc(c_kh, 1)

            def cx_high(i, u, ld):
                eng.wait_ge(c_ld[u], 16 * ld)
                eng.wait_ge(c_k, given(c_k) + 2 * i)
                eng.activation(cxh[:, :], cx[:, u, :], ACT.Copy).then_inc(c_cxh, 1)

            def v_out(i, u, m):
                eng.wait_ge(c_v, given(c_v) + 2 * i + m + 1)
                eng.wait_ge(c_pv, given(c_pv) + NS * (i - 1))
                eng.activation(V[:, u, 2 * m:2 * m + 2, :], ps[:, FA, :],
                               ACT.Copy).then_inc(c_ve, 1)

            def ot_out(t, u):
                eng.wait_ge(c_t2, given(c_t2) + t + 1)
                eng.wait_ge(c_wo, given(c_wo) + t - 1)
                eng.activation(OnT[:, u, :, :], ps[:, FB, 0:DIM], ACT.Copy).then_inc(c_t2e, 1)

            def weight_part(n):
                eng.wait_ge(q_ld, 48)
                if n:
                    eng.wait_ge(q_part, n)
                eng.activation(absw[:, :], raw3[n][:, :, :].rearrange("p c n -> p (c n)"), ACT.Abs,
                               accum_out=part[:, n:n + 1]).then_inc(q_part, 1)

            def body(i, u, front, mid, tail, ld):
                v = 1 - u

                def ex(*ks):
                    if mid:
                        for k in ks:
                            exps(i, u, k)
                ex(0)
                if front:
                    cx_high(i + 1, v, ld)
                ex(1)
                if front:
                    ln_act(eng, 0, i + 1, v, FA, lambda: eng.wait_ge(c_q, given(c_q) + i))
                ex(2)
                if mid and known(i, 1):
                    weight_part(0)
                if front:
                    q_out(i + 1, v)
                ex(3)
                if front:
                    k_out(i + 1, v, 0)
                ex(4)
                if mid and known(i, 1):
                    weight_part(1)
                if tail:
                    ot_out(i - 1, v)
                if front:
                    v_out(i + 1, v, 0)
                ex(5)
                if front:
                    v_out(i + 1, v, 1)
                ex(6)
                if mid and known(i, 1):
                    weight_part(2)
                if front:
                    k_out(i + 1, v, 1)
                ex(7)

            eng.wait_ge(s_const, all_consts)
            eng.activation(wkvh[:, :], wkv[:, :], ACT.Copy).then_inc(c_w, 1)
            pipeline(eng, body)

        @block.gpsimd
        def _(eng):
            g["give"](eng, "gpsimd")
            eng.wait_ge(s_half, 2)
            eng.wait_ge(s_const, all_consts)

            eng.wait_ge(c_w, 1)
            eng.tensor_tensor(wkvl[:, :], wkv[:, :], wkvh[:, :].bitcast(F32), ALU.subtract).then_inc(c_w, 1)

            def cx_low(i, u):
                eng.wait_ge(c_cxh, i + 1)
                eng.wait_ge(c_k, given(c_k) + 2 * i)
                eng.tensor_tensor(cxl[:, :], cx[:, u, :], cxh[:, :].bitcast(F32), ALU.subtract).then_inc(c_cxl, 1)

            def spread(i, u):
                eng.wait_ge(c_qe, i + 1)
                eng.wait_ge(c_qbd, given(c_qbd) + 8 * i)
                eng.tensor_tensor(Ql[:, :, :], Qs[:, u, :, :], Qh[:, u, :, :].bitcast(F32),
                                  ALU.subtract).then_inc(c_ql, 1)
                eng.wait_ge(c_ql, i + 1)
                eng.wait_ge(c_s, given(c_s) + NS * (i - 1))
                for half in range(HALF):
                    for src, dst in ((Qh[:, u, :, :].bitcast(F32), Qbh), (Ql[:, :, :], Qbl)):
                        for b in range(2):
                            eng.tensor_tensor(
                                dst[:, u, half, b, :].rearrange("p (j q) -> p j q", q=SEQ),
                                src[:, half, b * SEQ:(b + 1) * SEQ].unsqueeze(1).to_broadcast([P, 8, SEQ]),
                                headmask[:, :].unsqueeze(2).to_broadcast([P, 8, SEQ]),
                                ALU.mult).then_inc(c_qbd, 1)

            def body(i, u, front, mid, tail, ld):
                if front:
                    ln_pool(eng, 0, i + 1, 1 - u)
                    cx_low(i + 1, 1 - u)
                    spread(i + 1, 1 - u)
                elif closing(i):
                    ln_pool(eng, 1, 0, 1 - u)

            pipeline(eng, body)


def self_heads(nc, ctx, env, layer):
    g = env
    sb, sem, ps, X = g["sb"], g["sem"], g["ps"], g["X"]
    ident, headmask, oddmask, causal, hT = g["ident"], g["headmask"], g["oddmask"], g["causal"], g["hT"]
    ln_dve, ln_dve2, ln_pool, ln_pe, ln_act, transpose2 = (g[k] for k in (
        "ln_dve", "ln_dve2", "ln_pool", "ln_pe", "ln_act", "transpose2"))
    ln_hT, s_xdone = g["ln_hT"], g["s_xdone"]
    w, bqk, bv = g["wqkv"][layer], g["bqk"][layer], g["bv"][layer]
    proj = layer == 2
    bqs = g["bqs"][layer]
    wproj, bproj = g["wproj"], g["bproj"]
    L = layer - 1
    base = NPAIR * L
    Qs = sb("Qs", [P, 2, HALF, P])
    Qbd = sb("Qbd", [P, 2, HALF, 2, 8 * SEQ])
    KT = sb("KT", [P, 2, HALF, P])
    V = g["Vs"]
    Sm = sb("Sm", [P, 4, 2, 2, SEQ])
    Pr = sb("Pr", [P, 4, 2, P])
    PT = sb("PT", [P, 2, 2, P])
    mx = sb("mx", [P, 4, 4])
    den = sb("den", [P, 2, HALF, 4, 2])
    rden = sb("rden", [P, HALF, 4, 2])
    Oe = sb("Oe", [P, 2 * HALF, SEQ])
    OT = sb("OT", [P, 2, 2 * HALF, SEQ])
    On = sb("On", [P, 2, DIM])
    OnT = sb("OnT", [P, 2, HALF, P])
    xb = sb("xb", [P, 2, DIM])

    x_st, x_mv, x_eps, x_rs, x_mean = (g["x_" + k] for k in ("st", "mv", "eps", "rs", "mean"))
    nst = sb("nst", [P, 2, 6]); nmv = sb("nmv", [P, 2, 2]); neps = sb("neps", [P, 2, 1])

    NS = 4
    SB = [0, 1, 2, 0]
    TB = [3, 4]
    OB = 5
    FA, FB = 6, 7
    per_pair = {"qk": 1, "qke": 4, "qbd": 4, "v": 1, "ve": 2, "s": 4, "m": 4, "max": 4, "exp": 4, "t": 4, "te": 4,
                "pv": 4, "o1": 1, "o2": 1, "rd": 4, "t1": 1, "on": 1, "t2": 1, "t2e": 1, "wo": 1, "xb": 1}

    def counter(name, credit=0, by=None):
        if layer == 2:
            g["a_" + name] = sem("a_" + name, credit, by)
        else:
            GIVEN[g["a_" + name].name] = credit + per_pair[name] * NPAIR
        return g["a_" + name]

    a_qk = counter("qk", 2, "tensor"); a_qke = counter("qke"); a_qbd = counter("qbd", 5, "gpsimd")
    a_v = counter("v"); a_ve = counter("ve")
    a_s = counter("s", 5, "tensor"); a_m = counter("m", 3, "vector"); a_max = counter("max")
    a_exp = counter("exp", 5, "scalar");
    a_t = counter("t", 5, "tensor"); a_te = counter("te", 2, "scalar"); a_pv = counter("pv", 5, "tensor")
    a_o1 = counter("o1"); a_o2 = counter("o2", 1, "vector"); a_rd = counter("rd", 8, "vector")
    a_t1 = counter("t1", 2, "tensor"); a_on = counter("on", 2, "vector")
    a_t2 = counter("t2", 2, "tensor"); a_t2e = counter("t2e", 2, "scalar"); a_wo = counter("wo", 2, "tensor")
    a_xb = counter("xb")

    with nc.Block() as block:
        @block.tensor
        def _(eng):
            g["give"](eng, "tensor")
            def scores(i, u, k):
                half, s = divmod(k, 2)
                if s == 0:
                    eng.wait_ge(a_qbd, given(a_qbd) + 4 * i + 2 * half + 2)
                eng.wait_ge(a_m, given(a_m) + prev_use(SB, i, k))
                for pl in range(2):
                    p = 2 * s + pl
                    for b in range(2):
                        ins = eng.matmul(ps[:, SB[k], (2 * pl + b) * P:(2 * pl + b + 1) * P],
                                         Qbd[:, u, half, b, p * P:(p + 1) * P], KT[:, u, half, :],
                                         start=True, stop=True)
                ins.then_inc(a_s, 1)

            def turn(i, u, k):
                eng.wait_ge(a_exp, given(a_exp) + NS * i + k + 1)
                eng.wait_ge(a_te, given(a_te) + NS * i + k - 1)
                for pl in range(2):
                    ins = eng.transpose(ps[:, TB[k % 2], pl * P:(pl + 1) * P],
                                        Pr[:, k, pl, :], ident[:, :])
                ins.then_inc(a_t, 1)

            def pv(i, u, k):
                half, s = divmod(k, 2)
                if k == 0:
                    eng.wait_ge(a_o2, given(a_o2) + i)
                    eng.wait_ge(a_ve, given(a_ve) + 2 * i + 2)
                eng.wait_ge(a_te, given(a_te) + NS * i + k + 1)
                for b in range(2):
                    r = 2 * half + b
                    for pl in range(2):
                        p = 2 * s + pl
                        ins = eng.matmul(ps[32 * p:32 * p + 32, OB, r * P:(r + 1) * P],
                                         V[:, u, b, half * P + 32 * p:half * P + 32 * p + 32],
                                         PT[:, k % 2, pl, :], start=True, stop=True,
                                         tile_position=(0, 32 * p))
                ins.then_inc(a_pv, 1)

            def qkproj(i, u):
                eng.wait_ge(ln_hT, g["lnt"][L] + i + 1)
                for m in range(4):
                    for c in range(2):
                        ins = eng.matmul(ps[:, FA, m * P:(m + 1) * P], w[:, c, m * P:(m + 1) * P],
                                         hT[:, u, c, :], start=(c == 0), stop=(c == 1))
                ins.then_inc(a_qk, 1)

            def vproj(i, u):
                eng.wait_ge(a_qke, given(a_qke) + 4 * i + 4)
                for c in range(2):
                    ins = eng.matmul(ps[:, FA, 0:DIM], hT[:, u, c, :], w[:, c, 2 * DIM:3 * DIM],
                                     start=(c == 0), stop=(c == 1))
                ins.then_inc(a_v, 1)

            def tail1(t, u):
                eng.wait_ge(a_o2, given(a_o2) + t + 1)
                if proj:
                    eng.wait_ge(s_xdone, given(s_xdone) + base + t)
                else:
                    eng.wait_ge(a_on, given(a_on) + t)
                src = OT[:, u, :, :].rearrange("p r q -> p (r q)")
                transpose2(eng, ps[:, FB, :], src).then_inc(a_t1, 1)

            def tail2(t, u):
                eng.wait_ge(a_on, given(a_on) + t + 1)
                transpose2(eng, ps[:, FB, :], On[:, u, :]).then_inc(a_t2, 1)

            def tail3(t, u):
                eng.wait_ge(a_t2e, given(a_t2e) + t + 1)
                for c in range(HALF):
                    ins = eng.matmul(ps[:, FB, 0:DIM], OnT[:, u, c, :], wproj[:, c, :],
                                     start=(c == 0), stop=(c == 1))
                ins.then_inc(a_wo, 1)

            def body(i, u, front, mid, tail, late, ld):
                v = 1 - u

                def step(k, between=None):
                    if mid:
                        scores(i, u, k)
                    if mid and k >= 2:
                        turn(i, u, k - 2)
                    elif tail and k < 2:
                        turn(i - 1, v, NS - 2 + k)
                    if between:
                        between()
                    if mid and k >= 3:
                        pv(i, u, k - 3)
                    elif tail and k < 3:
                        pv(i - 1, v, NS - 3 + k)

                if mid:
                    eng.wait_ge(a_qke, given(a_qke) + 4 * i + 4)
                step(0)
                if late and proj:
                    tail2(i - 2, u)

                def normed():
                    if front:
                        if not known(i, 0):
                            eng.wait_ge(a_ve, given(a_ve) + 2 * i + 2)
                        ln_pe(eng, L, i + 1, v, FA)

                def queries():
                    if front:
                        qkproj(i + 1, v)

                step(1, normed)
                step(2, queries)
                if late and proj:
                    tail3(i - 2, u)

                def values():
                    if tail:
                        tail1(i - 1, v)
                    if front:
                        vproj(i + 1, v)

                step(3, values)

            long_pipeline(eng, body)

        @block.vector
        def _(eng):
            g["give"](eng, "vector")
            def mask(i, k):
                eng.wait_ge(a_s, given(a_s) + NS * i + k + 1)
                eng.wait_ge(a_exp, given(a_exp) + NS * (i - 1) + k + 1)
                S = ps[:, SB[k], :].rearrange("p (a c n) -> p a c n", a=2, c=4)[:, :, 0:4:3, :]
                eng.tensor_tensor(Sm[:, k, :, :, :], S,
                                  causal[:, :].unsqueeze(1).unsqueeze(1).to_broadcast([P, 2, 2, SEQ]),
                                  ALU.add).then_inc(a_m, 1)
                eng.wait_ge(a_m, given(a_m) + NS * i + k + 1)
                eng.tensor_reduce(mx[:, k, :], Sm[:, k, :, :, :], AX.X, ALU.max,
                                  negate=True).then_inc(a_max, 1)

            def v_out(i, u):
                eng.wait_ge(a_v, given(a_v) + i + 1)
                eng.wait_ge(a_pv, given(a_pv) + NS * (i - 1))
                for b in range(2):
                    r = slice(64 * b, 64 * b + 64)
                    eng.tensor_tensor(V[r, u, b, :], ps[r, FA, 0:DIM], bv[r, :], ALU.add).then_inc(a_ve, 1)

            def o_out(i, u):
                eng.wait_ge(a_pv, given(a_pv) + NS * i + NS)
                eng.wait_ge(a_t1, given(a_t1) + i - 1)
                O = ps[:, OB, :].rearrange("p (r e q) -> p r e q", r=2 * HALF, e=2)
                eng.tensor_scalar(Oe[:, :, :], O[:, :, 0, :], oddmask[:, 0:1], None,
                                  ALU.mult).then_inc(a_o1, 1)
                eng.wait_ge(a_o1, given(a_o1) + i + 1)
                eng.scalar_tensor_tensor(out=OT[:, u, :, :], in0=O[:, :, 1, :], scalar=oddmask[:, 1:2],
                                         in1=Oe[:, :, :], op0=ALU.mult, op1=ALU.add).then_inc(a_o2, 1)

            def denominators(t, u):
                eng.wait_ge(a_exp, given(a_exp) + NS * (t + 1))
                eng.wait_ge(a_on, given(a_on) + t)
                for b in range(2):
                    for e in range(2):
                        eng.reciprocal(rden[64 * b:64 * b + 64, :, :, e],
                                       den[64 * e:64 * e + 64, u, :, :, b]).then_inc(a_rd, 1)

            def normalise(t, u):
                eng.wait_ge(a_t1, given(a_t1) + t + 1)
                eng.wait_ge(a_rd, given(a_rd) + 4 * t + 4)
                if proj:
                    eng.wait_ge(a_t2, given(a_t2) + t - 1)
                else:
                    eng.wait_ge(s_xdone, given(s_xdone) + base + t - 1)
                eng.tensor_tensor(On[:, u, :].rearrange("p (h d) -> p h d", d=HD),
                                  ps[:, FB, 0:DIM].rearrange("p (h d) -> p h d", d=HD),
                                  rden[:, :, :, :].rearrange("p a b c -> p (a b c)").unsqueeze(2)
                                  .to_broadcast([P, HEADS, HD]), ALU.mult).then_inc(a_on, 1)

            def add_x(t, u):
                if proj:
                    eng.wait_ge(a_wo, given(a_wo) + t + 1)
                    eng.wait_ge(a_xb, given(a_xb) + t + 1)
                    eng.tensor_tensor(X[:, t, :], ps[:, FB, 0:DIM], xb[:, u, :],
                                      ALU.add).then_inc(s_xdone, 1)
                else:
                    eng.wait_ge(a_on, given(a_on) + t + 1)
                    eng.tensor_tensor(X[:, t, :], On[:, u, :], X[:, t, :], ALU.add).then_inc(s_xdone, 1)

            def next_stats(t, u):
                eng.wait_ge(s_xdone, given(s_xdone) + base + t + 1)
                eng.nop(nofuse=True)
                eng.bn_stats(nst[:, u, :], X[:, t, :]).then_inc(x_st, 1)

            def next_mean(t, u):
                eng.wait_ge(x_st, t + 1)
                eng.wait_ge(x_rs, given(x_rs) + t - 1)
                eng.nop(nofuse=True)
                eng.bn_aggr(nmv[:, u, :], nst[:, u, :]).then_inc(x_mv, 1)

            def next_keep(t, u):
                eng.wait_ge(x_mv, t + 1)
                eng.tensor_copy(g["mean6"][:, bass.ds(t, 1)], nmv[:, u, 0:1]).then_inc(x_mean, 1)

            def body(i, u, front, mid, tail, late, ld):
                v = 1 - u
                if front and not opening(i):
                    ln_dve(eng, L, i + 1, v)
                elif closing(i) and proj:
                    ln_dve(eng, L + 1, 0, v)
                if late and not proj:
                    add_x(i - 2, u)
                if mid:
                    mask(i, 0)
                if front and not opening(i):
                    ln_dve2(eng, L, i + 1, v)
                elif closing(i) and proj:
                    ln_dve2(eng, L + 1, 0, v)
                if late and not proj:
                    next_stats(i - 2, u)
                if mid:
                    mask(i, 1)
                if late and not proj:
                    next_mean(i - 2, u)
                if tail:
                    denominators(i - 1, v)
                if mid:
                    mask(i, 2)
                if late and not proj:
                    next_keep(i - 2, u)
                if tail:
                    o_out(i - 1, v)
                if late and proj:
                    add_x(i - 2, u)
                if mid:
                    mask(i, 3)
                if tail:
                    normalise(i - 1, v)
                if front:
                    v_out(i + 1, v)

            long_pipeline(eng, body)

        @block.scalar
        def _(eng):
            g["give"](eng, "scalar")
            def exps(i, u, k):
                half, s = divmod(k, 2)
                eng.wait_ge(a_max, given(a_max) + NS * i + k + 1)
                eng.wait_ge(a_t, given(a_t) + NS * (i - 1) + k + 1)
                if k == 0:
                    eng.wait_ge(a_rd, given(a_rd) + 4 * (i - 1))
                for pl in range(2):
                    for b in range(2):
                        ins = eng.activation(Pr[:, k, pl, b * SEQ:(b + 1) * SEQ], Sm[:, k, pl, b, :], ACT.Exp,
                                             bias=mx[:, k, 2 * pl + b:2 * pl + b + 1],
                                             accum_out=den[:, u, half, 2 * s + pl, b:b + 1])
                ins.then_inc(a_exp, 1)

            def turned(i, k):
                eng.wait_ge(a_t, given(a_t) + NS * i + k + 1)
                eng.wait_ge(a_pv, given(a_pv) + NS * i + k - 1)
                eng.activation(PT[:, k % 2, :, :], ps[:, TB[k % 2], 0:2 * P], ACT.Copy).then_inc(a_te, 1)

            def qk_out(i, u):
                eng.wait_ge(a_qk, given(a_qk) + i + 1)
                eng.wait_ge(a_qbd, given(a_qbd) + 4 * (i - 1))
                for m in range(2):
                    eng.activation(Qs[:, u, m, :], ps[:, FA, m * P:(m + 1) * P], ACT.Identity,
                                   bias=bqs[:, m:m + 1], scale=SCALE).then_inc(a_qke, 1)
                eng.wait_ge(a_s, given(a_s) + NS * (i - 1))
                for m in range(2):
                    eng.activation(KT[:, u, m, :], ps[:, FA, (2 + m) * P:(3 + m) * P], ACT.Identity,
                                   bias=bqk[:, 2 + m:3 + m]).then_inc(a_qke, 1)

            def ot_out(t, u):
                eng.wait_ge(a_t2, given(a_t2) + t + 1)
                eng.wait_ge(a_wo, given(a_wo) + t - 1)
                eng.activation(OnT[:, u, :, :], ps[:, FB, 0:DIM], ACT.Copy).then_inc(a_t2e, 1)

            def body(i, u, front, mid, tail, late, ld):
                v = 1 - u
                if tail:
                    turned(i - 1, 2)
                if late and proj:
                    ot_out(i - 2, u)
                if mid:
                    exps(i, u, 0)
                if tail:
                    turned(i - 1, 3)
                if front:
                    if not known(i, 1):
                        eng.wait_ge(a_v, given(a_v) + i)
                    ln_act(eng, L, i + 1, v, FA)
                if mid:
                    exps(i, u, 1)
                    turned(i, 0)
                if front:
                    qk_out(i + 1, v)
                if mid:
                    exps(i, u, 2)
                    turned(i, 1)
                    exps(i, u, 3)

            long_pipeline(eng, body)

        @block.gpsimd
        def _(eng):
            g["give"](eng, "gpsimd")
            def spread(i, u, quarters):
                eng.wait_ge(a_qke, given(a_qke) + 4 * i + 2)
                eng.wait_ge(a_s, given(a_s) + NS * (i - 1))
                for half, b in quarters:
                    eng.tensor_tensor(
                        Qbd[:, u, half, b, :].rearrange("p (j q) -> p j q", q=SEQ),
                        Qs[:, u, half, b * SEQ:(b + 1) * SEQ].unsqueeze(1).to_broadcast([P, 8, SEQ]),
                        headmask[:, :].unsqueeze(2).to_broadcast([P, 8, SEQ]),
                        ALU.mult).then_inc(a_qbd, 1)

            def next_scale(t, u):
                eng.wait_ge(x_mv, t + 1)
                eng.tensor_tensor(neps[:, u, :], nmv[:, u, 1:2], g["epsc"][:, :], ALU.add).then_inc(x_eps, 1)
                eng.wait_ge(x_eps, t + 1)
                eng.tensor_tensor(g["rs6"][:, bass.ds(t, 1)], neps[:, u, :], g["mhalf"][:, :],
                                  ALU.pow).then_inc(x_rs, 1)

            def body(i, u, front, mid, tail, late, ld):
                v = 1 - u
                if front and not opening(i):
                    ln_pool(eng, L, i + 1, v)
                elif closing(i) and proj:
                    ln_pool(eng, L + 1, 0, v)
                if mid:
                    spread(i, u, ((1, 1),))
                if tail and proj:
                    eng.wait_ge(a_wo, given(a_wo) + i - 2)
                    eng.wait_ge(s_xdone, given(s_xdone) + base + i - 2)
                    eng.tensor_tensor(xb[:, v, :], X[:, i - 1, :], bproj[:, :], ALU.add).then_inc(a_xb, 1)
                if late and not proj:
                    next_scale(i - 2, u)
                if front:
                    spread(i + 1, v, ((0, 0), (0, 1), (1, 0)))

            long_pipeline(eng, body)


def quantised_ffn(nc, ctx, env):
    g = env
    sb, sem, ps, X = g["sb"], g["sem"], g["ps"], g["X"]
    ln_dve, ln_dve2, ln_pool = g["ln_dve"], g["ln_dve2"], g["ln_pool"]
    ln_h, ln_T, s_xdone, h, identb = g["ln_h"], g["ln_T"], g["s_xdone"], g["h"], g["identb"]
    wg, wu, wd = g["wq3"]
    wsc = g["wsc"]
    L = 2
    base = NPAIR * L
    am = sb("am3", [P, 2, 1]); ac = sb("ac3", [P, 2, 1]); sc = sb("sc3", [P, 2, 1]); dq = sb("dq3", [P, 2, 3])
    am2 = sb("am32", [P, 2, 1]); ac2 = sb("ac32", [P, 2, 1]); sc2 = sb("sc32", [P, 2, 1]); dq2 = sb("dq32", [P, 2, 1])
    r = sb("r3", [P, 2, DIM]); xq = sb("xq3", [P, 2, DIM], BF16); xqT = sb("xqT3", [P, 2, HALF, P], BF16)
    sg = sb("sg3", [P, 2, INNER]); a = sb("a3", [P, 2, INNER]); ar = sb("ar3", [P, 2, INNER])
    aq = sb("aq3", [P, 2, INNER], BF16); aqT = sb("aqT3", [P, 2, 8, P], BF16)
    rnd = sb("rnd3", [P, 2])
    GB, UB = [0, 2], [1, 3]
    XT, AT, OB = 4, 5, 6
    n = "f_"
    f_am = sem(n + "am"); f_ac = sem(n + "ac"); f_sc = sem(n + "sc"); f_dq = sem(n + "dq", 5, "vector")
    f_r = sem(n + "r", 2, "gpsimd"); f_xq = sem(n + "xq"); f_xt = sem(n + "xt", 2, "tensor"); f_xte = sem(n + "xte")
    f_g = sem(n + "g", 3, "tensor"); f_u = sem(n + "u"); f_sg = sem(n + "sg", 3, "scalar"); f_a = sem(n + "a", 3, "vector")
    f_am2 = sem(n + "am2"); f_ac2 = sem(n + "ac2"); f_sc2 = sem(n + "sc2"); f_dq2 = sem(n + "dq2")
    f_ar = sem(n + "ar", 3, "scalar"); f_aq = sem(n + "aq", 3, "scalar"); f_at = sem(n + "at", 3, "tensor")
    f_ate = sem(n + "ate", 2, "scalar"); f_o = sem(n + "o", 3, "tensor"); f_rnd = sem(n + "rnd")

    with nc.Block() as block:
        @block.tensor
        def _(eng):
            g["give"](eng, "tensor")

            def xt(i, u):
                eng.wait_ge(f_xq, i + 1)
                if not known(i, 1):
                    eng.wait_ge(f_xte, i)
                out = ps[:, XT, :].bitcast(BF16)
                for c in range(HALF):
                    ins = eng.transpose(out[:, c * P:(c + 1) * P], xq[:, u, c * P:(c + 1) * P], identb[:, :])
                ins.then_inc(f_xt, 1)

            def gu(i, u):
                eng.wait_ge(f_xte, i + 1)
                for q in range(2):
                    eng.wait_ge(f_sg, given(f_sg) + 2 * (i - 1) + q + 1)
                    for c in range(HALF):
                        ins = eng.matmul(ps[:, GB[q], :], xqT[:, u, c, :], wg[:, c, q * 512:(q + 1) * 512],
                                         start=(c == 0), stop=(c == 1))
                    ins.then_inc(f_g, 1)
                    eng.wait_ge(f_a, given(f_a) + 2 * (i - 1) + q + 1)
                    for c in range(HALF):
                        ins = eng.matmul(ps[:, UB[q], :], xqT[:, u, c, :], wu[:, c, q * 512:(q + 1) * 512],
                                         start=(c == 0), stop=(c == 1))
                    ins.then_inc(f_u, 1)

            def at(t, u):
                eng.wait_ge(f_aq, given(f_aq) + t + 1)
                eng.wait_ge(f_ate, given(f_ate) + t)
                out = ps[:, AT, :].bitcast(BF16)
                for c in range(8):
                    ins = eng.transpose(out[:, c * P:(c + 1) * P], aq[:, u, c * P:(c + 1) * P], identb[:, :])
                ins.then_inc(f_at, 1)

            def down(t, u):
                eng.wait_ge(f_ate, given(f_ate) + t + 1)
                eng.wait_ge(s_xdone, given(s_xdone) + base + t)
                for c in range(8):
                    ins = eng.matmul(ps[:, OB, 0:DIM], aqT[:, u, c, :], wd[:, c, :], start=(c == 0), stop=(c == 7))
                ins.then_inc(f_o, 1)

            def body(i, u, front, mid, tail, ld):
                v = 1 - u
                if front:
                    xt(i + 1, v)
                if tail:
                    at(i - 1, v)
                if front:
                    gu(i + 1, v)
                if tail:
                    down(i - 1, v)

            pipeline(eng, body)

        @block.vector
        def _(eng):
            g["give"](eng, "vector")
            eng.memset(rnd[:, 0:1], ROUND).then_inc(f_rnd, 1)
            eng.memset(rnd[:, 1:2], -ROUND).then_inc(f_rnd, 1)

            def front1(i, u):
                eng.wait_ge(ln_h, base + i + 1)
                eng.tensor_reduce(am[:, u, :], h[:, u, :], AX.X, ALU.max,
                                  apply_absolute_value=True).then_inc(f_am, 1)
                eng.wait_ge(f_am, i + 1)
                eng.tensor_scalar(ac[:, u, :], am[:, u, :], 1e-5, 1.0 / 127.0, ALU.max, ALU.mult).then_inc(f_ac, 1)
                eng.wait_ge(f_ac, i + 1)
                eng.reciprocal(sc[:, u, :], ac[:, u, :]).then_inc(f_sc, 1)
                eng.wait_ge(f_sg, given(f_sg) + 2 * (i - 1))
                eng.tensor_scalar(dq[:, u, :], wsc[:, :], ac[:, u, :], None, ALU.mult).then_inc(f_dq, 1)

            def mul(i, u, q):
                eng.wait_ge(f_sg, given(f_sg) + 2 * i + q + 1)
                eng.wait_ge(f_u, 2 * i + q + 1)
                eng.wait_ge(f_dq, given(f_dq) + i + 1)
                eng.wait_ge(f_ar, given(f_ar) + i - 1)
                eng.scalar_tensor_tensor(out=a[:, u, q * 512:(q + 1) * 512], in0=ps[:, UB[q], :],
                                         scalar=dq[:, u, 1:2], in1=sg[:, u, q * 512:(q + 1) * 512],
                                         op0=ALU.mult, op1=ALU.mult).then_inc(f_a, 1)

            def amax2(i, u):
                eng.wait_ge(f_a, given(f_a) + 2 * i + 2)
                eng.tensor_reduce(am2[:, u, :], a[:, u, :], AX.X, ALU.max,
                                  apply_absolute_value=True).then_inc(f_am2, 1)
                eng.wait_ge(f_am2, i + 1)
                eng.tensor_scalar(ac2[:, u, :], am2[:, u, :], 1e-5, 1.0 / 127.0, ALU.max, ALU.mult).then_inc(f_ac2, 1)
                eng.wait_ge(f_ac2, i + 1)
                eng.reciprocal(sc2[:, u, :], ac2[:, u, :]).then_inc(f_sc2, 1)
                eng.tensor_scalar(dq2[:, u, :], wsc[:, 2:3], ac2[:, u, :], None, ALU.mult).then_inc(f_dq2, 1)

            def add_x(t, u):
                eng.wait_ge(f_o, given(f_o) + t + 1)
                eng.wait_ge(f_dq2, t + 1)
                eng.scalar_tensor_tensor(out=X[:, t, :], in0=ps[:, OB, 0:DIM], scalar=dq2[:, u, :],
                                         in1=X[:, t, :], op0=ALU.mult, op1=ALU.add).then_inc(s_xdone, 1)

            def body(i, u, front, mid, tail, late, ld):
                v = 1 - u
                if opening(i):
                    ln_dve(eng, L, 1, 1)
                if (front and not opening(i)) or closing(i):
                    eng.wait_ge(f_r, given(f_r) + i)
                if front and not opening(i):
                    ln_dve2(eng, L, i + 1, v, f_r, 0)
                elif closing(i):
                    ln_dve2(eng, L + 1, 0, v)
                if front:
                    front1(i + 1, v)
                if mid:
                    mul(i, u, 0)
                    mul(i, u, 1)
                if ahead(i):
                    ln_dve(eng, L, i + 2, u, (lambda: add_x(i - 2, u)) if late else None)
                elif isinstance(i, int) and i == NPAIR - 2:
                    ln_dve(eng, L + 1, 0, u, lambda: add_x(i - 2, u))
                elif late:
                    add_x(i - 2, u)
                if mid:
                    amax2(i, u)

            long_pipeline(eng, body)

        @block.scalar
        def _(eng):
            g["give"](eng, "scalar")
            eng.wait_ge(f_rnd, 2)

            def silu(i, u, q):
                eng.wait_ge(f_g, given(f_g) + 2 * i + q + 1)
                eng.wait_ge(f_dq, given(f_dq) + i + 1)
                eng.wait_ge(f_a, given(f_a) + 2 * (i - 1))
                eng.activation(sg[:, u, q * 512:(q + 1) * 512], ps[:, GB[q], :], ACT.Silu,
                               scale=dq[:, u, 0:1]).then_inc(f_sg, 1)

            def round2(i, u):
                eng.wait_ge(f_sc2, i + 1)
                eng.wait_ge(f_aq, given(f_aq) + i - 1)
                eng.activation(ar[:, u, :], a[:, u, :], ACT.Identity, bias=rnd[:, 0:1],
                               scale=sc2[:, u, :]).then_inc(f_ar, 1)
                eng.wait_ge(f_ar, given(f_ar) + i + 1)
                eng.wait_ge(f_at, given(f_at) + i - 1)
                eng.activation(aq[:, u, :], ar[:, u, :], ACT.Identity, bias=rnd[:, 1:2]).then_inc(f_aq, 1)

            def xt_out(i, u):
                eng.wait_ge(f_xt, given(f_xt) + i + 1)
                eng.wait_ge(f_g, given(f_g) + 2 * (i - 1))
                if not known(i, 2):
                    eng.wait_ge(f_u, 2 * (i - 1))
                eng.activation(xqT[:, u, :, :], ps[:, XT, :].bitcast(BF16)[:, 0:DIM], ACT.Copy).then_inc(f_xte, 1)

            def at_out(t, u):
                eng.wait_ge(f_at, given(f_at) + t + 1)
                eng.wait_ge(f_o, given(f_o) + t - 1)
                eng.activation(aqT[:, u, :, :], ps[:, AT, :].bitcast(BF16), ACT.Copy).then_inc(f_ate, 1)

            def body(i, u, front, mid, tail, ld):
                v = 1 - u
                if front:
                    xt_out(i + 1, v)
                if tail:
                    at_out(i - 1, v)
                if front:
                    silu(i + 1, v, 0)
                    silu(i + 1, v, 1)
                if mid:
                    round2(i, u)

            pipeline(eng, body)

        @block.gpsimd
        def _(eng):
            g["give"](eng, "gpsimd")

            def round1(i, u):
                eng.wait_ge(f_sc, i + 1)
                eng.nop(nofuse=True)
                eng.tensor_scalar(r[:, u, :], h[:, u, :], sc[:, u, :], ROUND, ALU.mult, ALU.add).then_inc(f_r, 1)
                eng.wait_ge(f_r, given(f_r) + i + 1)
                eng.wait_ge(f_xt, given(f_xt) + i - 1)
                eng.nop(nofuse=True)
                eng.tensor_scalar(xq[:, u, :], r[:, u, :], ROUND, None, ALU.subtract).then_inc(f_xq, 1)

            def body(i, u, front, mid, tail, ld):
                v = 1 - u
                if front and not opening(i):
                    ln_pool(eng, L, i + 1, v)
                elif closing(i):
                    ln_pool(eng, L + 1, 0, v)
                if front:
                    round1(i + 1, v)

            pipeline(eng, body)


def cross_single(nc, ctx, env):
    g = env
    sb, sem, ps, X, io = g["sb"], g["sem"], g["ps"], g["X"], g["io"]
    ident, hT = g["ident"], g["hT"]
    ln_dve, ln_dve2, ln_pool, ln_pe, ln_act = (g[k] for k in ("ln_dve", "ln_dve2", "ln_pool", "ln_pe", "ln_act"))
    ln_hT, s_xdone = g["ln_hT"], g["s_xdone"]
    wq, wk, wv, bqk, bv = g["wq4"], g["wk4"], g["wv4"], g["bqk4"], g["bv"][4]
    cx = sb("cx", [P, 2, 2 * CTX])
    cxh = sb("cxh", [P, 2, 2 * CTX], F32R); cxl = sb("cxl", [P, 2, 2 * CTX], F32R)
    wh = {n: sb(f"w{n}4h", [P, DIM], F32R) for n in "kv"}; wl = {n: sb(f"w{n}4l", [P, DIM], F32R) for n in "kv"}
    QT = sb("QT4", [P, 2, HALF, P])
    KT = sb("KT4", [P, 2, HALF, 2 * CTX])
    V = sb("V4", [P, 2, 4, DIM])
    Pr = sb("Pr4", [P, 2, CTX]); PT = sb("PT4", [P, 2, 2, P])
    mx = sb("mx4", [P, 2, 1]); den = sb("den4", [P, 2, 1]); rd = sb("rd4", [P, 2, 1])
    L = 3
    base = NPAIR * L
    SB, TB, LQ, OB = [0, 1], 2, 3, [4, 5]
    FA, FB = 6, 7
    n = "d_"
    d_ld = [sem(n + "ld0"), sem(n + "ld1")]
    d_q = sem(n + "q"); d_qe = sem(n + "qe", 3, "scalar"); d_k = sem(n + "k", 3, "tensor"); d_ke = sem(n + "ke", 3, "scalar")
    d_v = sem(n + "v", 3, "tensor"); d_ve = sem(n + "ve", 2, "vector"); d_s = sem(n + "s", 2, "tensor")
    d_max = sem(n + "max"); d_exp = sem(n + "exp", 2, "scalar"); d_t = sem(n + "t", 2, "tensor")
    d_w = sem(n + "w"); d_cxh = sem(n + "cxh"); d_cxl = sem(n + "cxl", 2, "gpsimd")
    d_te = sem(n + "te", 2, "scalar"); d_o = sem(n + "o", 2, "tensor"); d_rd = sem(n + "rd", 2, "vector")

    with nc.Block() as block:
        @block.sync
        def _(sp):
            ctxT = io["ctxT"].rearrange("p (n c) -> p n c", c=2 * CTX)

            def load(i, u):
                sp.wait_ge(d_cxl, given(d_cxl) + i - 1)
                sp.dma_start(cx[:, u, :], ctxT[:, i, :]).then_inc(d_ld[u], 16)

            with sp.Fori(0, NPAIR // 2) as j:
                load(2 * j, 0)
                load(2 * j + 1, 1)

        @block.tensor
        def _(eng):
            g["give"](eng, "tensor")
            def qproj(i, u):
                eng.wait_ge(ln_hT, g["lnt"][L] + i + 1)
                for m in range(HALF):
                    for c in range(2):
                        ins = eng.matmul(ps[:, LQ, m * P:(m + 1) * P], wq[:, c, m * P:(m + 1) * P],
                                         hT[:, u, c, :], start=(c == 0), stop=(c == 1))
                ins.then_inc(d_q, 1)

            def kproj(i, u, m, ld):
                if m == 0:
                    eng.wait_ge(d_ve, given(d_ve) + 2 * i - 1)
                    eng.wait_ge(d_cxl, given(d_cxl) + i + 1)
                    if known(i, 1):
                        eng.wait_ge(d_w, 4)
                else:
                    eng.wait_ge(d_ve, given(d_ve) + 2 * i)
                out, w = ps[:, (FA, FB)[m], :], slice(m * P, (m + 1) * P)
                eng.matmul(out, wh["k"][:, w], cxh[:, u, :], start=True, stop=False)
                eng.matmul(out, wh["k"][:, w], cxl[:, u, :], start=False, stop=False)
                eng.matmul(out, wl["k"][:, w], cxh[:, u, :], start=False, stop=True).then_inc(d_k, 1)

            def vproj(i, u, m):
                eng.wait_ge(d_ke, given(d_ke) + 2 * i + m + 1)
                for t in range(2):
                    out = ps[:, (FA, FB)[m], t * DIM:(t + 1) * DIM]
                    c = slice((2 * m + t) * P, (2 * m + t + 1) * P)
                    eng.matmul(out, cxh[:, u, c], wh["v"][:, :], start=True, stop=False)
                    eng.matmul(out, cxl[:, u, c], wh["v"][:, :], start=False, stop=False)
                    ins = eng.matmul(out, cxh[:, u, c], wl["v"][:, :], start=False, stop=True)
                ins.then_inc(d_v, 1)

            def scores(i, u):
                eng.wait_ge(d_qe, given(d_qe) + 2 * i + 2)
                eng.wait_ge(d_ke, given(d_ke) + 2 * i + 2)
                eng.wait_ge(d_exp, given(d_exp) + i - 1)
                for b in range(2):
                    for c in range(HALF):
                        ins = eng.matmul(ps[64 * b:64 * b + 64, SB[u], 0:CTX], QT[:, u, c, 64 * b:64 * b + 64],
                                         KT[:, u, c, b * CTX:(b + 1) * CTX], start=(c == 0), stop=(c == 1),
                                         tile_position=(0, 64 * b))
                ins.then_inc(d_s, 1)

            def turn(i, u):
                eng.wait_ge(d_exp, given(d_exp) + i + 1)
                eng.wait_ge(d_te, given(d_te) + i)
                for kt in range(2):
                    ins = eng.transpose(ps[:, TB, kt * P:(kt + 1) * P], Pr[:, u, kt * P:(kt + 1) * P],
                                        ident[:, :])
                ins.then_inc(d_t, 1)

            def pv(i, u):
                eng.wait_ge(d_te, given(d_te) + i + 1)
                eng.wait_ge(d_ve, given(d_ve) + 2 * i + 2)
                eng.wait_ge(s_xdone, given(s_xdone) + base + i - 1)
                for b in range(2):
                    for kt in range(2):
                        ins = eng.matmul(ps[64 * b:64 * b + 64, OB[u], 0:DIM], PT[:, u, kt, 64 * b:64 * b + 64],
                                         V[:, u, 2 * b + kt, :], start=(kt == 0), stop=(kt == 1),
                                         tile_position=(0, 64 * b))
                ins.then_inc(d_o, 1)

            def body(i, u, front, mid, tail, ld):
                v = 1 - u
                if mid:
                    scores(i, u)
                if front:
                    kproj(i + 1, v, 0, ld)
                    kproj(i + 1, v, 1, ld)
                    eng.wait_ge(d_qe, given(d_qe) + 2 * i + 2)
                    ln_pe(eng, L, i + 1, v, LQ)
                if mid:
                    turn(i, u)
                if front:
                    vproj(i + 1, v, 0)
                    qproj(i + 1, v)
                if mid:
                    pv(i, u)
                if front:
                    vproj(i + 1, v, 1)

            pipeline(eng, body)

        @block.vector
        def _(eng):
            g["give"](eng, "vector")
            def rowmax(i, u):
                eng.wait_ge(d_s, given(d_s) + i + 1)
                eng.wait_ge(d_exp, given(d_exp) + i - 1)
                eng.tensor_reduce(mx[:, u, :], ps[:, SB[u], 0:CTX], AX.X, ALU.max, negate=True).then_inc(d_max, 1)

            def v_out(i, u, m):
                eng.wait_ge(d_v, given(d_v) + 2 * i + m + 1)
                eng.wait_ge(d_o, given(d_o) + i - 1)
                eng.tensor_tensor(V[:, u, 2 * m:2 * m + 2, :], ps[:, (FA, FB)[m], :].rearrange("p (t n) -> p t n", t=2),
                                  bv[:, :].unsqueeze(1).to_broadcast([P, 2, DIM]), ALU.add).then_inc(d_ve, 1)

            def add_x(i, u):
                eng.wait_ge(d_exp, given(d_exp) + i + 1)
                eng.reciprocal(rd[:, u, :], den[:, u, :]).then_inc(d_rd, 1)
                eng.wait_ge(d_rd, given(d_rd) + i + 1)
                eng.wait_ge(d_o, given(d_o) + i + 1)
                eng.scalar_tensor_tensor(out=X[:, i, :], in0=ps[:, OB[u], 0:DIM], scalar=rd[:, u, :],
                                         in1=X[:, i, :], op0=ALU.mult, op1=ALU.add).then_inc(s_xdone, 1)

            def body(i, u, front, mid, tail, late, ld):
                v = 1 - u
                if opening(i):
                    ln_dve(eng, L, 1, 1)
                if mid:
                    rowmax(i, u)
                if front and not opening(i):
                    ln_dve2(eng, L, i + 1, v)
                elif closing(i):
                    ln_dve2(eng, L + 1, 0, v)
                if isinstance(i, int) and i == NPAIR - 2:
                    ln_dve(eng, L + 1, 0, u)
                if ahead(i):
                    ln_dve(eng, L, i + 2, u)
                if front:
                    v_out(i + 1, v, 0)
                if mid:
                    add_x(i, u)
                if front:
                    v_out(i + 1, v, 1)

            long_pipeline(eng, body)

        @block.scalar
        def _(eng):
            g["give"](eng, "scalar")
            def q_out(i, u):
                eng.wait_ge(d_q, i + 1)
                eng.wait_ge(d_s, given(d_s) + i - 1)
                for m in range(HALF):
                    eng.activation(QT[:, u, m, :], ps[:, LQ, m * P:(m + 1) * P], ACT.Identity,
                                   bias=bqk[:, m:m + 1]).then_inc(d_qe, 1)

            def k_out(i, u, m):
                eng.wait_ge(d_k, given(d_k) + 2 * i + m + 1)
                eng.activation(KT[:, u, m, :], ps[:, (FA, FB)[m], :], ACT.Identity,
                               bias=bqk[:, 2 + m:3 + m]).then_inc(d_ke, 1)

            def cx_high(i, u, ld):
                eng.wait_ge(d_ld[u], 16 * ld)
                eng.wait_ge(d_v, given(d_v) + 2 * i - 2)
                eng.activation(cxh[:, u, :], cx[:, u, :], ACT.Copy).then_inc(d_cxh, 1)

            def exps(i, u):
                eng.wait_ge(d_max, i + 1)
                eng.wait_ge(d_t, given(d_t) + i - 1)
                eng.wait_ge(d_rd, given(d_rd) + i - 1)
                eng.activation(Pr[:, u, :], ps[:, SB[u], 0:CTX], ACT.Exp, bias=mx[:, u, :],
                               accum_out=den[:, u, :]).then_inc(d_exp, 1)

            def turned(i, u):
                eng.wait_ge(d_t, given(d_t) + i + 1)
                eng.wait_ge(d_o, given(d_o) + i - 1)
                eng.activation(PT[:, u, :, :], ps[:, TB, 0:DIM], ACT.Copy).then_inc(d_te, 1)

            def body(i, u, front, mid, tail, late, ld):
                v = 1 - u
                if known(i, 0):
                    cx_high(0, 0, 1)
                    cx_high(1, 1, 1)
                if ahead(i):
                    cx_high(i + 2, u, ld + 1 - u)
                if mid:
                    exps(i, u)
                if front:
                    k_out(i + 1, v, 0)
                    k_out(i + 1, v, 1)
                    if not known(i, 1):
                        eng.wait_ge(d_q, i)
                    ln_act(eng, L, i + 1, v, LQ)
                if mid:
                    turned(i, u)
                if front:
                    q_out(i + 1, v)

            for n, w in (("k", wk), ("v", wv)):
                eng.activation(wh[n][:, :], w[:, :], ACT.Copy).then_inc(d_w, 1)
            long_pipeline(eng, body)

        @block.gpsimd
        def _(eng):
            g["give"](eng, "gpsimd")
            eng.wait_ge(d_w, 2)
            for n, w in (("k", wk), ("v", wv)):
                eng.tensor_tensor(wl[n][:, :], w[:, :], wh[n][:, :].bitcast(F32), ALU.subtract).then_inc(d_w, 1)

            def cx_low(i, u):
                eng.wait_ge(d_cxh, i + 1)
                eng.wait_ge(d_v, given(d_v) + 2 * i - 2)
                eng.tensor_tensor(cxl[:, u, :], cx[:, u, :], cxh[:, u, :].bitcast(F32), ALU.subtract).then_inc(d_cxl, 1)

            def body(i, u, front, mid, tail, late, ld):
                if front and not opening(i):
                    ln_pool(eng, L, i + 1, 1 - u)
                elif closing(i):
                    ln_pool(eng, L + 1, 0, 1 - u)
                if known(i, 0):
                    cx_low(0, 0)
                    cx_low(1, 1)
                if ahead(i):
                    cx_low(i + 2, u)

            long_pipeline(eng, body)


def router(nc, ctx, env):
    g = env
    sb, sem, ps, X, io = g["sb"], g["sem"], g["ps"], g["X"], g["io"]
    ident, mean, rs = g["ident"], g["mean6"], g["rs6"]
    wr, br = g["wr6"], g["br6"]
    g["Hh"] = Hh = sb("Hh", [P, HALF, NPAIR, P], F32R)
    g["Hl"] = Hl = sb("Hl", [P, HALF, NPAIR, P], F32R)
    g["raw6"] = raw = sb("raw6", [P, 2, 768])
    NG, GE, TOPG = 4, EXPERTS // 4, 2
    QUAD, TWO = 4, 2
    hn = sb("hn6", [P, NPAIR, DIM]); hT = sb("hT6", [P, HALF, NPAIR, P])
    W = sb("W6", [P, NPAIR, NE])
    score = sb("score6", [P, NPAIR, EXPERTS])
    choice = sb("choice6", [P, NPAIR, EXPERTS])
    gm = sb("gm6", [P, NPAIR, NG, 8])
    gs = sb("gs6", [P, NPAIR, 10])
    g8 = sb("g86", [P, NPAIR, 8]); gr = sb("gr6", [P, NPAIR, 10]); gsel = sb("gsel6", [P, NPAIR, NG])
    msk = sb("msk6", [P, NPAIR, EXPERTS]); m8 = sb("m86", [P, NPAIR, 8]); mr = sb("mr6", [P, NPAIR, EXPERTS])
    tot = sb("tot6", [P, NPAIR, 1])
    g["WT6"] = WT = sb("WT6", [NE, TOK])
    LT_s = WT[0:EXPERTS, :]
    TRB, LT, LB = [0, 1, 2, 3], [5, 6], [4, 7]
    n = "r_"
    ln_h = g["ln_h"]
    before = 5 * NPAIR
    r_T = sem(n + "T"); r_ht = sem(n + "ht", 5, "scalar")
    r_l = sem(n + "l"); r_hl = sem(n + "hl"); r_lt = sem(n + "lt", 2, "scalar"); r_lb = sem(n + "lb"); r_sc = sem(n + "sc")
    r_c = sem(n + "c"); r_w = sem(n + "w"); r_t = sem(n + "t"); r_wt = sem(n + "wt")
    g["m_ld"] = m_ld = [sem("m_ld0"), sem("m_ld1")]
    steps = NPAIR // TWO
    done = [2]
    ROUTES = 2
    HP = NPAIR // ROUTES

    def two(j, b):
        return bass.ds(len(TRB) * TWO * j + TWO * b, TWO)

    def bank(b):
        return ps[:, TRB[b], :].rearrange("p (n c t) -> p c n t", n=TWO, c=HALF)

    def load_first(sp):
        for e in range(2):
            sp.dma_start(raw[:, e, :], io["ew6"][e, :, :]).then_inc(m_ld[e], 16)

    def transposes_logits(eng):
        def logits(k):
            eng.wait_ge(r_ht, given(r_ht) + k + 1)
            eng.wait_ge(r_lt, given(r_lt) + k - 1)
            for c in range(HALF):
                ins = eng.matmul(ps[0:EXPERTS, LT[k % 2], 0:TWO * P], wr[:, c, :],
                                 hT[:, c, TWO * k:TWO * k + TWO, :].rearrange("p n t -> p (n t)"),
                                 start=(c == 0), stop=(c == 1))
            ins.then_inc(r_l, 1)

        def logits_back(k):
            eng.wait_ge(r_lt, given(r_lt) + k + 1)
            for t in range(TWO * k, TWO * (k + 1)):
                ins = eng.transpose(ps[:, LB[t // HP], (t % HP) * EXPERTS:(t % HP + 1) * EXPERTS], LT_s[:, t * P:(t + 1) * P],
                                    ident[0:EXPERTS, 0:EXPERTS])
            if k % (steps // ROUTES) == steps // ROUTES - 1:
                ins.then_inc(r_lb, 1)

        for k in range(steps):
            b = k % len(TRB)
            eng.wait_ge(ln_h, before + TWO * k + TWO)
            eng.wait_ge(r_ht, given(r_ht) + k - 3)
            for q in range(TWO):
                for c in range(HALF):
                    at = (q * HALF + c) * P
                    ins = eng.transpose(ps[:, TRB[b], at:at + P],
                                        hn[:, TWO * k + q, c * P:(c + 1) * P], ident[:, :])
            ins.then_inc(r_T, 1)
            if k:
                logits(k - 1)
            if k > 1:
                logits_back(k - 2)
        logits(steps - 1)
        logits_back(steps - 2)
        logits_back(steps - 1)

    def weights_turn(eng, half):
        eng.wait_ge(r_w, half + 1)
        eng.wait_ge(r_sc, ROUTES)
        for t in range(HP):
            ins = eng.transpose(ps[0:NE, 4 + t // 4, (t % 4) * P:(t % 4 + 1) * P], W[:, half * HP + t, :],
                                ident[:, :])
        ins.then_inc(r_t, 1)

    def copies_scores(eng):
        def logits_out(k):
            eng.wait_ge(r_l, k + 1)
            eng.activation(LT_s[:, TWO * P * k:TWO * P * (k + 1)], ps[0:EXPERTS, LT[k % 2], 0:TWO * P],
                           ACT.Copy).then_inc(r_lt, 1)

        def scores(half):
            eng.wait_ge(r_lb, half + 1)
            eng.activation(score[:, half * HP:(half + 1) * HP, :].rearrange("p t e -> p (t e)"),
                           ps[:, LB[half], 0:HP * EXPERTS], ACT.Sigmoid).then_inc(r_sc, 1)

        for k in range(steps):
            eng.wait_ge(r_T, k + 1)
            at = slice(TWO * k, TWO * (k + 1))
            eng.activation(Hh[:, :, at, :], bank(k % len(TRB)), ACT.Copy)
            eng.activation(hT[:, :, at, :], bank(k % len(TRB)), ACT.Copy).then_inc(r_ht, 1)
            if k:
                logits_out(k - 1)
            if k == steps // 2 + 1:
                scores(0)
        logits_out(steps - 1)
        scores(1)

    def weights_out(eng, half):
        eng.wait_ge(r_t, half + 1)
        eng.activation(WT[:, half * HP * P:(half + 1) * HP * P].rearrange("e (b n) -> e b n", b=2),
                       ps[0:NE, 4:6, :], ACT.Copy).then_inc(r_wt, 1)

    def rows(eng):
        eng.memset(gs[:, :, :], NEG).then_inc(r_c, 1)
        eng.memset(W[:, :, 0:NE - EXPERTS], 1.0).then_inc(r_c, 1)
        with eng.Fori(0, NPAIR // QUAD) as j:
            for q in range(QUAD):
                t = QUAD * j + q
                eng.tensor_scalar(hn[:, t, :], X[:, t, :], mean[:, bass.ds(t, 1)], rs[:, bass.ds(t, 1)],
                                  ALU.subtract, ALU.mult).then_inc(ln_h, 1)

    def routing(eng, half, parts):
        T = slice(half * HP, (half + 1) * HP)

        def step(ins):
            ins.then_inc(r_c, 1)
            done[0] += 1
            eng.wait_ge(r_c, done[0])

        if 0 in parts:
            eng.wait_ge(r_sc, half + 1)
            step(eng.tensor_tensor(choice[:, T, :], score[:, T, :],
                                   br[:, :].unsqueeze(1).to_broadcast([P, HP, EXPERTS]), ALU.add))
            for t in range(half * HP, (half + 1) * HP):
                for q in range(NG):
                    ins = eng.max(gm[:, t, q, :], choice[:, t, q * GE:(q + 1) * GE])
            step(ins)
            step(eng.tensor_tensor(gs[:, T, 0:NG], gm[:, T, :, 0], gm[:, T, :, 1], ALU.add))
        if 1 in parts:
            for t in range(half * HP, (half + 1) * HP):
                ins = eng.max(g8[:, t, :], gs[:, t, :])
            step(ins)
            step(eng.memset(g8[:, T, TOPG:8], NEG))
            for t in range(half * HP, (half + 1) * HP):
                ins = eng.match_replace(gr[:, t, :], g8[:, t, :], gs[:, t, :], -NEG)
            step(ins)
            step(eng.tensor_tensor(gsel[:, T, :], gr[:, T, 0:NG], gs[:, T, 0:NG], ALU.not_equal))
            step(eng.tensor_tensor(msk[:, T, :].rearrange("p t (a b) -> p (t a) b", b=GE),
                                   choice[:, T, :].rearrange("p t (a b) -> p (t a) b", b=GE),
                                   gsel[:, T, :].rearrange("p t a -> p (t a)").unsqueeze(2)
                                   .to_broadcast([P, HP * NG, GE]), ALU.mult))
        if 2 in parts:
            for t in range(half * HP, (half + 1) * HP):
                ins = eng.max(m8[:, t, :], msk[:, t, :])
            step(ins)
            for t in range(half * HP, (half + 1) * HP):
                ins = eng.match_replace(mr[:, t, :], m8[:, t, :], msk[:, t, :], NEG)
            step(ins)
        if 3 in parts:
            step(eng.tensor_tensor(mr[:, T, :], mr[:, T, :], msk[:, T, :], ALU.not_equal))
            step(eng.tensor_tensor(msk[:, T, :], mr[:, T, :], score[:, T, :], ALU.mult))
            step(eng.tensor_reduce(tot[:, T, :], msk[:, T, :], AX.X, ALU.add))
            step(eng.tensor_scalar(tot[:, T, :], tot[:, T, :], 1e-20, None, ALU.add))
            step(eng.reciprocal(tot[:, T, :], tot[:, T, :]))
            step(eng.tensor_scalar(tot[:, T, :], tot[:, T, :], 2.5, None, ALU.mult))
            eng.tensor_tensor(W[:, T, NE - EXPERTS:NE], msk[:, T, :],
                              tot[:, T, :].to_broadcast([P, HP, EXPERTS]), ALU.mult).then_inc(r_w, 1)

    def low_halves(eng):
        for k in range(steps):
            at = slice(TWO * k, TWO * (k + 1))
            eng.wait_ge(r_ht, given(r_ht) + k + 1)
            eng.tensor_tensor(Hl[:, :, at, :], hT[:, :, at, :], Hh[:, :, at, :].bitcast(F32),
                              ALU.subtract).then_inc(r_hl, 1)

    def ready(eng):
        eng.wait_ge(r_ht, given(r_ht) + steps)
        eng.wait_ge(r_hl, steps)

    g["route"] = dict(load_first=load_first, transposes_logits=transposes_logits, weights_turn=weights_turn,
                      copies_scores=copies_scores, weights_out=weights_out, low_halves=low_halves, ready=ready,
                      rows=rows, routing=routing, r_wt=r_wt)


def experts(nc, ctx, env):
    g = env
    sb, sem, ps, X, io, out = g["sb"], g["sem"], g["ps"], g["X"], g["io"], g["out"]
    ident, Hh, Hl, dram = g["ident"], g["Hh"], g["Hl"], g["wdram"]
    SG = 2
    UT = 512
    raw, WT, route = g["raw6"], g["WT6"], g["route"]
    wh = sb("wh6", [P, 2, 768], F32R); wl = sb("wl6", [P, 2, 768], F32R)
    wb = sb("wb6", [P, 2, 2 * UT])
    sg = sb("sg6", [P, 2, UT]); sw = sb("sw6", [P, 2, UT]); a = sb("a6", [P, 2, UT])
    ah = sb("ah6", [P, 2, UT], F32R); al = sb("al6", [P, 2, UT], F32R)
    OT = sb("OT6", [P, 4, UT])
    GB, UB, OB = [0, 1], [2, 3], [[4, 5], [6, 7]]
    GU, DN = slice(0, 512), slice(512, 768)
    n = "m_"
    r_dram = sem("r_dram"); m_one = sem(n + "one")
    m_ld = g["m_ld"]; m_wb = [sem(n + "wb0"), sem(n + "wb1")]
    m_hg = sem(n + "hg"); m_lg = sem(n + "lg", 2, "vector"); m_hd = sem(n + "hd"); m_ld_ = sem(n + "lowd", 2, "vector")
    m_g = sem(n + "g", 5, "tensor"); m_u = sem(n + "u", 5, "tensor"); m_d = sem(n + "d", 5, "tensor")
    m_sg = sem(n + "sg", 3, "scalar"); m_sw = sem(n + "sw", 3, "gpsimd"); m_a = sem(n + "a", 3, "vector")
    m_ah = sem(n + "ah", 3, "scalar"); m_al = sem(n + "al", 3, "vector")
    m_ot = sem(n + "ot"); m_tt = sem(n + "tt"); m_y = sem(n + "y")
    g["m_out"] = m_out = sem(n + "out")
    HhT = Hh[:, :, :, :].rearrange("p c n t -> p c (n t)")
    HlT = Hl[:, :, :, :].rearrange("p c n t -> p c (n t)")

    def rows(i, n):
        return out.rearrange("(n p) d -> p n d", p=P)[:, i:i + n, :]

    def each_expert(eng, s, body):
        k, q = NE * s, NE // 2 * s
        body(0, k, 0, q + 1)
        body(1, k + 1, 1, q + 1)
        with eng.Fori(0, NE // 2 - 2) as j:
            body(2 * j + 2, 2 * j + 2 + k, 0, j + 2 + q)
            body(2 * j + 3, 2 * j + 3 + k, 1, j + 2 + q)
        body(NE - 2, NE - 2 + k, 0, NE // 2 + q)
        body(NE - 1, NE - 1 + k, 1, NE // 2 + q)

    with nc.Block() as block:
        @block.sync
        def _(sp):
            route["load_first"](sp)
            sp.wait_ge(route["r_wt"], 1)
            sp.dma_start(dram[:, 0:2 * UT], WT[:, 0:2 * UT]).then_inc(r_dram, 16)
            sp.wait_ge(r_dram, 16)
            for s in range(SG):
                def body(e, E, u, ld):
                    if known(E, 2):
                        return
                    sp.wait_ge(m_lg, given(m_lg) + E - 1)
                    sp.wait_ge(m_ld_, given(m_ld_) + E - 1)
                    sp.dma_start(raw[:, u, :], io["ew6"][e, :, :]).then_inc(m_ld[u], 16)
                    sp.wait_ge(m_sw, given(m_sw) + 2 * (E - 1))
                    src = (dram[e:e + 1, 0:2 * UT] if known(e, 2) else
                           dram[bass.ds(e, 1), 2 * UT * s:2 * UT * (s + 1)])
                    sp.dma_start(wb[:, u, :], src.to_broadcast([P, 2 * UT])).then_inc(m_wb[u], 16)
                    if known(e, 2) and e == 1:
                        sp.wait_ge(route["r_wt"], 2)
                        sp.dma_start(dram[:, 2 * UT:4 * UT], WT[:, 2 * UT:4 * UT]).then_inc(r_dram, 16)
                        sp.wait_ge(r_dram, 32)

                each_expert(sp, s, body)
            for q in range(4):
                sp.wait_ge(m_y, 8 * (SG - 1) + 2 * (q + 1))
                sp.dma_start(rows(8 * (SG - 1) + 2 * q, 2), X[:, 8 * (SG - 1) + 2 * q:8 * (SG - 1) + 2 * q + 2, :]
                             ).then_inc(m_out, 16)
            sp.wait_ge(m_out, 16 * (SG - 1 + 4))

        @block.tensor
        def _(eng):
            g["give"](eng, "tensor")
            route["transposes_logits"](eng)
            route["ready"](eng)
            for s in range(SG):
                def gate_up(E, u, tt):
                    if tt == 0:
                        eng.wait_ge(m_hg, E + 1)
                        eng.wait_ge(m_lg, given(m_lg) + E + 1)
                    cols = slice(2 * UT * s + UT * tt, 2 * UT * s + UT * (tt + 1))
                    for bank, at, free, done in ((GB[tt], 0, m_sg, m_g), (UB[tt], 256, m_a, m_u)):
                        eng.wait_ge(free, given(free) + 2 * (E - 1) + tt + 1)
                        for c in range(HALF):
                            w = slice(at + c * P, at + (c + 1) * P)
                            eng.matmul(ps[:, bank, :], wh[:, u, w], HhT[:, c, cols], start=(c == 0), stop=False)
                            eng.matmul(ps[:, bank, :], wh[:, u, w], HlT[:, c, cols], start=False, stop=False)
                            ins = eng.matmul(ps[:, bank, :], wl[:, u, w], HhT[:, c, cols], start=False,
                                             stop=(c == 1))
                        ins.then_inc(done, 1)

                def down(E, u, tt, first, last):
                    eng.wait_ge(m_al, given(m_al) + 2 * E + tt + 1)
                    if tt == 0:
                        eng.wait_ge(m_ld_, given(m_ld_) + E + 1)
                    for m in range(2):
                        w = slice(512 + m * P, 512 + (m + 1) * P)
                        bank = ps[:, OB[m][tt], :]
                        eng.matmul(bank, wh[:, u, w], ah[:, tt, :], start=first, stop=False)
                        eng.matmul(bank, wh[:, u, w], al[:, tt, :], start=False, stop=False)
                        ins = eng.matmul(bank, wl[:, u, w], ah[:, tt, :], start=False, stop=last)
                    ins.then_inc(m_d, 1)

                def turn_back(s):
                    eng.wait_ge(m_ot, 4 * s + 4)
                    for q in range(8):
                        for m in range(2):
                            ins = eng.transpose(ps[:, 4 + q // 2, (q % 2) * DIM + m * P:(q % 2) * DIM + (m + 1) * P],
                                                OT[:, 2 * m + q // 4, (q % 4) * P:(q % 4 + 1) * P], ident[:, :])
                        if q % 2:
                            ins.then_inc(m_tt, 1)

                k = NE * s
                gate_up(k, 0, 0)
                if s:
                    turn_back(s - 1)
                    eng.wait_ge(m_y, 8 * s)
                    route["weights_turn"](eng, s)
                gate_up(k, 0, 1)
                if s == 0:
                    route["weights_turn"](eng, 0)
                for tt in range(2):
                    gate_up(k + 1, 1, tt)
                    eng.wait_ge(route["r_wt"], s + 1)
                    if s:
                        eng.wait_ge(m_y, 8 * s)
                    down(k, 0, tt, True, False)
                with eng.Fori(0, NE // 2 - 1) as j:
                    for tt in range(2):
                        gate_up(2 * j + 2 + k, 0, tt)
                        down(2 * j + 1 + k, 1, tt, False, False)
                    for tt in range(2):
                        gate_up(2 * j + 3 + k, 1, tt)
                        down(2 * j + 2 + k, 0, tt, False, False)
                down(k + NE - 1, 1, 0, False, True)
                down(k + NE - 1, 1, 1, False, True)
                if s == SG - 1:
                    turn_back(s)

        @block.scalar
        def _(eng):
            g["give"](eng, "scalar")
            for s in range(SG):
                def high_gu(E, u, ld):
                    eng.wait_ge(m_ld[u], 16 * ld)
                    eng.wait_ge(m_u, given(m_u) + 2 * (E - 1))
                    eng.activation(wh[:, u, GU], raw[:, u, GU], ACT.Copy).then_inc(m_hg, 1)

                def high_d(E, u):
                    eng.wait_ge(m_d, given(m_d) + 2 * (E - 1))
                    eng.activation(wh[:, u, DN], raw[:, u, DN], ACT.Copy).then_inc(m_hd, 1)

                def silu(E, tt):
                    eng.wait_ge(m_g, given(m_g) + 2 * E + tt + 1)
                    eng.wait_ge(m_sw, given(m_sw) + 2 * (E - 1) + tt + 1)
                    eng.activation(sg[:, tt, :], ps[:, GB[tt], :], ACT.Silu).then_inc(m_sg, 1)

                def high_a(E, tt):
                    eng.wait_ge(m_a, given(m_a) + 2 * E + tt + 1)
                    eng.wait_ge(m_d, given(m_d) + 2 * (E - 1) + tt + 1)
                    eng.activation(ah[:, tt, :], a[:, tt, :], ACT.Copy).then_inc(m_ah, 1)

                def body(e, E, u, ld):
                    high_d(E, u)
                    silu(E, 0)
                    if known(E, 1):
                        silu(E, 1)
                    if not (isinstance(E, int) and E == SG * NE - 1):
                        high_gu(E + 1, 1 - u, ld if u == 0 else ld + 1)
                    if known(e, 1):
                        route["weights_out"](eng, s)
                    high_a(E, 0)
                    if not known(E, 1):
                        silu(E, 1)
                    high_a(E, 1)
                    if s and known(e, 2) and e == 1:
                        eng.wait_ge(m_y, 8 * s)
                        eng.dma_start(rows(8 * (s - 1), 8), X[:, 8 * (s - 1):8 * s, :]).then_inc(m_out, 16)

                if s == 0:
                    high_gu(0, 0, 1)
                    route["copies_scores"](eng)
                each_expert(eng, s, body)
                eng.wait_ge(m_d, given(m_d) + 2 * NE * (s + 1))
                if s:
                    eng.wait_ge(m_tt, 4 * s)
                for m in range(2):
                    for tt in range(2):
                        eng.activation(OT[:, 2 * m + tt, :], ps[:, OB[m][tt], :], ACT.Copy).then_inc(m_ot, 1)

        @block.vector
        def _(eng):
            g["give"](eng, "vector")
            for s in range(SG):
                def low_gu(E, u):
                    eng.wait_ge(m_hg, E + 1)
                    eng.tensor_tensor(wl[:, u, GU], raw[:, u, GU], wh[:, u, GU].bitcast(F32),
                                      ALU.subtract).then_inc(m_lg, 1)

                def low_d(E, u):
                    eng.wait_ge(m_hd, E + 1)
                    eng.tensor_tensor(wl[:, u, DN], raw[:, u, DN], wh[:, u, DN].bitcast(F32),
                                      ALU.subtract).then_inc(m_ld_, 1)

                def mul(E, tt):
                    eng.wait_ge(m_sw, given(m_sw) + 2 * E + tt + 1)
                    eng.wait_ge(m_u, given(m_u) + 2 * E + tt + 1)
                    eng.wait_ge(m_ah, given(m_ah) + 2 * (E - 1) + tt + 1)
                    if known(E, 2) and E == 1:
                        eng.wait_ge(m_al, given(m_al) + tt + 1)
                    eng.tensor_tensor(a[:, tt, :], sw[:, tt, :], ps[:, UB[tt], :], ALU.mult).then_inc(m_a, 1)

                def low_a(E, tt):
                    eng.wait_ge(m_ah, given(m_ah) + 2 * E + tt + 1)
                    eng.tensor_tensor(al[:, tt, :], a[:, tt, :], ah[:, tt, :].bitcast(F32),
                                      ALU.subtract).then_inc(m_al, 1)

                def body(e, E, u, ld):
                    low_d(E, u)
                    mul(E, 0)
                    if not (isinstance(E, int) and E == SG * NE - 1):
                        low_gu(E + 1, 1 - u)
                    low_a(E, 0)
                    if known(E, 2):
                        route["routing"](eng, 1, [2 * E])
                    mul(E, 1)
                    low_a(E, 1)
                    if known(E, 2):
                        route["routing"](eng, 1, [2 * E + 1])

                if s == 0:
                    route["rows"](eng)
                    low_gu(0, 0)
                    route["routing"](eng, 0, range(4))

                each_expert(eng, s, body)
                for q in range(4):
                    eng.wait_ge(m_tt, 4 * s + q + 1)
                    for r in range(2):
                        i = 8 * s + 2 * q + r
                        eng.tensor_tensor(X[:, i, :], ps[:, 4 + q, r * DIM:(r + 1) * DIM], X[:, i, :],
                                          ALU.add).then_inc(m_y, 1)

        @block.gpsimd
        def _(eng):
            g["give"](eng, "gpsimd")
            eng.memset(wb[:, :, :], 1.0).then_inc(m_one, 1)
            eng.wait_ge(m_one, 1)
            route["low_halves"](eng)
            for s in range(SG):
                def body(e, E, u, ld):
                    if not known(E, 2):
                        eng.wait_ge(m_wb[u], 16 * (ld - 1))
                    for tt in range(2):
                        eng.wait_ge(m_sg, given(m_sg) + 2 * E + tt + 1)
                        eng.wait_ge(m_a, given(m_a) + 2 * (E - 1) + tt + 1)
                        eng.tensor_tensor(sw[:, tt, :], sg[:, tt, :], wb[:, u, tt * UT:(tt + 1) * UT],
                                          ALU.mult).then_inc(m_sw, 1)

                each_expert(eng, s, body)


def layout(inputs):
    import numpy as np
    a = {k: np.asarray(v) for k, v in inputs.items()}
    f = np.float32
    row = lambda v: np.ascontiguousarray(v.reshape(1, -1))
    cols = lambda v: np.ascontiguousarray(v.reshape(-1, P).T)
    c = np.arange(P)
    q = c % SEQ

    def part(name, at):
        gate, up, down = (a[f"L1_ffn_{name}_{k}"] for k in ("gate", "up", "down"))
        if name == "shared":
            gate, up, down = gate[None, at], up[None, at], down[None, :, at]
        up_ = lambda w: w.reshape(-1, EDIM, 2, P).transpose(0, 3, 2, 1).reshape(-1, P, 2 * EDIM)
        return np.concatenate([up_(gate), up_(up), down.transpose(0, 2, 1)], axis=2)

    ew = np.concatenate([part("shared", slice(0, EDIM)), part("shared", slice(EDIM, 2 * EDIM)),
                         part("expert", None)], axis=0)
    arrays = {
        "x": a["x"].reshape(TOK, DIM),
        "ctxT": a["ctx_512"].reshape(BATCH * CTX, CDIM).T,
        "wq1": a["L0_xattn_Wq"].T, "wkv1": a["L0_xattn_Wkv"].T, "wo1": a["L0_xattn_Wo"].T,
        "wqkv2": a["L0_attn_w_attn"], "bqk2": cols(a["L0_attn_b_attn"][:2 * DIM]),
        "bv2": row(a["L0_attn_b_attn"][2 * DIM:]),
        "wproj": a["L0_attn_w_proj"], "bproj": row(a["L0_attn_b_proj"]),
        "wg3": a["L0_ffn_w_gate"].T, "wu3": a["L0_ffn_w_up"].T, "wd3": a["L0_ffn_w_down"].T,
        "wq4": a["L1_xattn_Wq"], "wk4": a["L1_xattn_Wk"], "wv4": a["L1_xattn_Wv"],
        "bqk4": np.concatenate([cols(a["L1_xattn_bq"]), cols(a["L1_xattn_bk"])], axis=1),
        "bv4": row(a["L1_xattn_bv"]),
        "wqkv5": a["L1_attn_W"].T, "bqk5": cols(a["L1_attn_b"][:2 * DIM]), "bv5": row(a["L1_attn_b"][2 * DIM:]),
        "wr6": a["L1_ffn_gate_w"].T, "br6": row(a["L1_ffn_gate_bias"]),
        "ew6": ew,
        "c_ident": np.eye(P, dtype=f),
        "c_headmask": (c[:, None] // HD == np.arange(8)[None]).astype(f),
        "c_oddmask": ((c[:, None] // HD) % 2 == np.arange(2)[None]).astype(f),
        "c_causal": np.where(np.arange(SEQ)[None] > q[:, None], NEG, 0.0).astype(f),
        "c_ones": np.ones((P, P), f),
    }
    return {k: np.ascontiguousarray(v) for k, v in arrays.items()}


def kernel(**inputs):
    import concourse.bacc as bacc
    from concourse.bass_utils import run_bass_kernel_spmd

    nc = bacc.Bacc("TRN2", target_bir_lowering=False, num_devices=1)
    arrays = {"in_" + k: v for k, v in layout(inputs).items()}
    io = {k[3:]: nc.dram_tensor(k, v.shape, mybir.dt.from_np(v.dtype), kind="ExternalInput").ap()
          for k, v in arrays.items()}
    out = nc.dram_tensor("out", (TOK, DIM), F32, kind="ExternalOutput").ap()
    build(nc, io, out)
    r = run_bass_kernel_spmd(nc, [arrays], core_ids=[0])
    return r.results[0]["out"].reshape(BATCH, SEQ, DIM)
```
